# Optimizing a Trainium2 kernel written in Bass

```python
import numpy as np
import jax
import jax.numpy as jnp

def _softmax(x, axis=-1):
    return jax.nn.softmax(x, axis=axis)

def _gelu(x):
    return jax.nn.gelu(x, approximate=True)

def _silu(x):
    return jax.nn.silu(x)

def _sigmoid(x):
    return jax.nn.sigmoid(x)

def _layernorm(x, axis=-1, eps=1e-05):
    m = jnp.mean(x, axis=axis, keepdims=True)
    v = jnp.var(x, axis=axis, keepdims=True)
    return (x - m) / jnp.sqrt(v + eps)

def _scatter_add(tgt, idx, src, axis=0):
    return tgt.at[idx].add(src)

def _segment_sum(src, seg, n):
    return jax.ops.segment_sum(src, seg, n)
kernel_name = 'mk_conv_preact_d4_conv_nchw128_r2_4c5b57'

def setup_inputs(seed: int=0):
    np.random.seed(seed)
    _w = jnp.asarray

    def _rec_inputs():
        import jax
        import jax.numpy as jnp
        _gk = jax.random.key(seed)
        x = 7.22e-05 + 1 * jax.random.normal(jax.random.fold_in(_gk, 1), (16, 64, 32, 32), jnp.float32)
        return x
    x = _rec_inputs()

    def _L0_conv_setup():
        import jax, jax.numpy as jnp
        import numpy as np
        from jax import lax
        D_MODEL = 64
        OUT_C = 64
        D_STATE = 2
        EXPAND = 1
        D_INNER = EXPAND * D_MODEL
        DT_RANK = -(-D_MODEL // 16)
        D_CONV = 4
        B_SZ, H_SP, W_SP = (16, 32, 32)
        LN_EPS = 1e-05

        def _mamba_forward(x, W_in, conv_w, conv_b, W_xproj, W_dt, b_dt, A_log, D_param, W_out):
            B, L, _ = x.shape
            xz = jnp.einsum('bld,ed->ble', x, W_in)
            xs, z = jnp.split(xz, 2, axis=-1)
            xc = xs.transpose(0, 2, 1)
            xc = lax.conv_general_dilated(xc, conv_w, (1,), [(D_CONV - 1, 0)], dimension_numbers=('NCH', 'OIH', 'NCH'), feature_group_count=D_INNER)
            xc = xc + conv_b[None, :, None]
            xs = jax.nn.silu(xc).transpose(0, 2, 1)
            dbl = jnp.einsum('bld,ed->ble', xs, W_xproj)
            dt = dbl[..., :DT_RANK]
            Bm = dbl[..., DT_RANK:DT_RANK + D_STATE]
            Cm = dbl[..., DT_RANK + D_STATE:]
            dt = jax.nn.softplus(jnp.einsum('blr,dr->bld', dt, W_dt) + b_dt)
            A = -jnp.exp(A_log)
            deltaA = jnp.exp(dt[..., None] * A)
            deltaBx = dt[..., None] * Bm[:, :, None, :] * xs[..., None]

            def step(hst, inp):
                dA, dBx, Ct = inp
                hst = dA * hst + dBx
                y = jnp.einsum('bdn,bn->bd', hst, Ct)
                return (hst, y)
            h0 = jnp.zeros((B, D_INNER, D_STATE), dtype=xs.dtype)
            _, ys = lax.scan(step, h0, (deltaA.transpose(1, 0, 2, 3), deltaBx.transpose(1, 0, 2, 3), Cm.transpose(1, 0, 2)))
            ys = ys.transpose(1, 0, 2)
            y = ys + xs * D_param
            y = y * jax.nn.silu(z)
            return jnp.einsum('bld,od->blo', y, W_out)
        key = jax.random.key(seed)
        ks = jax.random.split(key, 12)
        s = 0.02
        x1 = jax.random.normal(ks[0], (B_SZ, D_MODEL, H_SP, W_SP), dtype=jnp.float32)
        W_in = jax.random.normal(ks[1], (2 * D_INNER, D_MODEL), dtype=jnp.float32) * s
        conv_w = jax.random.normal(ks[2], (D_INNER, 1, D_CONV), dtype=jnp.float32) * s
        conv_b = jnp.zeros((D_INNER,), dtype=jnp.float32)
        W_xproj = jax.random.normal(ks[3], (DT_RANK + 2 * D_STATE, D_INNER), dtype=jnp.float32) * s
        W_dt = jax.random.normal(ks[4], (D_INNER, DT_RANK), dtype=jnp.float32) * s
        b_dt = jax.random.uniform(ks[5], (D_INNER,), dtype=jnp.float32, minval=-4.0, maxval=-2.0)
        A_log = jnp.log(jnp.broadcast_to(jnp.arange(1, D_STATE + 1, dtype=jnp.float32), (D_INNER, D_STATE)))
        D_param = jnp.ones((D_INNER,), dtype=jnp.float32)
        W_out = jax.random.normal(ks[6], (OUT_C, D_INNER), dtype=jnp.float32) * s
        ln_g = jnp.ones((OUT_C,), dtype=jnp.float32)
        ln_b = jnp.zeros((OUT_C,), dtype=jnp.float32)
        return {'x1': x1, 'W_in': W_in, 'conv_w': conv_w, 'conv_b': conv_b, 'W_xproj': W_xproj, 'W_dt': W_dt, 'b_dt': b_dt, 'A_log': A_log, 'D_param': D_param, 'W_out': W_out, 'ln_g': ln_g, 'ln_b': ln_b}
    _L0_conv_all = _L0_conv_setup()
    _L0_conv_in = {k: v for k, v in _L0_conv_all.items() if k in ('W_in', 'conv_w', 'conv_b', 'W_xproj', 'W_dt', 'b_dt', 'A_log', 'D_param', 'W_out', 'ln_g', 'ln_b')}
    del _L0_conv_all

    def _L1_conv_setup():
        import jax, jax.numpy as jnp
        import numpy as np
        BN_EPS = 1e-05

        def _ternary_weights(key, shape, sparsity):
            k1, k2 = jax.random.split(key)
            signs = jnp.where(jax.random.uniform(k1, shape) < 0.5, -1.0, 1.0)
            active = jax.random.uniform(k2, shape) <= 0.5
            return jnp.where(active, signs, 0.0).astype(jnp.float32)
        key = jax.random.key(seed)
        ks = jax.random.split(key, 5)
        B, C, H, W = (8, 64, 128, 128)
        Cout = 64
        x = jax.random.normal(ks[0], (B, C, H, W), dtype=jnp.float32)
        gamma = jnp.ones((C,), dtype=jnp.float32)
        beta = jnp.zeros((C,), dtype=jnp.float32)
        w_lbp = _ternary_weights(ks[1], (C, C, 3, 3), 0.5)
        fan_in = C * 1 * 1
        bound = 1.0 / np.sqrt(fan_in)
        w_1x1 = jax.random.uniform(ks[2], (Cout, C, 1, 1), minval=-bound, maxval=bound, dtype=jnp.float32)
        b_1x1 = jax.random.uniform(ks[3], (Cout,), minval=-bound, maxval=bound, dtype=jnp.float32)
        return {'x': x, 'gamma': gamma, 'beta': beta, 'w_lbp': w_lbp, 'w_1x1': w_1x1, 'b_1x1': b_1x1}
    _L1_conv_all = _L1_conv_setup()
    _L1_conv_in = {k: v for k, v in _L1_conv_all.items() if k in ('gamma', 'beta', 'w_lbp', 'w_1x1', 'b_1x1')}
    del _L1_conv_all

    def _L2_conv_setup():
        import jax, jax.numpy as jnp
        import numpy as np

        def _prelu(x, a):
            return jnp.where(x >= 0, x, a * x)

        def _conv1x1(x, w, b, a):
            y = jnp.einsum('oc,nchw->nohw', w, x) + b[None, :, None, None]
            return _prelu(y, a)
        key = jax.random.key(seed)
        ks = jax.random.split(key, 8)
        N, C, H, W = (4, 64, 32, 32)
        Cr = C // 2
        sC = 1.0 / np.sqrt(C)
        x = jax.random.normal(ks[0], (N, C, H, W), dtype=jnp.float32)
        w1 = jax.random.normal(ks[1], (Cr, C), dtype=jnp.float32) * sC
        b1 = jnp.zeros((Cr,), dtype=jnp.float32)
        a1 = jnp.asarray(0.25, dtype=jnp.float32)
        w2 = jax.random.normal(ks[2], (Cr, C), dtype=jnp.float32) * sC
        b2 = jnp.zeros((Cr,), dtype=jnp.float32)
        a2 = jnp.asarray(0.25, dtype=jnp.float32)
        wa = jax.random.normal(ks[3], (C, C), dtype=jnp.float32) * sC
        ba = jnp.zeros((C,), dtype=jnp.float32)
        aa = jnp.asarray(0.25, dtype=jnp.float32)
        return {'x': x, 'w1': w1, 'b1': b1, 'a1': a1, 'w2': w2, 'b2': b2, 'a2': a2, 'wa': wa, 'ba': ba, 'aa': aa}
    _L2_conv_all = _L2_conv_setup()
    _L2_conv_in = {k: v for k, v in _L2_conv_all.items() if k in ('w1', 'b1', 'a1', 'w2', 'b2', 'a2', 'wa', 'ba', 'aa')}
    del _L2_conv_all

    def _L3_conv_setup():
        import jax, jax.numpy as jnp
        import numpy as np
        B, C, H, W, O = (8, 64, 128, 128, 64)
        key = jax.random.key(seed)
        k1, k2, k3, k4 = jax.random.split(key, 4)
        x = jax.random.normal(k1, (B, C, H, W), dtype=jnp.float32)
        theta_s = jax.random.uniform(k2, (C, 2), dtype=jnp.float32, minval=-1.0, maxval=1.0)
        w_dw = jax.random.normal(k3, (C,), dtype=jnp.float32) * 0.1
        w_pw = jax.random.normal(k4, (O, C), dtype=jnp.float32) * (1.0 / np.sqrt(C))
        return {'x': x, 'theta_s': theta_s, 'w_dw': w_dw, 'w_pw': w_pw}
    _L3_conv_all = _L3_conv_setup()
    _L3_conv_in = {k: v for k, v in _L3_conv_all.items() if k in ('theta_s', 'w_dw', 'w_pw')}
    del _L3_conv_all
    return {'x': x, 'L0_conv_W_in': _L0_conv_in['W_in'], 'L0_conv_conv_w': _L0_conv_in['conv_w'], 'L0_conv_conv_b': _L0_conv_in['conv_b'], 'L0_conv_W_xproj': _L0_conv_in['W_xproj'], 'L0_conv_W_dt': _L0_conv_in['W_dt'], 'L0_conv_b_dt': _L0_conv_in['b_dt'], 'L0_conv_A_log': _L0_conv_in['A_log'], 'L0_conv_D_param': _L0_conv_in['D_param'], 'L0_conv_W_out': _L0_conv_in['W_out'], 'L0_conv_ln_g': _L0_conv_in['ln_g'], 'L0_conv_ln_b': _L0_conv_in['ln_b'], 'L1_conv_gamma': _L1_conv_in['gamma'], 'L1_conv_beta': _L1_conv_in['beta'], 'L1_conv_w_lbp': _L1_conv_in['w_lbp'], 'L1_conv_w_1x1': _L1_conv_in['w_1x1'], 'L1_conv_b_1x1': _L1_conv_in['b_1x1'], 'L2_conv_w1': _L2_conv_in['w1'], 'L2_conv_b1': _L2_conv_in['b1'], 'L2_conv_a1': _L2_conv_in['a1'], 'L2_conv_w2': _L2_conv_in['w2'], 'L2_conv_b2': _L2_conv_in['b2'], 'L2_conv_a2': _L2_conv_in['a2'], 'L2_conv_wa': _L2_conv_in['wa'], 'L2_conv_ba': _L2_conv_in['ba'], 'L2_conv_aa': _L2_conv_in['aa'], 'L3_conv_theta_s': _L3_conv_in['theta_s'], 'L3_conv_w_dw': _L3_conv_in['w_dw'], 'L3_conv_w_pw': _L3_conv_in['w_pw']}

def reference(x, L0_conv_W_in, L0_conv_conv_w, L0_conv_conv_b, L0_conv_W_xproj, L0_conv_W_dt, L0_conv_b_dt, L0_conv_A_log, L0_conv_D_param, L0_conv_W_out, L0_conv_ln_g, L0_conv_ln_b, L1_conv_gamma, L1_conv_beta, L1_conv_w_lbp, L1_conv_w_1x1, L1_conv_b_1x1, L2_conv_w1, L2_conv_b1, L2_conv_a1, L2_conv_w2, L2_conv_b2, L2_conv_a2, L2_conv_wa, L2_conv_ba, L2_conv_aa, L3_conv_theta_s, L3_conv_w_dw, L3_conv_w_pw):
    import jax
    import jax.numpy as jnp

    def _L0_conv_ref(x1, W_in, conv_w, conv_b, W_xproj, W_dt, b_dt, A_log, D_param, W_out, ln_g, ln_b):
        import jax, jax.numpy as jnp
        import numpy as np
        from jax import lax
        D_MODEL = 64
        OUT_C = 64
        D_STATE = 2
        EXPAND = 1
        D_INNER = EXPAND * D_MODEL
        DT_RANK = -(-D_MODEL // 16)
        D_CONV = 4
        B_SZ, H_SP, W_SP = (16, 32, 32)
        LN_EPS = 1e-05

        def _mamba_forward(x, W_in, conv_w, conv_b, W_xproj, W_dt, b_dt, A_log, D_param, W_out):
            B, L, _ = x.shape
            xz = jnp.einsum('bld,ed->ble', x, W_in)
            xs, z = jnp.split(xz, 2, axis=-1)
            xc = xs.transpose(0, 2, 1)
            xc = lax.conv_general_dilated(xc, conv_w, (1,), [(D_CONV - 1, 0)], dimension_numbers=('NCH', 'OIH', 'NCH'), feature_group_count=D_INNER)
            xc = xc + conv_b[None, :, None]
            xs = jax.nn.silu(xc).transpose(0, 2, 1)
            dbl = jnp.einsum('bld,ed->ble', xs, W_xproj)
            dt = dbl[..., :DT_RANK]
            Bm = dbl[..., DT_RANK:DT_RANK + D_STATE]
            Cm = dbl[..., DT_RANK + D_STATE:]
            dt = jax.nn.softplus(jnp.einsum('blr,dr->bld', dt, W_dt) + b_dt)
            A = -jnp.exp(A_log)
            deltaA = jnp.exp(dt[..., None] * A)
            deltaBx = dt[..., None] * Bm[:, :, None, :] * xs[..., None]

            def step(hst, inp):
                dA, dBx, Ct = inp
                hst = dA * hst + dBx
                y = jnp.einsum('bdn,bn->bd', hst, Ct)
                return (hst, y)
            h0 = jnp.zeros((B, D_INNER, D_STATE), dtype=xs.dtype)
            _, ys = lax.scan(step, h0, (deltaA.transpose(1, 0, 2, 3), deltaBx.transpose(1, 0, 2, 3), Cm.transpose(1, 0, 2)))
            ys = ys.transpose(1, 0, 2)
            y = ys + xs * D_param
            y = y * jax.nn.silu(z)
            return jnp.einsum('bld,od->blo', y, W_out)
        b, c, h, w = x1.shape
        x = x1.transpose(0, 2, 3, 1).reshape(b, h * w, c)
        y = _mamba_forward(x, W_in, conv_w, conv_b, W_xproj, W_dt, b_dt, A_log, D_param, W_out)
        mu = jnp.mean(y, axis=-1, keepdims=True)
        var = jnp.mean(jnp.square(y - mu), axis=-1, keepdims=True)
        y = (y - mu) * lax.rsqrt(var + LN_EPS) * ln_g + ln_b
        return y.reshape(b, h, w, OUT_C).transpose(0, 3, 1, 2)

    def _L1_conv_ref(x, gamma, beta, w_lbp, w_1x1, b_1x1):
        import jax, jax.numpy as jnp
        import numpy as np
        BN_EPS = 1e-05

        def _ternary_weights(key, shape, sparsity):
            k1, k2 = jax.random.split(key)
            signs = jnp.where(jax.random.uniform(k1, shape) < 0.5, -1.0, 1.0)
            active = jax.random.uniform(k2, shape) <= 0.5
            return jnp.where(active, signs, 0.0).astype(jnp.float32)
        mean = jnp.mean(x, axis=(0, 2, 3), keepdims=True)
        var = jnp.var(x, axis=(0, 2, 3), keepdims=True)
        xn = (x - mean) * jax.lax.rsqrt(var + BN_EPS)
        xn = xn * gamma[None, :, None, None] + beta[None, :, None, None]
        y = jax.lax.conv_general_dilated(xn, w_lbp, window_strides=(1, 1), padding=((1, 1), (1, 1)), dimension_numbers=('NCHW', 'OIHW', 'NCHW'))
        y = jax.nn.relu(y) + x
        out = jnp.einsum('bchw,oc->bohw', y, w_1x1[:, :, 0, 0]) + b_1x1[None, :, None, None]
        return out

    def _L2_conv_ref(x, w1, b1, a1, w2, b2, a2, wa, ba, aa):
        import jax, jax.numpy as jnp
        import numpy as np

        def _prelu(x, a):
            return jnp.where(x >= 0, x, a * x)

        def _conv1x1(x, w, b, a):
            y = jnp.einsum('oc,nchw->nohw', w, x) + b[None, :, None, None]
            return _prelu(y, a)
        N, C, H, W = x.shape
        HW = H * W
        e1 = _conv1x1(x, w1, b1, a1).reshape(N, -1, HW)
        e2 = _conv1x1(x, w2, b2, a2).reshape(N, -1, HW)
        asm = _conv1x1(x, wa, ba, aa).reshape(N, C, HW)
        score = jnp.einsum('nci,ncj->nij', e1, e2)
        score = jax.nn.softmax(score, axis=2)
        out = jnp.einsum('nij,ncj->nci', score, asm)
        return out.reshape(N, C, H, W)

    def _L3_conv_ref(x, theta_s, w_dw, w_pw):
        import jax, jax.numpy as jnp
        import numpy as np
        B, C, H, W, O = (8, 64, 128, 128, 64)
        b, c, h, w = x.shape
        xp = jnp.pad(x, ((0, 0), (0, 0), (1, 1), (1, 1)))
        hp, wp = (h + 2, w + 2)
        t = -theta_s
        ft = jnp.floor(t)
        dt = t - ft
        ft = ft.astype(jnp.int32)
        m = jnp.arange(1, h + 1)
        n = jnp.arange(1, w + 1)
        y0 = jnp.clip(m[None, :] + ft[:, 0:1], 0, hp - 1)
        y1 = jnp.clip(m[None, :] + ft[:, 0:1] + 1, 0, hp - 1)
        x0 = jnp.clip(n[None, :] + ft[:, 1:2], 0, wp - 1)
        x1 = jnp.clip(n[None, :] + ft[:, 1:2] + 1, 0, wp - 1)
        cidx = jnp.arange(c)[:, None, None]
        z1 = xp[:, cidx, y0[:, :, None], x0[:, None, :]]
        z2 = xp[:, cidx, y0[:, :, None], x1[:, None, :]]
        z3 = xp[:, cidx, y1[:, :, None], x0[:, None, :]]
        z4 = xp[:, cidx, y1[:, :, None], x1[:, None, :]]
        dy = dt[:, 0][None, :, None, None]
        dx = dt[:, 1][None, :, None, None]
        s = z1 * (1 - dy) * (1 - dx) + z2 * (1 - dy) * dx + z3 * dy * (1 - dx) + z4 * dy * dx
        s = s * w_dw[None, :, None, None]
        return jnp.einsum('bchw,oc->bohw', s, w_pw)

    def _gn(v, G=32, eps=1e-05):
        B_, C_, H_, W_ = v.shape
        g = v.reshape(B_, G, C_ // G, H_, W_)
        m = jnp.mean(g, axis=(2, 3, 4), keepdims=True)
        s = jnp.var(g, axis=(2, 3, 4), keepdims=True)
        return ((g - m) / jnp.sqrt(s + eps)).reshape(v.shape)

    def _ln_c(v, eps=1e-06):
        m = jnp.mean(v, axis=1, keepdims=True)
        s = jnp.var(v, axis=1, keepdims=True)
        return (v - m) / jnp.sqrt(s + eps)

    def _ln_t(v, eps=1e-05):
        m = jnp.mean(v, axis=-1, keepdims=True)
        s = jnp.var(v, axis=-1, keepdims=True)
        return (v - m) / jnp.sqrt(s + eps)

    def _to_tokens(v):
        B_, C_, H_, W_ = v.shape
        return v.reshape(B_, C_, H_ * W_).transpose(0, 2, 1)

    def _from_tokens(t, like):
        B_, C_, H_, W_ = like.shape
        return t.transpose(0, 2, 1).reshape(B_, C_, H_, W_)
    x = x + _L0_conv_ref(_gn(x), L0_conv_W_in, L0_conv_conv_w, L0_conv_conv_b, L0_conv_W_xproj, L0_conv_W_dt, L0_conv_b_dt, L0_conv_A_log, L0_conv_D_param, L0_conv_W_out, L0_conv_ln_g, L0_conv_ln_b)
    x = x + _L1_conv_ref(_gn(x), L1_conv_gamma, L1_conv_beta, L1_conv_w_lbp, L1_conv_w_1x1, L1_conv_b_1x1)
    x = x + _L2_conv_ref(_gn(x), L2_conv_w1, L2_conv_b1, L2_conv_a1, L2_conv_w2, L2_conv_b2, L2_conv_a2, L2_conv_wa, L2_conv_ba, L2_conv_aa)
    x = x + _L3_conv_ref(_gn(x), L3_conv_theta_s, L3_conv_w_dw, L3_conv_w_pw)
    return x

_drawn_inputs = setup_inputs


def setup_inputs(seed=0):
    import zlib

    import numpy as np

    out = dict(_drawn_inputs(seed))
    spreads = {'L0_conv_conv_b': (0.0, 0.1),
     'L0_conv_D_param': (1.0, 0.2),
     'L0_conv_ln_g': (1.0, 0.2),
     'L0_conv_ln_b': (0.0, 0.501),
     'L1_conv_gamma': (1.0, 0.2),
     'L1_conv_beta': (0.0, 0.1),
     'L2_conv_b1': (0.0, 0.8),
     'L2_conv_b2': (0.0, 2.0),
     'L2_conv_ba': (0.0, 0.8)}
    factors = {'L0_conv_conv_w': 3.917,
     'L0_conv_W_xproj': 64.0,
     'L0_conv_W_dt': 64.0,
     'L0_conv_b_dt': 64.0,
     'L0_conv_A_log': 64.0,
     'L1_conv_b_1x1': 4.878,
     'L3_conv_theta_s': 8.0,
     'L3_conv_w_dw': 5.781,
     'L3_conv_w_pw': 6.094}
    for name, (base, spread) in spreads.items():
        noise = np.random.default_rng([zlib.crc32(name.encode()), seed]).standard_normal(out[name].shape)
        drawn = base * np.exp(spread * noise) if base else spread * noise
        out[name] = jnp.asarray(drawn.astype(out[name].dtype))
    for name, factor in factors.items():
        out[name] = (out[name] * factor).astype(out[name].dtype)
    return out
```

```python
import numpy as np
import concourse.bass as bass
from concourse import mybir
from concourse.alu_op_type import AluOpType as ALU
from contextlib import ExitStack

F32 = mybir.dt.float32
F32R = mybir.dt.float32r
BF16 = mybir.dt.bfloat16
ACT = mybir.ActivationFunctionType
AX = mybir.AxisListType

P = 128
IMAGES, C, HH, WW = 16, 64, 32, 32
L = HH * WW
HALF = L // 2
PAIRS = IMAGES // 2
STATE = 2
RANK = 4
TAPS = 4
CR = C // 2
CHUNKS = L // P
PW = WW + 2
EPS = 1e-5

MATS = (["winx", "winz"] + ["bc%d" % n for n in range(2 * STATE)] + ["wout", "w11", "wpw", "wa",
        "ba", "e1w", "e2w", "mean64", "pairs", "batch", "ident"] + ["lbp%d" % t for t in range(9)])
COLS = ["cw0", "cw1", "cw2", "cw3", "cb", "bdt", "al0", "al1", "dpar", "lng", "lnb", "gamma",
        "beta", "b11", "b1", "b2", "a1", "a2", "aa", "wdw"]
OFF, _at = {}, 0
for _n in MATS:
    OFF[_n] = _at
    _at += P
for _n, _w in (("dtl", P), ("dtr", P), ("thy", C), ("thx", C), ("grid", WW), ("ones", C)):
    OFF[_n] = _at
    _at += _w
for _n in COLS:
    OFF[_n] = _at
    _at += 1
NPACK = _at


class Chain:

    def __init__(self, eng, sem):
        self.eng, self.sem, self.base, self.k, self.fixed = eng, sem, 0, 0, 0

    def link(self, ins):
        self.k += 1
        ins.then_inc(self.sem, 1)
        self.eng.wait_ge(self.sem, self.base + self.k)

    def enter(self, i, per):
        self.fixed, self.per = self.fixed + self.k, per
        self.base, self.k = self.fixed + i * per, 0

    def leave(self, turns):
        assert self.k == self.per, (self.k, self.per)
        self.fixed += turns * self.per
        self.base, self.k = self.fixed, 0


def need(eng, sem, value):
    if not (isinstance(value, int) and value <= 0):
        eng.wait_ge(sem, value)


def before(p, h):
    return (p, 0) if h else (p - 1, 1)


def after(p, h):
    return (p + 1, 0) if h else (p, 1)


def build(nc, x, pack, out):
    with ExitStack() as ctx:
        def sb(name, shape, dt=F32):
            return ctx.enter_context(nc.sbuf_tensor(name, shape, dt))

        X = sb("X", [P, PAIRS, L])
        W = sb("W", [P, NPACK])
        RA = sb("RA", [P, PAIRS, L])
        RB = sb("RB", [P, 2 * PAIRS * L])
        R = sb("R", [P, 8 * L], F32R)
        WS = sb("WS", [P, 2, 9, P], F32R)
        WDT = sb("WDT", [P, P])
        SM = sb("SM", [P, 512])
        EX = sb("EX", [P, 4 * L])
        MB = sb("MB", [P, 2, CHUNKS, 2], BF16)
        IB = sb("IB", [P, P], BF16)
        PS = ctx.enter_context(nc.psum_tensor("PS", [P, 8, HALF], F32))

        def mat(name, w=P):
            return W[:, OFF[name]:OFF[name] + w]

        def col(name, n=P):
            return W[0:n, OFF[name]:OFF[name] + 1]

        def bank(n):
            return PS[:, n, :]

        def two(n):
            return PS[:, n:n + 2, :].rearrange("p a b -> p (a b)")

        def pair(t, p):
            if isinstance(p, int):
                return t[:, p, :]
            return t[:, bass.ds(p, 1), :].rearrange("p a n -> p (a n)")

        def half(t, p, h):
            if isinstance(p, int):
                return t[:, p, h * HALF:(h + 1) * HALF]
            return t[:, bass.ds(p, 1), h * HALF:(h + 1) * HALF].rearrange("p a n -> p (a n)")

        at = [0]

        def small(*shape):
            n = int(np.prod(shape))
            v = SM[:, at[0]:at[0] + n]
            at[0] += n
            assert at[0] <= 512
            names = "abc"[:len(shape)]
            if len(shape) > 1:
                v = v.rearrange("p (%s) -> p %s" % (" ".join(names), " ".join(names)),
                                **dict(zip(names[:-1], shape)))
            return v

        BST = small(PAIRS, 2, 6)
        MV = small(PAIRS, 2)
        GS = small(PAIRS, 2)
        SQ = small(PAIRS)
        VAR = small(PAIRS)
        MHALF = small(PAIRS)
        SC = small(PAIRS)
        SH = small(PAIRS)
        SB = small(PAIRS)
        TB = small(PAIRS)
        BM = small(2, PAIRS)
        BS = small(2)
        BT = small(8)
        ANEG = small(STATE)
        AEXP = small(STATE)
        OMA = small(2)
        AB = small(2)
        MEANO = small(1)
        MX = small(2, CHUNKS, 2)
        MXX = small(2, CHUNKS)
        EPSC = small(1)

        XS = RA
        ZS = RB[:, 0:PAIRS * L].rearrange("p (a n) -> p a n", a=PAIRS)
        TMP = RB[:, PAIRS * L:2 * PAIRS * L]
        G = [TMP[:, b * L:(b + 1) * L] for b in range(2)]
        AC = [TMP[:, (2 + b) * L:(3 + b) * L] for b in range(2)]

        def temp(n):
            k = [2 * n, 2 * n + 1]
            return [TMP[:, i * HALF:(i + 1) * HALF] if i < 16 else EX[:, (i - 16) * HALF:(i - 15) * HALF]
                    for i in k]

        tE = temp(0)
        tU = temp(1)
        tN = temp(2)
        tM = temp(3)
        tX = temp(4)
        tA = list(zip(temp(5), temp(6)))
        tB = list(zip(temp(7), temp(8)))
        tQ = temp(9)
        tR = temp(10)
        tY = temp(11)

        def padded(n):
            return R[:, n * PW * PW:(n + 1) * PW * PW].rearrange("p (a c) -> p a c", a=PW)
        UH, UL = [padded(0), padded(1)], [padded(2), padded(3)]
        UF = [TMP[:, b * L:(b + 1) * L] for b in range(2)]
        GF = [TMP[:, (2 + b) * L:(3 + b) * L] for b in range(2)]
        YF = [TMP[:, (4 + b) * L:(5 + b) * L] for b in range(2)]

        def inner(u):
            return u[:, 1:HH + 1, 1:WW + 1]

        def stack(b, par, e):
            k = (b * 2 + par) * 2 + e
            return R[:, k * L:(k + 1) * L]
        G3 = RA
        SLOTS = 4
        PT = [[RB[:, (2 * n + par) * L:(2 * n + par + 1) * L] for par in range(2)] for n in range(SLOTS)]
        SA = [[RB[:, (8 + 2 * g + par) * L:(9 + 2 * g + par) * L] for par in range(2)] for g in range(2)]
        V = [RB[:, (12 + b) * L:(13 + b) * L].rearrange("p (c m) -> p c m", c=CHUNKS) for b in range(2)]
        GB = RB[:, 14 * L:15 * L]
        RC = RB[:, 15 * L:16 * L]
        ex = [EX[:, i * HALF:(i + 1) * HALF] for i in range(8)]
        EQ, ER, EF, VT, OT = ex[0:2], ex[2:4], ex[4:6], ex[6], ex[7]

        CG = 16
        D = RB[:, 0:PAIRS * L].rearrange("p (c g) -> p c g", c=C)
        AM = [[RB[:, PAIRS * L + (2 * n + a) * CG * P:PAIRS * L + (2 * n + a + 1) * CG * P]
               .rearrange("p (c m) -> p c m", c=CG) for a in range(2)] for n in range(2)]
        D1 = ex[0:2]
        HATV, HATW = [EX[:, i * HALF:(i + 1) * HALF].rearrange("p (c y) -> p c y", c=CG) for i in (2, 3)]
        E = RA.rearrange("p b n -> p (b n)").rearrange("p (x g c) -> p x g c", g=4, c=C)
        S3 = RB[:, 0:PAIRS * L].rearrange("p (b n) -> p b n", b=PAIRS)

        names = """packed zero_done exp_a wdt_mm wdt_done setup_done dve_step act_step pool_step
            stat_ready group_mm var_ready pow_done coef_ready
            g_ready xb_done xz_mm taps_done silux_done siluz_done
            dt_mm b_mm c_mm o_mm v_mm e_done dta_read u_done dt_read nd_done ln_done dt_done dtx_done
            b_read da_done scan_done c_read hc_done y_done sq_done r_done o_read blk0_done
            u_ready g1_ready uh_done ul_done conv_mm y1_done w1_mm x1_done
            minus_done gb_ready asm_mm e_mm asm_read e_read hi_done lo_done v_part v_done s_mm s_read m_ready
            mrow_mm m_copied t_mm p_ready pv_done add_done sum_mm sum_read rec_done acc_read x2_done
            g3_act g3_pool am_zero am_ready tr_mm tr_act tr_dve s1_mm s1_copied s2_mm s2_copied
            bk_mm bk_act bk_dve pw_mm res_done stored""".split()
        s = {n: ctx.enter_context(nc.semaphore(n)) for n in names}
        x_in = [ctx.enter_context(nc.semaphore("x_in%d" % p)) for p in range(PAIRS)]

        block = ctx.enter_context(nc.Block())
        xd = x.rearrange("(p two) c h w -> (two c) p (h w)", two=2)
        od = out.rearrange("(p two) c h w -> (two c) p (h w)", two=2)

        def transposed_out(copy, n):
            q, xb = divmod(n, 8)
            src = bank(n % 4).rearrange("p (x a c) -> p x a c", x=4, a=2)
            dst = D.rearrange("p c (q a x) -> p q x a c", q=2, a=2)[:, q, 4 * xb:4 * xb + 4]
            for a in range(2):
                last = copy(dst[:, :, a], src[:, :, a])
            return last

        def back_out(copy, n):
            q, xb = divmod(n, 8)
            src = bank(n % 4).rearrange("p (x b y) -> p x b y", x=4, b=4)
            dst = S3[:, 4 * q:4 * q + 4, :].rearrange("p b (y x) -> p x b y", x=WW)[:, 4 * xb:4 * xb + 4]
            return copy(dst, src)

        @block.sync
        def _(sp):
            sp.dma_start(W[:, :], pack).then_inc(s["packed"], 16)
            for p in range(PAIRS):
                sp.dma_start(X[:, p, :], xd[:, p, :]).then_inc(x_in[p], 16)
            for p in range(PAIRS):
                sp.wait_ge(s["res_done"], 2 * p + 2)
                sp.dma_start(od[:, p, :], X[:, p, :]).then_inc(s["stored"], 16)
            sp.wait_ge(s["stored"], 16 * PAIRS)

        @block.vector
        def _(v):
            ch = Chain(v, s["dve_step"])
            link = ch.link

            def coefs(turn):
                for p in range(PAIRS):
                    i = v.bn_aggr(MV[:, p, :], BST[:, p, :, :].rearrange("p h k -> p (h k)"))
                link(i)
                mean, var = MV[:, :, 0], MV[:, :, 1]
                link(v.tensor_tensor(SQ, mean, mean, ALU.mult))
                v.tensor_tensor(var, var, SQ, ALU.add).then_inc(s["stat_ready"], 1)
                v.wait_ge(s["group_mm"], turn + 1)
                link(v.tensor_copy(GS.rearrange("p a b -> p (a b)"), PS[:, 7, 0:2 * PAIRS]))
                link(v.tensor_tensor(SQ, GS[:, :, 0], GS[:, :, 0], ALU.mult))
                link(v.tensor_tensor(VAR, GS[:, :, 1], SQ, ALU.subtract))
                v.tensor_scalar(VAR, VAR, EPS, None, ALU.add).then_inc(s["var_ready"], 1)
                v.wait_ge(s["pow_done"], turn + 1)
                v.scalar_tensor_tensor(SH, GS[:, :, 0], -1.0, SC, ALU.mult, ALU.mult)\
                    .then_inc(s["coef_ready"], 1)
                v.wait_ge(s["coef_ready"], turn + 1)

            def stats(p, h):
                if isinstance(p, int):
                    return v.bn_stats(BST[:, p, h, :], half(X, p, h))
                return v.bn_stats(BST[:, bass.ds(p, 1), h, :].rearrange("p a k -> p (a k)"), half(X, p, h))

            link(v.memset(MHALF, -0.5))
            link(v.memset(EPSC, EPS))
            v.wait_ge(s["packed"], 16)
            link(v.tensor_copy(IB[:, :], mat("ident")))
            for par in range(2):
                q = slice(par * C, (par + 1) * C)
                o = slice(OFF["wout"] + par * C, OFF["wout"] + (par + 1) * C)
                link(v.tensor_reduce(MEANO[q], W[q, o], AX.X, ALU.add))
                link(v.tensor_scalar(MEANO[q], MEANO[q], 1.0 / C, None, ALU.mult))
                link(v.tensor_scalar(W[q, o], W[q, o], MEANO[q], None, ALU.subtract))
            for n in range(2):
                link(v.tensor_scalar(OMA[:, n:n + 1], col("a%d" % (n + 1)), -1.0, 1.0, ALU.mult, ALU.add))
                link(v.tensor_tensor(AB[:, n:n + 1], col("a%d" % (n + 1)), col("b%d" % (n + 1)), ALU.mult))
            link(v.tensor_scalar(mat("wpw"), mat("wpw"), col("wdw"), None, ALU.mult))
            lbp = W[:, OFF["lbp0"]:OFF["lbp0"] + 9 * P]
            link(v.tensor_copy(WS[:, 0, :, :].rearrange("p a b -> p (a b)"), lbp))
            link(v.tensor_tensor(WS[:, 1, :, :].rearrange("p a b -> p (a b)"), lbp,
                                 WS[:, 0, :, :].rearrange("p a b -> p (a b)"), ALU.subtract))
            v.wait_ge(s["wdt_mm"], 1)
            link(v.tensor_copy(WDT[:, :], PS[:, 6, 0:P]))
            v.wait_ge(s["exp_a"], 1)
            v.tensor_scalar(ANEG, AEXP, -1.0, None, ALU.mult).then_inc(s["setup_done"], 1)
            v.wait_ge(s["setup_done"], 1)

            for p in range(PAIRS):
                v.wait_ge(x_in[p], 16)
                for h in range(2):
                    i = stats(p, h)
            link(i)
            coefs(0)

            def taps(p, b):
                v.wait_ge(s["xz_mm"], p + 1)
                need(v, s["silux_done"], p - 1)
                xp = two(4 * b)
                link(v.tensor_scalar(AC[b], xp, col("cw3"), col("cb"), ALU.mult, ALU.add))
                for j in (1, 2, 3):
                    i = v.scalar_tensor_tensor(AC[b][:, j:L], xp[:, 0:L - j], col("cw%d" % (3 - j)),
                                               AC[b][:, j:L], ALU.mult, ALU.add)
                    if j < 3:
                        link(i)
                i.then_inc(s["taps_done"], 1)

            taps(0, 0)
            taps(1, 1)
            with v.Fori(1, PAIRS // 2) as k:
                ch.enter(k - 1, 6)
                taps(2 * k, 0)
                taps(2 * k + 1, 1)
                ch.leave(PAIRS // 2 - 1)

            def soft(p, h):
                n = 2 * p + h
                v.wait_ge(s["e_done"], n + 1)
                need(v, s["dt_done"], n - 1)
                v.tensor_scalar(tU[h], tE[h], 1.0, None, ALU.add).then_inc(s["u_done"], 1)
                v.wait_ge(s["dt_mm"], n + 1)
                need(v, s["da_done"], n - 1)
                need(v, s["dtx_done"], n - 1)
                v.tensor_scalar(tM[h], bank(0), col("bdt"), 0.0, ALU.add, ALU.max).then_inc(s["dt_read"], 1)
                v.wait_ge(s["u_done"], n + 1)
                v.scalar_tensor_tensor(tN[h], tU[h], -1.0, tE[h], ALU.add, ALU.subtract)\
                    .then_inc(s["nd_done"], 1)

            def scan(p, h):
                n = 2 * p + h
                v.wait_ge(s["dtx_done"], n + 1)
                v.wait_ge(s["b_mm"], n + 1)
                for j in range(STATE):
                    i = v.tensor_tensor(tB[h][j], bank(1 + j), tX[h], ALU.mult)
                i.then_inc(s["b_read"], 1)
                v.wait_ge(s["b_read"], n + 1)
                v.wait_ge(s["da_done"], n + 1)
                for j in range(STATE):
                    first = 0.0 if h == 0 else tB[0][j][:, HALF - 1:HALF]
                    i = v.tensor_tensor_scan(tB[h][j], tA[h][j], tB[h][j], first, ALU.mult, ALU.add)
                i.then_inc(s["scan_done"], 1)
                v.wait_ge(s["scan_done"], n + 1)
                v.wait_ge(s["c_mm"], n + 1)
                for j in range(STATE):
                    i = v.tensor_tensor(tA[h][j], bank(3 + j), tB[h][j], ALU.mult)
                i.then_inc(s["c_read"], 1)
                v.wait_ge(s["c_read"], n + 1)
                v.scalar_tensor_tensor(tA[h][0], half(XS, p, h), col("dpar"), tA[h][0], ALU.mult, ALU.add)\
                    .then_inc(s["hc_done"], 1)

            def norm(p, h):
                n = 2 * p + h
                v.wait_ge(s["r_done"], n + 1)
                v.tensor_tensor(tR[h], bank(5), tR[h], ALU.mult).then_inc(s["o_read"], 1)
                v.wait_ge(s["o_read"], n + 1)
                v.scalar_tensor_tensor(half(X, p, h), tR[h], col("lng"), half(X, p, h), ALU.mult, ALU.add)\
                    .then_inc(s["blk0_done"], 1)
                v.wait_ge(s["blk0_done"], n + 1)
                return stats(p, h)

            def turn(p, h, lead=True, lag=True):
                scan(p, h)
                if lead:
                    soft(*after(p, h))
                if lag:
                    norm(*before(p, h))

            v.wait_ge(s["xb_done"], PAIRS)
            soft(0, 0)
            turn(0, 0, lag=False)
            turn(0, 1)
            with v.Fori(1, PAIRS - 1) as p:
                turn(p, 0)
                turn(p, 1)
            turn(PAIRS - 1, 0)
            turn(PAIRS - 1, 1, lead=False)
            link(norm(PAIRS - 1, 1))

            coefs(1)
            mean, msq, b0, b1 = MV[:, :, 0], MV[:, :, 1], BM[:, 0, :], BM[:, 1, :]
            link(v.tensor_tensor(b0, mean, SC, ALU.mult))
            link(v.tensor_tensor(SQ, b0, SH, ALU.mult))
            link(v.tensor_tensor(b0, b0, SH, ALU.add))
            link(v.tensor_tensor(b1, msq, SC, ALU.mult))
            link(v.tensor_tensor(b1, b1, SC, ALU.mult))
            link(v.scalar_tensor_tensor(b1, SQ, 2.0, b1, ALU.mult, ALU.add))
            link(v.tensor_tensor(SQ, SH, SH, ALU.mult))
            link(v.tensor_tensor(b1, b1, SQ, ALU.add))
            v.tensor_reduce(BS, BM, AX.X, ALU.add).then_inc(s["stat_ready"], 1)
            v.wait_ge(s["group_mm"], 3)
            link(v.tensor_copy(BT[:, 0:2], PS[:, 7, 0:2]))
            link(v.tensor_tensor(BT[:, 2:3], BT[:, 0:1], BT[:, 0:1], ALU.mult))
            link(v.tensor_tensor(BT[:, 3:4], BT[:, 1:2], BT[:, 2:3], ALU.subtract))
            v.tensor_scalar(BT[:, 3:4], BT[:, 3:4], EPS, None, ALU.add).then_inc(s["var_ready"], 1)
            v.wait_ge(s["pow_done"], 3)
            link(v.tensor_tensor(BT[:, 5:6], BT[:, 4:5], col("gamma"), ALU.mult))
            link(v.tensor_tensor(BT[:, 6:7], BT[:, 5:6], BT[:, 0:1], ALU.mult))
            link(v.tensor_tensor(BT[:, 6:7], col("beta"), BT[:, 6:7], ALU.subtract))
            link(v.tensor_scalar(SB, SC, BT[:, 5:6], None, ALU.mult))
            v.tensor_scalar(TB, SH, BT[:, 5:6], BT[:, 6:7], ALU.mult, ALU.add).then_inc(s["coef_ready"], 1)
            v.wait_ge(s["coef_ready"], 3)

            def low(p, b):
                v.wait_ge(s["uh_done"], p + 1)
                need(v, s["conv_mm"], 2 * p - 2)
                v.tensor_tensor(inner(UL[b]), UF[b].rearrange("p (y x) -> p y x", y=HH), inner(UH[b]),
                                ALU.subtract).then_inc(s["ul_done"], 1)

            def relu(p, b):
                v.wait_ge(s["g1_ready"], p + 1)
                need(v, s["w1_mm"], 2 * p - 2)
                for h in range(2):
                    q = slice(h * HALF, (h + 1) * HALF)
                    v.wait_ge(s["conv_mm"], 2 * p + h + 1)
                    v.scalar_tensor_tensor(YF[b][:, q], bank(2 * b + h), 0.0, GF[b][:, q], ALU.max, ALU.add)\
                        .then_inc(s["y1_done"], 1)

            def add1(p, b):
                for h in range(2):
                    v.wait_ge(s["w1_mm"], 2 * p + h + 1)
                    v.scalar_tensor_tensor(half(X, p, h), bank(4 + 2 * b + h), col("b11"), half(X, p, h),
                                           ALU.add, ALU.add).then_inc(s["x1_done"], 1)
                v.wait_ge(s["x1_done"], 2 * p + 2)
                for h in range(2):
                    i = stats(p, h)
                return i

            def turn1(p, b, lead=True, lag=True):
                if lead:
                    low(p + 1, 1 - b)
                relu(p, b)
                if lag:
                    return add1(p - 1, 1 - b)

            low(0, 0)
            turn1(0, 0, lag=False)
            turn1(1, 1)
            with v.Fori(1, PAIRS // 2 - 1) as k:
                turn1(2 * k, 0)
                turn1(2 * k + 1, 1)
            turn1(PAIRS - 2, 0)
            turn1(PAIRS - 1, 1, lead=False)
            link(add1(PAIRS - 1, 1))
            coefs(3)

            for b in range(2):
                for par in range(2):
                    i = v.memset(stack(b, par, 1)[96:98, :].bitcast(F32), -1.0)
            i.then_inc(s["minus_done"], 1)

            def values(q, b):
                for c in range(2):
                    v.wait_ge(s["asm_mm"], 2 * q + c + 1)
                    ba = mat("ba").unsqueeze(1).to_broadcast([P, CHUNKS // 2, P])
                    v.tensor_tensor(VT.rearrange("p (c m) -> p c m", c=CHUNKS // 2),
                                    bank(6 + c).rearrange("p (c m) -> p c m", c=CHUNKS // 2),
                                    ba, ALU.add).then_inc(s["asm_read"], 1)
                    v.wait_ge(s["asm_read"], 2 * q + c + 1)
                    vh = V[b][:, c * 4:c * 4 + 4, :].rearrange("p c m -> p (c m)")
                    v.tensor_scalar(vh, VT, 0.0, col("aa"), ALU.min, ALU.mult).then_inc(s["v_part"], 1)
                    v.wait_ge(s["v_part"], 2 * q + c + 1)
                    v.scalar_tensor_tensor(vh, VT, 0.0, vh, ALU.max, ALU.add).then_inc(s["v_done"], 1)
                    v.wait_ge(s["v_done"], 2 * q + c + 1)

            def operand(q, b, t):
                e, h = divmod(t, 2)
                cols = slice(h * HALF, (h + 1) * HALF)
                for par in range(2):
                    n = 8 * q + 2 * t + par
                    st = stack(b, par, e)
                    v.wait_ge(s["e_read"], n + 1)
                    link(v.scalar_tensor_tensor(EF[par][0:96, :], ER[par][0:96, :], OMA[0:96, e:e + 1],
                                                EQ[par][0:96, :], ALU.mult, ALU.add))
                    v.tensor_copy(st[0:96, cols], EF[par][0:96, :]).then_inc(s["hi_done"], 1)
                    v.wait_ge(s["hi_done"], n + 1)
                    r = slice(64, 96) if e == 0 else slice(32, 64)
                    v.tensor_tensor(st[r, cols], EF[par][r, :], st[r, cols], ALU.subtract)\
                        .then_inc(s["lo_done"], 1)

            def maxima(q, par):
                for t in range(CHUNKS):
                    for h in range(2):
                        v.wait_ge(s["s_mm"], 32 * q + 16 * par + 2 * t + h + 1)
                        v.tensor_reduce(MX[:, par, t, h:h + 1], bank(2 + h), AX.X, ALU.max)\
                            .then_inc(s["s_read"], 1)
                v.wait_ge(s["s_read"], 32 * q + 16 * par + 16)
                need(v, s["mrow_mm"], 4 * q - 2 + 2 * par)
                link(v.tensor_reduce(MXX[:, par], MX[:, par], AX.X, ALU.max))
                link(v.tensor_copy(MB[:, par, :, 0], MXX[:, par]))
                v.tensor_tensor(MB[:, par, :, 1], MXX[:, par], MB[:, par, :, 0], ALU.subtract)\
                    .then_inc(s["m_ready"], 1)

            def finish(p):
                v.wait_ge(s["pv_done"], CHUNKS * (p + 1))
                for h in range(2):
                    n = 2 * p + h
                    v.wait_ge(s["rec_done"], n + 1)
                    v.tensor_tensor(OT, bank(h), RC[:, h * HALF:(h + 1) * HALF], ALU.mult)\
                        .then_inc(s["acc_read"], 1)
                    v.wait_ge(s["acc_read"], n + 1)
                    v.tensor_tensor(half(X, p, h), OT, half(X, p, h), ALU.add).then_inc(s["x2_done"], 1)
                    v.wait_ge(s["x2_done"], n + 1)
                    i = stats(p, h)
                return i

            def attend(p, b, lead=True, lag=True):
                if lag:
                    finish(p - 1)
                if lead:
                    scores(p + 1, 1 - b)

            def scores(q, b):
                values(q, b)
                for t in range(4):
                    operand(q, b, t)
                for par in range(2):
                    maxima(q, par)

            scores(0, 0)
            attend(0, 0, lag=False)
            with v.Fori(0, PAIRS // 2 - 1) as k:
                ch.enter(k, 2 * 12)
                attend(2 * k + 1, 1)
                attend(2 * k + 2, 0)
                ch.leave(PAIRS // 2 - 1)
            attend(PAIRS - 1, 1, lead=False)
            link(finish(PAIRS - 1))
            coefs(4)

            v.memset(RB[:, PAIRS * L:PAIRS * L + 2 * CG * P], 0.0).then_inc(s["am_zero"], 1)
            v.wait_ge(s["am_zero"], 2)
            grid = mat("grid", WW).unsqueeze(1).to_broadcast([P, CG, WW])

            def hats(g):
                if g >= 2:
                    v.wait_ge(s["s2_mm"], (g - 1) * CG // 4)
                for a, th in ((0, "thy"), (1, "thx")):
                    tv = mat(th, C)[:, g * CG:(g + 1) * CG].unsqueeze(2).to_broadcast([P, CG, WW])
                    link(v.tensor_tensor(HATV, grid, tv, ALU.add))
                    link(v.tensor_scalar(HATW, HATV, -1.0, 1.0, ALU.mult, ALU.add))
                    link(v.scalar_tensor_tensor(HATW, HATV, 1.0, HATW, ALU.add, ALU.min))
                    for q in range(4):
                        r = slice(32 * q, 32 * q + 32)
                        i = v.tensor_scalar(AM[g % 2][a][r, :, 32 * q:32 * q + 32], HATW[r], 0.0, None, ALU.max)
                    i.then_inc(s["am_ready"], 1)

            hats(0)
            for n in range(1, 16, 2):
                v.wait_ge(s["tr_mm"], n + 1)
                transposed_out(v.tensor_copy, n).then_inc(s["tr_dve"], 1)
            hats(1)
            for n in range(16):
                v.wait_ge(s["s1_mm"], n + 1)
                need(v, s["s2_mm"], n - 1)
                v.tensor_copy(D1[n % 2], bank(n % 2)).then_inc(s["s1_copied"], 1)
                if n in (5, 9):
                    hats(2 + n // 9)
            for n in range(1, 16, 2):
                v.wait_ge(s["bk_mm"], n + 1)
                back_out(v.tensor_copy, n).then_inc(s["bk_dve"], 1)
            with v.Fori(0, PAIRS // 2) as k:
                for j in range(4):
                    v.wait_ge(s["pw_mm"], 4 * k + j + 1)
                    v.tensor_tensor(half(X, 2 * k + j // 2, j % 2), bank(4 + j),
                                    half(X, 2 * k + j // 2, j % 2), ALU.add).then_inc(s["res_done"], 1)

        @block.scalar
        def _(a):
            act = a.activation
            ch = Chain(a, s["act_step"])
            link = ch.link
            a.wait_ge(s["packed"], 16)
            act(AEXP, W[:, OFF["al0"]:OFF["al0"] + STATE], ACT.Exp).then_inc(s["exp_a"], 1)

            def gates(p, b):
                a.wait_ge(s["xz_mm"], p + 1)
                act(pair(ZS, p), two(4 * b + 2), ACT.Silu).then_inc(s["siluz_done"], 1)
                a.wait_ge(s["taps_done"], p + 1)
                act(pair(XS, p), AC[b], ACT.Silu).then_inc(s["silux_done"], 1)

            with a.Fori(0, PAIRS // 2) as k:
                gates(2 * k, 0)
                gates(2 * k + 1, 1)

            a.preload_act_table_set("natural_log_exp_and_others")
            a.wait_ge(s["setup_done"], 1)

            def soft(p, h):
                n = 2 * p + h
                a.wait_ge(s["dt_mm"], n + 1)
                need(a, s["nd_done"], n - 1)
                act(tE[h], bank(0), ACT.Abs, bias=col("bdt")).then_inc(s["dta_read"], 1)
                a.wait_ge(s["dta_read"], n + 1)
                act(tE[h], tE[h], ACT.Exp, scale=-1.0).then_inc(s["e_done"], 1)

            def soft_log(p, h):
                n = 2 * p + h
                a.wait_ge(s["nd_done"], n + 1)
                act(tU[h], tU[h], ACT.Ln).then_inc(s["ln_done"], 1)

            def grow(p, h):
                n = 2 * p + h
                a.wait_ge(s["dt_done"], n + 1)
                need(a, s["y_done"], n - 1)
                for j in range(STATE):
                    i = act(tA[h][j], tM[h], ACT.Exp, scale=ANEG[:, j:j + 1])
                i.then_inc(s["da_done"], 1)

            def norm(p, h):
                n = 2 * p + h
                a.wait_ge(s["o_mm"], n + 1)
                need(a, s["v_mm"], n - 1)
                act(tQ[h], bank(5), ACT.Square).then_inc(s["sq_done"], 1)
                a.wait_ge(s["v_mm"], n + 1)
                need(a, s["blk0_done"], n - 1)
                link(act(tR[h], bank(6), ACT.Ln, bias=EPSC))
                act(tR[h], tR[h], ACT.Exp, scale=-0.5).then_inc(s["r_done"], 1)

            def turn(p, h, lead=True, lag=True):
                grow(p, h)
                if lead:
                    soft(*after(p, h))
                if lag:
                    norm(*before(p, h))
                if lead:
                    soft_log(*after(p, h))

            soft(0, 0)
            soft_log(0, 0)
            turn(0, 0, lag=False)
            turn(0, 1)
            with a.Fori(1, PAIRS - 1) as p:
                ch.enter(p - 1, 2)
                turn(p, 0)
                turn(p, 1)
                ch.leave(PAIRS - 2)
            turn(PAIRS - 1, 0)
            turn(PAIRS - 1, 1, lead=False)
            norm(PAIRS - 1, 1)

            def high(p, b):
                a.wait_ge(s["u_ready"], p + 1)
                need(a, s["conv_mm"], 2 * p - 2)
                act(inner(UH[b]), UF[b].rearrange("p (y x) -> p y x", y=HH), ACT.Copy)\
                    .then_inc(s["uh_done"], 1)

            a.wait_ge(s["zero_done"], 1)
            high(0, 0)
            high(1, 1)
            with a.Fori(1, PAIRS // 2) as k:
                high(2 * k, 0)
                high(2 * k + 1, 1)

            a.wait_ge(s["coef_ready"], 4)

            def parts(q, t):
                e = t // 2
                for par in range(2):
                    n = 8 * q + 2 * t + par
                    a.wait_ge(s["e_mm"], n + 1)
                    need(a, s["hi_done"], n - 1)
                    act(EQ[par][0:96, :], PS[0:96, 6 + par, :], ACT.Identity,
                        bias=AB[0:96, e:e + 1], scale=col("a%d" % (e + 1), 96))
                    act(ER[par][0:96, :], PS[0:96, 6 + par, :], ACT.Relu, bias=col("b%d" % (e + 1), 96))\
                        .then_inc(s["e_read"], 1)

            def probs(p, j, par):
                slot = PT[j % SLOTS]
                n = CHUNKS * p + j
                if par == 0:
                    need(a, s["pv_done"], n - SLOTS + 1)
                    need(a, s["add_done"], 6 * p + (-2, -2, -1, 0, 1, 1, 2, 3)[j])
                for h in range(2):
                    a.wait_ge(s["t_mm"], 4 * n + 2 * par + h + 1)
                    act(slot[par][:, h * HALF:(h + 1) * HALF], bank(4 + h), ACT.Exp)\
                        .then_inc(s["p_ready"], 1)

            def max_rows(q, b, par):
                for h in range(2):
                    a.wait_ge(s["mrow_mm"], 4 * q + 2 * par + h + 1)
                    act(stack(b, par, 0)[96:98, h * HALF:(h + 1) * HALF], PS[96:98, 2 + h, :],
                        ACT.Copy).then_inc(s["m_copied"], 1)

            def inverse(p):
                for h in range(2):
                    n = 2 * p + h
                    q = slice(h * HALF, (h + 1) * HALF)
                    a.wait_ge(s["sum_mm"], n + 1)
                    act(RC[:, q], bank(6 + h), ACT.Ln).then_inc(s["sum_read"], 1)
                    a.wait_ge(s["sum_read"], n + 1)
                    act(RC[:, q], RC[:, q], ACT.Exp, scale=-1.0).then_inc(s["rec_done"], 1)

            def attend(p, b, lead=True, lag=True):
                for n in range(2 * CHUNKS):
                    probs(p, n // 2, n % 2)
                    if n == 0 and lag:
                        inverse(p - 1)
                    if n in PARTS_AT and lead:
                        parts(p + 1, PARTS_AT.index(n))
                    if n == 2 * CHUNKS - 1 and lead:
                        max_rows(p + 1, 1 - b, 0)
                        max_rows(p + 1, 1 - b, 1)

            PARTS_AT = (3, 5, 7, 8)
            for t in range(4):
                parts(0, t)
            for par in range(2):
                max_rows(0, 0, par)
            attend(0, 0, lag=False)
            with a.Fori(0, PAIRS // 2 - 1) as k:
                attend(2 * k + 1, 1)
                attend(2 * k + 2, 0)
            attend(PAIRS - 1, 1, lead=False)
            inverse(PAIRS - 1)

            a.wait_ge(s["coef_ready"], 5)
            for p in (0, 1, 4, 5):
                act(G3[:, p, :], X[:, p, :], ACT.Identity, bias=SH[:, p:p + 1], scale=SC[:, p:p + 1])\
                    .then_inc(s["g3_act"], 1)

            def copy(o, i):
                return act(o, i, ACT.Copy)
            for n in range(0, 16, 2):
                a.wait_ge(s["tr_mm"], n + 1)
                transposed_out(copy, n).then_inc(s["tr_act"], 1)
            for n in range(16):
                a.wait_ge(s["s2_mm"], n + 1)
                act(E[:, :, :, 4 * n:4 * n + 4].rearrange("p x g c -> p c g x"),
                    bank(2 + n % 2).rearrange("p (c g x) -> p c g x", c=4, g=4), ACT.Copy)\
                    .then_inc(s["s2_copied"], 1)
            for n in range(0, 16, 2):
                a.wait_ge(s["bk_mm"], n + 1)
                back_out(copy, n).then_inc(s["bk_act"], 1)

        @block.gpsimd
        def _(g):
            ch = Chain(g, s["pool_step"])
            link = ch.link

            def power(turn):
                g.wait_ge(s["var_ready"], turn + 1)
                if turn == 2:
                    g.tensor_tensor(BT[:, 4:5], BT[:, 3:4], MHALF[:, 0:1], ALU.pow).then_inc(s["pow_done"], 1)
                else:
                    g.tensor_tensor(SC, VAR, MHALF, ALU.pow).then_inc(s["pow_done"], 1)

            g.memset(R[:, 0:4 * PW * PW].bitcast(F32), 0.0).then_inc(s["zero_done"], 1)

            power(0)
            g.wait_ge(s["coef_ready"], 1)
            for p in range(PAIRS):
                need(g, s["xz_mm"], p - 1)
                g.tensor_scalar(G[p % 2], X[:, p, :], SC[:, p:p + 1], SH[:, p:p + 1], ALU.mult, ALU.add)\
                    .then_inc(s["g_ready"], 1)
                g.wait_ge(s["g_ready"], p + 1)
                g.tensor_scalar(X[:, p, :], X[:, p, :], col("lnb"), None, ALU.add).then_inc(s["xb_done"], 1)

            def soft(p, h):
                n = 2 * p + h
                g.wait_ge(s["ln_done"], n + 1)
                g.wait_ge(s["dt_read"], n + 1)
                link(g.tensor_tensor(tM[h], tM[h], tU[h], ALU.add))
                g.tensor_tensor(tM[h], tM[h], tN[h], ALU.subtract).then_inc(s["dt_done"], 1)
                g.wait_ge(s["dt_done"], n + 1)
                need(g, s["b_read"], n - 1)
                g.tensor_tensor(tX[h], tM[h], half(XS, p, h), ALU.mult).then_inc(s["dtx_done"], 1)

            def output(p, h):
                n = 2 * p + h
                g.wait_ge(s["hc_done"], n + 1)
                need(g, s["o_mm"], n - 1)
                link(g.tensor_tensor(tY[h], tA[h][0], tA[h][1], ALU.add))
                g.tensor_tensor(tY[h], tY[h], half(ZS, p, h), ALU.mult).then_inc(s["y_done"], 1)

            g.wait_ge(s["silux_done"], PAIRS)
            g.wait_ge(s["siluz_done"], PAIRS)
            soft(0, 0)
            output(0, 0)
            soft(0, 1)
            output(0, 1)
            with g.Fori(1, PAIRS) as p:
                ch.enter(p - 1, 4)
                soft(p, 0)
                output(p, 0)
                soft(p, 1)
                output(p, 1)
                ch.leave(PAIRS - 1)

            power(1)
            power(2)
            g.wait_ge(s["coef_ready"], 3)
            for p in range(PAIRS):
                b = p % 2
                need(g, s["ul_done"], p - 1)
                g.tensor_scalar(UF[b], X[:, p, :], SB[:, p:p + 1], TB[:, p:p + 1], ALU.mult, ALU.add)\
                    .then_inc(s["u_ready"], 1)
                need(g, s["y1_done"], 2 * p - 2)
                g.tensor_scalar(GF[b], X[:, p, :], SC[:, p:p + 1], SH[:, p:p + 1], ALU.mult, ALU.add)\
                    .then_inc(s["g1_ready"], 1)
            power(3)
            g.wait_ge(s["coef_ready"], 4)

            def normed(q):
                need(g, s["e_mm"], 8 * q)
                g.tensor_scalar(GB, X[:, q, :], SC[:, q:q + 1], SH[:, q:q + 1], ALU.mult, ALU.add)\
                    .then_inc(s["gb_ready"], 1)

            def sums(p, lead=True):
                for j in (1, 2, 3, 5, 6, 7):
                    grp = j // 4
                    g.wait_ge(s["p_ready"], 4 * (CHUNKS * p + j) + 4)
                    if j % 4 == 1:
                        need(g, s["sum_mm"], 2 * p)
                    for par in range(2):
                        first = PT[(j - 1) % SLOTS][par] if j % 4 == 1 else SA[grp][par]
                        i = g.tensor_tensor(SA[grp][par], first, PT[j % SLOTS][par], ALU.add)
                    i.then_inc(s["add_done"], 1)
                    g.wait_ge(s["add_done"], 6 * p + (0, 1, 2, 3, 0, 4, 5, 6)[j])
                    if j == 3 and lead:
                        normed(p + 2)

            normed(0)
            normed(1)
            for p in range(PAIRS):
                sums(p, p + 2 < PAIRS)

            power(4)
            g.memset(RB[:, PAIRS * L + 2 * CG * P:2 * PAIRS * L], 0.0).then_inc(s["am_zero"], 1)
            g.wait_ge(s["coef_ready"], 5)
            for p in (2, 3, 6, 7):
                g.tensor_scalar(G3[:, p, :], X[:, p, :], SC[:, p:p + 1], SH[:, p:p + 1], ALU.mult, ALU.add)\
                    .then_inc(s["g3_pool"], 1)

        @block.tensor
        def _(t):
            mm = t.matmul

            def group(turn):
                t.wait_ge(s["stat_ready"], turn + 1)
                if turn == 2:
                    i = mm(PS[:, 7, 0:2], mat("batch"), BS)
                else:
                    i = mm(PS[:, 7, 0:2 * PAIRS], mat("pairs"), MV.rearrange("p a b -> p (a b)"))
                i.then_inc(s["group_mm"], 1)

            t.wait_ge(s["packed"], 16)
            mm(PS[:, 6, 0:P], W[0:2 * RANK, OFF["dtl"]:OFF["dtl"] + P],
               W[0:2 * RANK, OFF["dtr"]:OFF["dtr"] + P]).then_inc(s["wdt_mm"], 1)
            group(0)
            t.wait_ge(s["coef_ready"], 1)

            def project(p, b):
                t.wait_ge(s["g_ready"], p + 1)
                need(t, s["taps_done"], p - 1)
                need(t, s["siluz_done"], p - 1)
                for w, o in (("winx", 0), ("winz", 2)):
                    for h in range(2):
                        i = mm(bank(4 * b + o + h), mat(w), G[b][:, h * HALF:(h + 1) * HALF])
                i.then_inc(s["xz_mm"], 1)

            project(0, 0)
            project(1, 1)
            with t.Fori(1, PAIRS // 2) as k:
                project(2 * k, 0)
                project(2 * k + 1, 1)

            t.wait_ge(s["silux_done"], PAIRS)
            t.wait_ge(s["siluz_done"], PAIRS)
            t.wait_ge(s["setup_done"], 1)

            def dt(p, h):
                n = 2 * p + h
                need(t, s["dt_read"], n)
                need(t, s["dta_read"], n)
                mm(bank(0), WDT[:, :], half(XS, p, h)).then_inc(s["dt_mm"], 1)

            def states(p, h, o):
                n = 2 * p + h
                need(t, s["c_read" if o else "b_read"], n)
                for j in range(STATE):
                    i = mm(bank(1 + 2 * o + j), mat("bc%d" % (2 * o + j)), half(XS, p, h))
                i.then_inc(s["c_mm" if o else "b_mm"], 1)

            def project_out(p, h):
                n = 2 * p + h
                t.wait_ge(s["y_done"], n + 1)
                need(t, s["o_read"], n)
                mm(bank(5), mat("wout"), tY[h]).then_inc(s["o_mm"], 1)

            def variance(p, h):
                n = 2 * p + h
                t.wait_ge(s["sq_done"], n + 1)
                need(t, s["r_done"], n)
                mm(bank(6), mat("mean64"), tQ[h]).then_inc(s["v_mm"], 1)

            def turn(p, h, lead=True, lag=True):
                if lead:
                    dt(*after(p, h))
                if lag:
                    project_out(*before(p, h))
                if lead:
                    states(*after(p, h), 0)
                if lag:
                    variance(*before(p, h))
                if lead:
                    states(*after(p, h), 1)

            dt(0, 0)
            states(0, 0, 0)
            states(0, 0, 1)
            turn(0, 0, lag=False)
            turn(0, 1)
            with t.Fori(1, PAIRS - 1) as p:
                turn(p, 0)
                turn(p, 1)
            turn(PAIRS - 1, 0)
            turn(PAIRS - 1, 1, lead=False)
            project_out(PAIRS - 1, 1)
            variance(PAIRS - 1, 1)
            group(1)
            group(2)

            t.wait_ge(s["coef_ready"], 3)

            def conv(p, b, h):
                if h == 0:
                    t.wait_ge(s["uh_done"], p + 1)
                    t.wait_ge(s["ul_done"], p + 1)
                need(t, s["y1_done"], 2 * p + h - 3)
                rows = HH // 2
                for n, (w, u) in enumerate(((0, UH), (0, UL), (1, UH))):
                    for tap in range(9):
                        y, xx = divmod(tap, 3)
                        i = mm(PS[:, 2 * b + h, :].rearrange("p (y x) -> p y x", y=rows), WS[:, w, tap, :],
                               u[b][:, h * rows + y:h * rows + y + rows, xx:xx + WW],
                               start=(n == 0 and tap == 0), stop=(n == 2 and tap == 8))
                i.then_inc(s["conv_mm"], 1)

            def pointwise(p, b, h):
                t.wait_ge(s["y1_done"], 2 * p + h + 1)
                mm(bank(4 + 2 * b + h), mat("w11"), YF[b][:, h * HALF:(h + 1) * HALF]).then_inc(s["w1_mm"], 1)

            def turn1(p, b, lag=True):
                conv(p, b, 0)
                conv(p, b, 1)
                if lag:
                    pointwise(p - 1, 1 - b, 0)
                    pointwise(p - 1, 1 - b, 1)

            turn1(0, 0, lag=False)
            turn1(1, 1)
            with t.Fori(1, PAIRS // 2) as k:
                turn1(2 * k, 0)
                turn1(2 * k + 1, 1)
            pointwise(PAIRS - 1, 1, 0)
            pointwise(PAIRS - 1, 1, 1)
            group(3)

            t.wait_ge(s["coef_ready"], 4)
            t.wait_ge(s["minus_done"], 1)

            def values(q):
                t.wait_ge(s["gb_ready"], q + 1)
                if not (isinstance(q, int) and q == 0):
                    t.wait_ge(s["e_read"], 8 * q)
                    need(t, s["sum_read"], 2 * q - 2)
                for c in range(CHUNKS):
                    i = mm(PS[:, 6 + c // 4, (c % 4) * P:(c % 4 + 1) * P], GB[:, c * P:(c + 1) * P], mat("wa"))
                    if c % 4 == 3:
                        i.then_inc(s["asm_mm"], 1)

            def operand(q, tile):
                e, h = divmod(tile, 2)
                if tile == 0:
                    t.wait_ge(s["asm_read"], 2 * q + 2)
                else:
                    t.wait_ge(s["e_read"], 8 * q + 2 * tile)
                for par in range(2):
                    r = slice(par * C, (par + 1) * C)
                    mm(PS[0:96, 6 + par, :], W[r, OFF["e1w"] + e * P:OFF["e1w"] + e * P + 96],
                       GB[r, h * HALF:(h + 1) * HALF]).then_inc(s["e_mm"], 1)

            def rows(q, b, n):
                par, tile = divmod(n, CHUNKS)
                if n == 0:
                    t.wait_ge(s["lo_done"], 8 * q + 8)
                    need(t, s["m_copied"], 4 * q)
                for h in range(2):
                    if n:
                        t.wait_ge(s["s_read"], 32 * q + 2 * n + h - 1)
                    if n == ROWS_SEEN + 1:
                        t.wait_ge(s["m_copied"], 4 * q + h + 1)
                    mm(bank(2 + h), stack(b, par, 0)[0:96, tile * P:(tile + 1) * P],
                       stack(b, par, 1)[0:96, h * HALF:(h + 1) * HALF]).then_inc(s["s_mm"], 1)
                if n == ROWS_SEEN:
                    max_rows(q, 0)

            def max_rows(q, par):
                t.wait_ge(s["m_ready"], 2 * q + par + 1)
                for h in range(2):
                    if par:
                        t.wait_ge(s["m_copied"], 4 * q + h + 1)
                    else:
                        t.wait_ge(s["s_read"], 32 * q + 2 * ROWS_SEEN + h + 1)
                    for c in range(4):
                        i = mm(PS[96:98, 2 + h, c * P:(c + 1) * P], MB[:, par, 4 * h + c, :], IB[:, :])
                    i.then_inc(s["mrow_mm"], 1)

            def scores(p, b, j, par):
                if j == 0:
                    t.wait_ge(s["m_copied"], 4 * p + 2 + 2 * par)
                for h in range(2):
                    n = 4 * (CHUNKS * p + j) + 2 * par + h
                    need(t, s["p_ready"], n - 1)
                    mm(bank(4 + h), stack(b, par, 1)[0:98, j * P:(j + 1) * P],
                       stack(b, par, 0)[0:98, h * HALF:(h + 1) * HALF]).then_inc(s["t_mm"], 1)

            def products(p, b, j, h):
                n = CHUNKS * p + j
                if h == 0:
                    t.wait_ge(s["p_ready"], 4 * n + 4)
                if j == 0 and h == 0:
                    t.wait_ge(s["v_done"], 2 * p + 2)
                    need(t, s["acc_read"], 2 * p)
                for par in range(2):
                    i = mm(PS[par * C:(par + 1) * C, h, :], V[b][:, j, par * C:(par + 1) * C],
                           PT[j % SLOTS][par][:, h * HALF:(h + 1) * HALF],
                           start=(j == 0), stop=(j == CHUNKS - 1))
                if h == 1:
                    i.then_inc(s["pv_done"], 1)

            def sums(p):
                t.wait_ge(s["add_done"], 6 * p + 6)
                if isinstance(p, int) and p == PAIRS - 1:
                    t.wait_ge(s["e_read"], 8 * PAIRS)
                else:
                    t.wait_ge(s["e_read"], 8 * p + 16)
                for h in range(2):
                    for grp in range(2):
                        for par in range(2):
                            i = mm(PS[par * C:(par + 1) * C, 6 + h, :], mat("ones", C),
                                   SA[grp][par][:, h * HALF:(h + 1) * HALF], start=(grp == 0), stop=(grp == 1))
                    i.then_inc(s["sum_mm"], 1)

            def attend(p, b, lead=True, lag=True):
                unit = 0
                for n in range(2 * CHUNKS + 4):
                    if n < 2 * CHUNKS:
                        scores(p, b, n // 2, n % 2)
                    if n >= 4:
                        products(p, b, n // 2 - 2, n % 2)
                    if n == 0 and lag:
                        sums(p - 1)
                    if n == 1 and lead:
                        values(p + 1)
                    if n in OPERANDS_AT and lead:
                        operand(p + 1, OPERANDS_AT.index(n))
                    for _ in range(ROWS_AT.get(n, 0) if lead else 0):
                        rows(p + 1, 1 - b, unit)
                        unit += 1
                assert unit == (2 * CHUNKS if lead else 0)
                if lead:
                    max_rows(p + 1, 1)

            OPERANDS_AT = (2, 4, 6, 7)
            ROWS_AT = {n: 2 for n in range(9, 16)} | {16: 1, 17: 1}
            ROWS_SEEN = 13
            values(0)
            for tile in range(4):
                operand(0, tile)
            for n in range(2 * CHUNKS):
                rows(0, 0, n)
            max_rows(0, 1)
            attend(0, 0, lag=False)
            with t.Fori(0, PAIRS // 2 - 1) as k:
                attend(2 * k + 1, 1)
                attend(2 * k + 2, 0)
            attend(PAIRS - 1, 1, lead=False)
            sums(PAIRS - 1)
            group(4)

            t.wait_ge(s["coef_ready"], 5)

            for n in range(16):
                q, xb = divmod(n, 8)
                if xb == 0:
                    t.wait_ge(s["g3_act"], 2 * q + 2)
                    t.wait_ge(s["g3_pool"], 2 * q + 2)
                if n >= 4:
                    t.wait_ge(s["tr_dve" if n % 2 else "tr_act"], (n - 4) // 2 + 1)
                for c in range(4):
                    xx = 4 * xb + c
                    src = G3[:, 4 * q:4 * q + 4, :].rearrange("p b (y x) -> p x (b y)", x=WW)[:, xx]
                    i = t.transpose(PS[:, n % 4, c * P:(c + 1) * P], src, mat("ident"))
                i.then_inc(s["tr_mm"], 1)

            def shift_y(n):
                if n % 4 == 0:
                    t.wait_ge(s["am_ready"], 2 * (n // 4) + 2)
                need(t, s["s1_copied"], n - 1)
                for c in range(4):
                    ch = 4 * n + c
                    i = mm(PS[:, n % 2, c * P:(c + 1) * P], D[:, ch, :], AM[ch // CG % 2][0][:, ch % CG, :])
                i.then_inc(s["s1_mm"], 1)

            def shift_x(n):
                t.wait_ge(s["s1_copied"], n + 1)
                need(t, s["s2_copied"], n - 1)
                for c in range(4):
                    ch = 4 * n + c
                    i = mm(PS[:, 2 + n % 2, c * P:(c + 1) * P], D1[n % 2][:, c * P:(c + 1) * P],
                           AM[ch // CG % 2][1][:, ch % CG, :])
                i.then_inc(s["s2_mm"], 1)

            t.wait_ge(s["tr_act"], 8)
            t.wait_ge(s["tr_dve"], 8)
            for n in range(17):
                if n < 16:
                    shift_y(n)
                if n:
                    shift_x(n - 1)
            t.wait_ge(s["s2_copied"], 16)
            for n in range(16):
                q, xb = divmod(n, 8)
                if n >= 4:
                    t.wait_ge(s["bk_dve" if n % 2 else "bk_act"], (n - 4) // 2 + 1)
                for c in range(4):
                    xx = 4 * xb + c
                    src = E[:, xx, 2 * q:2 * q + 2, :].rearrange("p a c -> p (a c)")
                    i = t.transpose(PS[:, n % 4, c * P:(c + 1) * P], src, mat("ident"))
                i.then_inc(s["bk_mm"], 1)
            t.wait_ge(s["bk_act"], 8)
            t.wait_ge(s["bk_dve"], 8)
            for j in range(4):
                mm(bank(4 + j), mat("wpw"), half(S3, j // 2, j % 2)).then_inc(s["pw_mm"], 1)
            with t.Fori(1, PAIRS // 2) as k:
                for j in range(4):
                    t.wait_ge(s["res_done"], 4 * k + j - 3)
                    mm(bank(4 + j), mat("wpw"), half(S3, 2 * k + j // 2, j % 2)).then_inc(s["pw_mm"], 1)


def _packed(w):
    pack = np.zeros((P, NPACK), np.float32)

    def both(name, m):
        for par in range(2):
            o = OFF[name] + par * C
            pack[par * C:(par + 1) * C, o:o + m.shape[1]] = m

    def column(name, v, n=2):
        pack[:n * len(v), OFF[name]] = np.tile(v, n)

    win, wxp = w["L0_conv_W_in"], w["L0_conv_W_xproj"]
    both("winx", win[:C].T)
    both("winz", win[C:].T)
    for n in range(2 * STATE):
        both("bc%d" % n, np.broadcast_to(wxp[RANK + n][:, None], (C, C)))
    both("wout", w["L0_conv_W_out"].T)
    both("w11", w["L1_conv_w_1x1"][:, :, 0, 0].T)
    both("wpw", w["L3_conv_w_pw"].T)
    both("wa", w["L2_conv_wa"].T)
    pack[:, OFF["ba"]:OFF["ba"] + P] = np.tile(w["L2_conv_ba"], 2)[None]
    for name, m in (("e1w", w["L2_conv_w1"]), ("e2w", w["L2_conv_w2"])):
        pack[:, OFF[name]:OFF[name] + 3 * CR] = np.tile(m.T, (2, 3))
    for t in range(9):
        both("lbp%d" % t, w["L1_conv_w_lbp"][:, :, t // 3, t % 3].T)
    for par in range(2):
        r = slice(par * RANK, (par + 1) * RANK)
        pack[r, OFF["dtl"] + par * C:OFF["dtl"] + (par + 1) * C] = wxp[:RANK]
        pack[r, OFF["dtr"] + par * C:OFF["dtr"] + (par + 1) * C] = w["L0_conv_W_dt"].T
    pack[:, OFF["thy"]:OFF["thy"] + C] = w["L3_conv_theta_s"][None, :, 0]
    pack[:, OFF["thx"]:OFF["thx"] + C] = w["L3_conv_theta_s"][None, :, 1]
    for j in range(TAPS):
        column("cw%d" % j, w["L0_conv_conv_w"][:, 0, j])
    for name, key in (("cb", "L0_conv_conv_b"), ("bdt", "L0_conv_b_dt"), ("dpar", "L0_conv_D_param"),
                      ("lng", "L0_conv_ln_g"), ("lnb", "L0_conv_ln_b"), ("gamma", "L1_conv_gamma"),
                      ("beta", "L1_conv_beta"), ("b11", "L1_conv_b_1x1"), ("wdw", "L3_conv_w_dw")):
        column(name, w[key])
    for j in range(STATE):
        column("al%d" % j, w["L0_conv_A_log"][:, j])
    column("b1", w["L2_conv_b1"], 3)
    column("b2", w["L2_conv_b2"], 3)
    for name in ("a1", "a2", "aa"):
        pack[:, OFF[name]] = w["L2_conv_" + name]
    i = np.arange(P)
    pack[:, OFF["mean64"]:OFF["mean64"] + P] = (i[:, None] // C == i[None] // C) / C
    pack[:, OFF["pairs"]:OFF["pairs"] + P] = (i[:, None] // 2 == i[None] // 2) / 2
    pack[:, OFF["batch"]:OFF["batch"] + P] = (i[:, None] % C == i[None] % C) / IMAGES
    pack[:, OFF["ident"]:OFF["ident"] + P] = np.eye(P)
    pack[:, OFF["grid"]:OFF["grid"] + WW] = (i % HH)[:, None] - np.arange(WW)[None]
    pack[:, OFF["ones"]:OFF["ones"] + C] = 1
    return pack


def kernel(**inputs):
    import concourse.bacc as bacc
    from concourse.bass_utils import run_bass_kernel_spmd

    w = {k: np.asarray(v) for k, v in inputs.items()}
    arrays = {"x": np.ascontiguousarray(w["x"]), "pack": _packed(w)}
    nc = bacc.Bacc("TRN2", target_bir_lowering=False, num_devices=1)
    args = [nc.dram_tensor(n, a.shape, F32, kind="ExternalInput").ap() for n, a in arrays.items()]
    args.append(nc.dram_tensor("out", arrays["x"].shape, F32, kind="ExternalOutput").ap())
    build(nc, *args)
    return run_bass_kernel_spmd(nc, [arrays], core_ids=[0]).results[0]["out"]
```

```python
import numpy as np
import concourse.bass as bass
from concourse import mybir
from concourse.alu_op_type import AluOpType as ALU
from contextlib import ExitStack

F32 = mybir.dt.float32
F32R = mybir.dt.float32r
BF16 = mybir.dt.bfloat16
ACT = mybir.ActivationFunctionType
AX = mybir.AxisListType

P = 128
IMAGES, C, HH, WW = 16, 64, 32, 32
L = HH * WW
HALF = L // 2
PAIRS = IMAGES // 2
STATE = 2
RANK = 4
TAPS = 4
CR = C // 2
CHUNKS = L // P
PW = WW + 2
EPS = 1e-5

MATS = (["winx", "winz"] + ["bc%d" % n for n in range(2 * STATE)] + ["wout", "w11", "wpw", "wa",
        "ba", "e12", "mean64", "pairs", "batch", "ident"])
COLS = ["cw0", "cw1", "cw2", "cw3", "cb", "bdt", "al0", "al1", "dpar", "lng", "lnb", "gamma",
        "beta", "b11", "b12", "a12", "aa", "wdw"]
OFF, _at = {}, 0
for _n in MATS:
    OFF[_n] = _at
    _at += P
for _n, _w in (("dtl", P), ("dtr", P), ("thy", C), ("thx", C), ("grid", WW), ("ones", C)):
    OFF[_n] = _at
    _at += _w
for _n in COLS:
    OFF[_n] = _at
    _at += 1
NPACK = _at


class Chain:

    def __init__(self, eng, sem):
        self.eng, self.sem, self.base, self.k, self.fixed = eng, sem, 0, 0, 0

    def link(self, ins):
        self.k += 1
        ins.then_inc(self.sem, 1)
        self.eng.wait_ge(self.sem, self.base + self.k)

    def enter(self, i, per):
        self.fixed, self.per = self.fixed + self.k, per
        self.base, self.k = self.fixed + i * per, 0

    def leave(self, turns):
        assert self.k == self.per, (self.k, self.per)
        self.fixed += turns * self.per
        self.base, self.k = self.fixed, 0


def need(eng, sem, value):
    if not (isinstance(value, int) and value <= 0):
        eng.wait_ge(sem, value)


def before(p, h):
    return (p, 0) if h else (p - 1, 1)


def after(p, h):
    return (p + 1, 0) if h else (p, 1)


def build(nc, x, pack, out):
    with ExitStack() as ctx:
        def sb(name, shape, dt=F32):
            return ctx.enter_context(nc.sbuf_tensor(name, shape, dt))

        X = sb("X", [P, PAIRS, L])
        W = sb("W", [P, NPACK])
        RA = sb("RA", [P, PAIRS, L])
        RB = sb("RB", [P, 2 * PAIRS * L])
        R = sb("R", [P, 12 * L], F32R)
        WS = sb("WS", [P, 2, 9, P], F32R)
        WDT = sb("WDT", [P, P])
        SM = sb("SM", [P, 512])
        EX = sb("EX", [P, 2 * L])
        MB = sb("MB", [P, 2, CHUNKS, 2], BF16)
        IB = sb("IB", [P, P], BF16)
        PS = ctx.enter_context(nc.psum_tensor("PS", [P, 8, HALF], F32))

        def mat(name, w=P):
            return W[:, OFF[name]:OFF[name] + w]

        def col(name, n=P):
            return W[0:n, OFF[name]:OFF[name] + 1]

        def bank(n):
            return PS[:, n, :]

        def two(n):
            return PS[:, n:n + 2, :].rearrange("p a b -> p (a b)")

        def pair(t, p):
            if isinstance(p, int):
                return t[:, p, :]
            return t[:, bass.ds(p, 1), :].rearrange("p a n -> p (a n)")

        def half(t, p, h):
            if isinstance(p, int):
                return t[:, p, h * HALF:(h + 1) * HALF]
            return t[:, bass.ds(p, 1), h * HALF:(h + 1) * HALF].rearrange("p a n -> p (a n)")

        at = [0]

        def small(*shape):
            n = int(np.prod(shape))
            v = SM[:, at[0]:at[0] + n]
            at[0] += n
            assert at[0] <= 512
            names = "abc"[:len(shape)]
            if len(shape) > 1:
                v = v.rearrange("p (%s) -> p %s" % (" ".join(names), " ".join(names)),
                                **dict(zip(names[:-1], shape)))
            return v

        BST = small(PAIRS, 2, 6)
        MV = small(PAIRS, 2)
        GS = small(PAIRS, 2)
        SQ = small(PAIRS)
        VAR = small(PAIRS)
        MHALF = small(PAIRS)
        SC = small(PAIRS)
        SH = small(PAIRS)
        SB = small(PAIRS)
        TB = small(PAIRS)
        BM = small(2, PAIRS)
        BS = small(2)
        BT = small(8)
        ANEG = small(STATE)
        AEXP = small(STATE)
        OMA = small(1)
        AB = small(1)
        MEANO = small(1)
        MX = small(2, CHUNKS, 2)
        MXX = small(2, CHUNKS)
        EPSC = small(1)
        ONE = small(1)

        XS = RA
        ZS = RB[:, 0:PAIRS * L].rearrange("p (a n) -> p a n", a=PAIRS)
        TMP = RB[:, PAIRS * L:2 * PAIRS * L]
        G = [TMP[:, b * L:(b + 1) * L] for b in range(2)]
        AC = [TMP[:, (2 + b) * L:(3 + b) * L] for b in range(2)]

        def temp(n):
            k = [2 * n, 2 * n + 1]
            return [TMP[:, i * HALF:(i + 1) * HALF] if i < 16 else EX[:, (i - 16) * HALF:(i - 15) * HALF]
                    for i in k]

        tE = temp(0)
        tU = temp(1)
        tM = temp(2)
        tA = list(zip(temp(3), temp(4)))
        tB = list(zip(temp(5), temp(6)))
        tQ = temp(7)
        tR = temp(8)
        tY = temp(9)
        LBP = TMP[:, 4 * L:4 * L + 9 * P]

        def padded(n):
            return R[:, n * PW * PW:(n + 1) * PW * PW].rearrange("p (a c) -> p a c", a=PW)
        UH, UL = [padded(0), padded(1)], [padded(2), padded(3)]
        UF = [TMP[:, b * L:(b + 1) * L] for b in range(2)]
        GF = [TMP[:, (2 + b) * L:(3 + b) * L] for b in range(2)]
        YF = [TMP[:, (4 + b) * L:(5 + b) * L] for b in range(2)]

        def inner(u):
            return u[:, 1:HH + 1, 1:WW + 1]

        def stack(b, par, e):
            k = 2 * par + e
            return R[:, (4 * b + k) * L:(4 * b + k + 1) * L]
        G3 = RA
        SLOTS = 4
        PT = [[RB[:, (2 * n + par) * L:(2 * n + par + 1) * L] for par in range(2)] for n in range(SLOTS)]
        SA = [[RB[:, (8 + 2 * g + par) * L:(9 + 2 * g + par) * L] for par in range(2)] for g in range(2)]
        V = [v.rearrange("p (c m) -> p c m", c=CHUNKS)
             for v in (RB[:, 12 * L:13 * L], RB[:, 13 * L:14 * L], RA[:, 4, :])]
        GB = [RB[:, 14 * L:15 * L], RA[:, 5, :], RA[:, 6, :]]
        RC = RB[:, 15 * L:16 * L]
        OT = [RA[:, 7, 0:HALF], RA[:, 7, HALF:L]]
        EQ, ER, EF, (VT, _) = [[RA[:, i, h * HALF:(h + 1) * HALF] for h in range(2)] for i in range(4)]
        ZH, ZL = [WS[:, i, :, :].rearrange("p a b -> p (a b)")[:, 0:L] for i in range(2)]
        STEPS = [(0, 0), (1, 0), (0, 1), (1, 1)] + [(j, par) for j in range(2, CHUNKS) for par in range(2)]
        LAST = [2, 3] + list(range(5, 2 * CHUNKS, 2))
        NMOVES = 12

        CG = 16
        D = RB[:, 0:PAIRS * L].rearrange("p (c g) -> p c g", c=C)
        AM = [[RB[:, PAIRS * L + (2 * n + a) * CG * P:PAIRS * L + (2 * n + a + 1) * CG * P]
               .rearrange("p (c m) -> p c m", c=CG) for a in range(2)] for n in range(2)]
        D1 = [EX[:, i * HALF:(i + 1) * HALF] for i in range(2)]
        HATV, HATW = [EX[:, i * HALF:(i + 1) * HALF].rearrange("p (c y) -> p c y", c=CG) for i in (2, 3)]
        E = RA.rearrange("p b n -> p (b n)").rearrange("p (x g c) -> p x g c", g=4, c=C)
        S3 = RB[:, 0:PAIRS * L].rearrange("p (b n) -> p b n", b=PAIRS)

        names = """packed lbp_in zero_done exp_a wdt_mm setup_done dve_step act_step pool_step
            stat_ready group_mm var_ready pow_done coef_ready
            g_ready xb_done xz_mm taps_done silux_done siluz_done
            dt_mm b_mm c_mm o_mm v_mm e_done dta_read u_done dt_read nd_done ln_done dt_done dtx_done
            b_read da_done scan_done c_read hc_done y_done sq_done r_done o_read blk0_done
            u_ready g1_ready uh_done ul_done conv_mm y1_done w1_mm x1_done
            minus_done gb_ready z_mm z_read zf_done hi_done lo_done stack_in asm_mm asm_read v_part v_done
            s_mm s_read m_ready
            mrow_mm m_copied t_mm p_ready pv_done add_done sum_mm sum_read rec_done acc_read x2_done
            g3_act g3_pool am_zero am_ready tr_mm tr_act tr_dve s1_mm s1_copied s2_mm s2_copied
            bk_mm bk_act bk_dve pw_mm res_done stored""".split()
        s = {n: ctx.enter_context(nc.semaphore(n)) for n in names}
        x_in = [ctx.enter_context(nc.semaphore("x_in%d" % p)) for p in range(PAIRS)]

        block = ctx.enter_context(nc.Block())
        xd = x.rearrange("(p two) c h w -> (two c) p (h w)", two=2)
        od = out.rearrange("(p two) c h w -> (two c) p (h w)", two=2)

        def transposed_out(copy, n):
            q, xb = divmod(n, 8)
            src = bank(n % 4).rearrange("p (x a c) -> p x a c", x=4, a=2)
            dst = D.rearrange("p c (q a x) -> p q x a c", q=2, a=2)[:, q, 4 * xb:4 * xb + 4]
            for a in range(2):
                last = copy(dst[:, :, a], src[:, :, a])
            return last

        def back_out(copy, n):
            q, xb = divmod(n, 8)
            src = bank(n % 4).rearrange("p (x b y) -> p x b y", x=4, b=4)
            dst = S3[:, 4 * q:4 * q + 4, :].rearrange("p b (y x) -> p x b y", x=WW)[:, 4 * xb:4 * xb + 4]
            return copy(dst, src)

        @block.sync
        def _(sp):
            sp.dma_start(W[:, :], pack[:, 0:NPACK]).then_inc(s["packed"], 16)
            sp.dma_start(LBP, pack[:, NPACK:NPACK + 9 * P]).then_inc(s["lbp_in"], 16)
            for p in range(PAIRS):
                sp.dma_start(X[:, p, :], xd[:, p, :]).then_inc(x_in[p], 16)

            def stacked(q, b):
                need(sp, s["t_mm"], 32 * q - 64)
                sp.wait_ge(s["hi_done"], 2 * q + 2)
                for src, places in ((ZH, ((0, 32), (0, 64))), (ZL, ((64,), (32,)))):
                    if src is ZL:
                        sp.wait_ge(s["lo_done"], 2 * q + 2)
                    for par in range(2):
                        for e in range(2):
                            for r in places[e]:
                                k = 2 * e + par
                                sp.dma_start(stack(b, par, e)[r:r + CR, :].bitcast(F32),
                                             src[k * CR:(k + 1) * CR, :].bitcast(F32))\
                                    .then_inc(s["stack_in"], 16)

            for q in range(3):
                stacked(q, q)
            with sp.Fori(1, 3) as k:
                for c in range(3):
                    stacked(3 * k + c, c)
            sp.wait_ge(s["stack_in"], 16 * NMOVES * (PAIRS + 1))

            for p in range(PAIRS):
                sp.wait_ge(s["res_done"], 2 * p + 2)
                sp.dma_start(od[:, p, :], X[:, p, :]).then_inc(s["stored"], 16)
            sp.wait_ge(s["stored"], 16 * PAIRS)

        @block.vector
        def _(v):
            ch = Chain(v, s["dve_step"])
            link = ch.link

            def coefs(turn):
                for p in range(PAIRS):
                    i = v.bn_aggr(MV[:, p, :], BST[:, p, :, :].rearrange("p h k -> p (h k)"))
                link(i)
                mean, var = MV[:, :, 0], MV[:, :, 1]
                link(v.tensor_tensor(SQ, mean, mean, ALU.mult))
                v.tensor_tensor(var, var, SQ, ALU.add).then_inc(s["stat_ready"], 1)
                v.wait_ge(s["group_mm"], turn + 1)
                link(v.tensor_copy(GS.rearrange("p a b -> p (a b)"), PS[:, 7, 0:2 * PAIRS]))
                link(v.tensor_tensor(SQ, GS[:, :, 0], GS[:, :, 0], ALU.mult))
                link(v.tensor_tensor(VAR, GS[:, :, 1], SQ, ALU.subtract))
                v.tensor_scalar(VAR, VAR, EPS, None, ALU.add).then_inc(s["var_ready"], 1)
                v.wait_ge(s["pow_done"], turn + 1)
                v.scalar_tensor_tensor(SH, GS[:, :, 0], -1.0, SC, ALU.mult, ALU.mult)\
                    .then_inc(s["coef_ready"], 1)
                v.wait_ge(s["coef_ready"], turn + 1)

            def stats(p, h):
                if isinstance(p, int):
                    return v.bn_stats(BST[:, p, h, :], half(X, p, h))
                return v.bn_stats(BST[:, bass.ds(p, 1), h, :].rearrange("p a k -> p (a k)"), half(X, p, h))

            link(v.memset(MHALF, -0.5))
            link(v.memset(EPSC, EPS))
            link(v.memset(ONE, 1.0))
            v.wait_ge(s["packed"], 16)
            link(v.tensor_copy(IB[:, :], mat("ident")))
            for par in range(2):
                q = slice(par * C, (par + 1) * C)
                o = slice(OFF["wout"] + par * C, OFF["wout"] + (par + 1) * C)
                link(v.tensor_reduce(MEANO[q], W[q, o], AX.X, ALU.add))
                link(v.tensor_scalar(MEANO[q], MEANO[q], 1.0 / C, None, ALU.mult))
                link(v.tensor_scalar(W[q, o], W[q, o], MEANO[q], None, ALU.subtract))
            link(v.tensor_scalar(OMA, col("a12"), -1.0, 1.0, ALU.mult, ALU.add))
            link(v.tensor_tensor(AB, col("a12"), col("b12"), ALU.mult))
            link(v.tensor_scalar(mat("wpw"), mat("wpw"), col("wdw"), None, ALU.mult))
            v.wait_ge(s["lbp_in"], 16)
            link(v.tensor_copy(WS[:, 0, :, :].rearrange("p a b -> p (a b)"), LBP))
            link(v.tensor_tensor(WS[:, 1, :, :].rearrange("p a b -> p (a b)"), LBP,
                                 WS[:, 0, :, :].rearrange("p a b -> p (a b)"), ALU.subtract))
            v.wait_ge(s["wdt_mm"], 1)
            link(v.tensor_copy(WDT[:, :], PS[:, 6, 0:P]))
            v.wait_ge(s["exp_a"], 1)
            v.tensor_scalar(ANEG, AEXP, -1.0, None, ALU.mult).then_inc(s["setup_done"], 1)
            v.wait_ge(s["setup_done"], 1)

            for p in range(PAIRS):
                v.wait_ge(x_in[p], 16)
                for h in range(2):
                    i = stats(p, h)
            link(i)
            coefs(0)

            def taps(p, b):
                v.wait_ge(s["xz_mm"], p + 1)
                need(v, s["silux_done"], p - 1)
                xp = two(4 * b)
                link(v.tensor_scalar(AC[b], xp, col("cw3"), col("cb"), ALU.mult, ALU.add))
                for j in (1, 2, 3):
                    i = v.scalar_tensor_tensor(AC[b][:, j:L], xp[:, 0:L - j], col("cw%d" % (3 - j)),
                                               AC[b][:, j:L], ALU.mult, ALU.add)
                    if j < 3:
                        link(i)
                i.then_inc(s["taps_done"], 1)

            taps(0, 0)
            taps(1, 1)
            with v.Fori(1, PAIRS // 2) as k:
                ch.enter(k - 1, 6)
                taps(2 * k, 0)
                taps(2 * k + 1, 1)
                ch.leave(PAIRS // 2 - 1)

            def soft(p, h):
                n = 2 * p + h
                v.wait_ge(s["u_done"], n + 1)
                v.scalar_tensor_tensor(tE[h], tU[h], -1.0, tE[h], ALU.add, ALU.subtract)\
                    .then_inc(s["nd_done"], 1)

            def inputs(p, h):
                n = 2 * p + h
                v.wait_ge(s["dtx_done"], n + 1)
                v.wait_ge(s["b_mm"], n + 1)
                for j in range(STATE):
                    i = v.tensor_tensor(tB[h][j], bank(1 + j), tU[h], ALU.mult)
                i.then_inc(s["b_read"], 1)

            def scan(p, h):
                n = 2 * p + h
                v.wait_ge(s["b_read"], n + 1)
                v.wait_ge(s["da_done"], n + 1)
                for j in range(STATE):
                    first = 0.0 if h == 0 else tB[0][j][:, HALF - 1:HALF]
                    i = v.tensor_tensor_scan(tB[h][j], tA[h][j], tB[h][j], first, ALU.mult, ALU.add)
                i.then_inc(s["scan_done"], 1)

            def outputs(p, h):
                n = 2 * p + h
                v.wait_ge(s["scan_done"], n + 1)
                v.wait_ge(s["c_mm"], n + 1)
                for j in range(STATE):
                    i = v.tensor_tensor(tA[h][j], bank(3 + j), tB[h][j], ALU.mult)
                i.then_inc(s["c_read"], 1)

            def skip(p, h):
                n = 2 * p + h
                v.wait_ge(s["c_read"], n + 1)
                v.scalar_tensor_tensor(tA[h][0], half(XS, p, h), col("dpar"), tA[h][0], ALU.mult, ALU.add)\
                    .then_inc(s["hc_done"], 1)

            def norm(p, h):
                n = 2 * p + h
                v.wait_ge(s["r_done"], n + 1)
                v.tensor_tensor(tR[h], bank(5), tR[h], ALU.mult).then_inc(s["o_read"], 1)

            def residual0(p, h):
                n = 2 * p + h
                v.wait_ge(s["o_read"], n + 1)
                v.scalar_tensor_tensor(half(X, p, h), tR[h], col("lng"), half(X, p, h), ALU.mult, ALU.add)\
                    .then_inc(s["blk0_done"], 1)

            def stats0(p, h):
                v.wait_ge(s["blk0_done"], 2 * p + h + 1)
                return stats(p, h)

            def turn(p, h, lead=True, lag=True):
                inputs(p, h)
                scan(p, h)
                outputs(p, h)
                skip(p, h)
                if lag:
                    norm(*before(p, h))
                if lead:
                    soft(p + 1, h)
                if lag:
                    residual0(*before(p, h))
                    stats0(*before(p, h))

            v.wait_ge(s["xb_done"], PAIRS)
            soft(0, 0)
            soft(0, 1)
            turn(0, 0, lag=False)
            turn(0, 1)
            with v.Fori(1, PAIRS - 1) as p:
                turn(p, 0)
                turn(p, 1)
            turn(PAIRS - 1, 0, lead=False)
            turn(PAIRS - 1, 1, lead=False)
            norm(PAIRS - 1, 1)
            residual0(PAIRS - 1, 1)
            link(stats0(PAIRS - 1, 1))

            coefs(1)
            mean, msq, b0, b1 = MV[:, :, 0], MV[:, :, 1], BM[:, 0, :], BM[:, 1, :]
            link(v.tensor_tensor(b0, mean, SC, ALU.mult))
            link(v.tensor_tensor(SQ, b0, SH, ALU.mult))
            link(v.tensor_tensor(b0, b0, SH, ALU.add))
            link(v.tensor_tensor(b1, msq, SC, ALU.mult))
            link(v.tensor_tensor(b1, b1, SC, ALU.mult))
            link(v.scalar_tensor_tensor(b1, SQ, 2.0, b1, ALU.mult, ALU.add))
            link(v.tensor_tensor(SQ, SH, SH, ALU.mult))
            link(v.tensor_tensor(b1, b1, SQ, ALU.add))
            v.tensor_reduce(BS, BM, AX.X, ALU.add).then_inc(s["stat_ready"], 1)
            v.wait_ge(s["group_mm"], 3)
            link(v.tensor_copy(BT[:, 0:2], PS[:, 7, 0:2]))
            link(v.tensor_tensor(BT[:, 2:3], BT[:, 0:1], BT[:, 0:1], ALU.mult))
            link(v.tensor_tensor(BT[:, 3:4], BT[:, 1:2], BT[:, 2:3], ALU.subtract))
            v.tensor_scalar(BT[:, 3:4], BT[:, 3:4], EPS, None, ALU.add).then_inc(s["var_ready"], 1)
            v.wait_ge(s["pow_done"], 3)
            link(v.tensor_tensor(BT[:, 5:6], BT[:, 4:5], col("gamma"), ALU.mult))
            link(v.tensor_tensor(BT[:, 6:7], BT[:, 5:6], BT[:, 0:1], ALU.mult))
            link(v.tensor_tensor(BT[:, 6:7], col("beta"), BT[:, 6:7], ALU.subtract))
            link(v.tensor_scalar(SB, SC, BT[:, 5:6], None, ALU.mult))
            v.tensor_scalar(TB, SH, BT[:, 5:6], BT[:, 6:7], ALU.mult, ALU.add).then_inc(s["coef_ready"], 1)
            v.wait_ge(s["coef_ready"], 3)

            def low(p, b):
                v.wait_ge(s["uh_done"], p + 1)
                need(v, s["conv_mm"], 2 * p - 2)
                v.tensor_tensor(inner(UL[b]), UF[b].rearrange("p (y x) -> p y x", y=HH), inner(UH[b]),
                                ALU.subtract).then_inc(s["ul_done"], 1)

            def relu(p, b):
                v.wait_ge(s["g1_ready"], p + 1)
                need(v, s["w1_mm"], 2 * p - 2)
                for h in range(2):
                    q = slice(h * HALF, (h + 1) * HALF)
                    v.wait_ge(s["conv_mm"], 2 * p + h + 1)
                    v.scalar_tensor_tensor(YF[b][:, q], bank(2 * b + h), 0.0, GF[b][:, q], ALU.max, ALU.add)\
                        .then_inc(s["y1_done"], 1)

            def add1(p, b):
                for h in range(2):
                    v.wait_ge(s["w1_mm"], 2 * p + h + 1)
                    v.scalar_tensor_tensor(half(X, p, h), bank(4 + 2 * b + h), col("b11"), half(X, p, h),
                                           ALU.add, ALU.add).then_inc(s["x1_done"], 1)
                v.wait_ge(s["x1_done"], 2 * p + 2)
                for h in range(2):
                    i = stats(p, h)
                return i

            def turn1(p, b, lead=True, lag=True):
                if lead:
                    low(p + 1, 1 - b)
                relu(p, b)
                if lag:
                    return add1(p - 1, 1 - b)

            low(0, 0)
            turn1(0, 0, lag=False)
            turn1(1, 1)
            with v.Fori(1, PAIRS // 2 - 1) as k:
                turn1(2 * k, 0)
                turn1(2 * k + 1, 1)
            turn1(PAIRS - 2, 0)
            turn1(PAIRS - 1, 1, lead=False)
            link(add1(PAIRS - 1, 1))
            coefs(3)

            for b in range(3):
                for par in range(2):
                    i = v.memset(stack(b, par, 1)[96:98, :].bitcast(F32), -1.0)
            i.then_inc(s["minus_done"], 1)

            def operands(q, h):
                v.wait_ge(s["z_read"], 2 * q + h + 1)
                need(v, s["hi_done"], 2 * q + h - 1)
                need(v, s["lo_done"], 2 * q + h - 1)
                v.scalar_tensor_tensor(EF[h], ER[h], OMA, EQ[h], ALU.mult, ALU.add).then_inc(s["zf_done"], 1)

            def biased(q, c):
                v.wait_ge(s["asm_mm"], 2 * q + c + 1)
                ba = mat("ba").unsqueeze(1).to_broadcast([P, CHUNKS // 2, P])
                v.tensor_tensor(VT.rearrange("p (c m) -> p c m", c=CHUNKS // 2),
                                bank(6 + c).rearrange("p (c m) -> p c m", c=CHUNKS // 2),
                                ba, ALU.add).then_inc(s["asm_read"], 1)

            def values(q, b, c):
                v.wait_ge(s["asm_read"], 2 * q + c + 1)
                vh = V[b][:, c * 4:c * 4 + 4, :].rearrange("p c m -> p (c m)")
                v.tensor_scalar(vh, VT, 0.0, col("aa"), ALU.min, ALU.mult).then_inc(s["v_part"], 1)
                v.wait_ge(s["v_part"], 2 * q + c + 1)
                v.scalar_tensor_tensor(vh, VT, 0.0, vh, ALU.max, ALU.add).then_inc(s["v_done"], 1)
                v.wait_ge(s["v_done"], 2 * q + c + 1)

            def maxima(q, n):
                par, tile = divmod(n, CHUNKS)
                for h in range(2):
                    v.wait_ge(s["s_mm"], 32 * q + 2 * n + h + 1)
                    v.tensor_reduce(MX[:, par, tile, h:h + 1], bank(2 + h), AX.X, ALU.max)\
                        .then_inc(s["s_read"], 1)

            def both_parts(q, par):
                v.wait_ge(s["s_read"], 32 * q + 16 * par + 16)
                need(v, s["mrow_mm"], 4 * q - 2 + 2 * par)
                link(v.tensor_reduce(MXX[:, par], MX[:, par], AX.X, ALU.max))
                link(v.tensor_copy(MB[:, par, :, 0], MXX[:, par]))
                v.tensor_tensor(MB[:, par, :, 1], MXX[:, par], MB[:, par, :, 0], ALU.subtract)\
                    .then_inc(s["m_ready"], 1)

            def scaled(p, h):
                v.wait_ge(s["acc_read"], 2 * p + h + 1)
                v.wait_ge(s["rec_done"], 2 * p + h + 1)
                link(v.tensor_tensor(OT[h], OT[h], RC[:, h * HALF:(h + 1) * HALF], ALU.mult))

            def residual(p, h):
                v.tensor_tensor(half(X, p, h), OT[h], half(X, p, h), ALU.add).then_inc(s["x2_done"], 1)

            def end_stats(p, h):
                v.wait_ge(s["x2_done"], 2 * p + h + 1)
                return stats(p, h)

            def attend(p, b, lead=True, lag=True):
                for n in range(2 * CHUNKS):
                    if lead:
                        maxima(p + 1, n)
                        if n in (2, 3):
                            operands(p + 2, n - 2)
                        if n in (7, 8):
                            biased(p + 1, n - 7)
                        if n in (7, 9):
                            values(p + 1, (b + 1) % 3, n // 9)
                        if n == 12:
                            both_parts(p + 1, 0)
                    if lag:
                        if n in (5, 6):
                            scaled(p - 1, n - 5)
                            residual(p - 1, n - 5)
                        if n in (10, 11):
                            end_stats(p - 1, n - 10)
                if lead:
                    both_parts(p + 1, 1)

            for q in range(2):
                for h in range(2):
                    operands(q, h)
            for c in range(2):
                biased(0, c)
                values(0, 0, c)
            for n in range(2 * CHUNKS):
                maxima(0, n)
                if n == 12:
                    both_parts(0, 0)
            both_parts(0, 1)
            attend(0, 0, lag=False)
            with v.Fori(0, 2) as k:
                ch.enter(k, 3 * 6)
                for c in range(3):
                    attend(3 * k + c + 1, (c + 1) % 3)
                ch.leave(2)
            attend(PAIRS - 1, 1, lead=False)
            for h in range(2):
                scaled(PAIRS - 1, h)
                residual(PAIRS - 1, h)
                i = end_stats(PAIRS - 1, h)
            link(i)
            coefs(4)

            v.memset(RB[:, PAIRS * L:PAIRS * L + 2 * CG * P], 0.0).then_inc(s["am_zero"], 1)
            v.wait_ge(s["am_zero"], 2)
            grid = mat("grid", WW).unsqueeze(1).to_broadcast([P, CG, WW])

            def hats(g):
                if g >= 2:
                    v.wait_ge(s["s2_mm"], (g - 1) * CG // 4)
                for a, th in ((0, "thy"), (1, "thx")):
                    tv = mat(th, C)[:, g * CG:(g + 1) * CG].unsqueeze(2).to_broadcast([P, CG, WW])
                    link(v.tensor_tensor(HATV, grid, tv, ALU.add))
                    link(v.tensor_scalar(HATW, HATV, -1.0, 1.0, ALU.mult, ALU.add))
                    link(v.scalar_tensor_tensor(HATW, HATV, 1.0, HATW, ALU.add, ALU.min))
                    for q in range(4):
                        r = slice(32 * q, 32 * q + 32)
                        i = v.tensor_scalar(AM[g % 2][a][r, :, 32 * q:32 * q + 32], HATW[r], 0.0, None, ALU.max)
                    i.then_inc(s["am_ready"], 1)

            hats(0)
            for n in range(1, 16, 2):
                v.wait_ge(s["tr_mm"], n + 1)
                transposed_out(v.tensor_copy, n).then_inc(s["tr_dve"], 1)
            hats(1)
            for n in range(16):
                v.wait_ge(s["s1_mm"], n + 1)
                need(v, s["s2_mm"], n - 1)
                v.tensor_copy(D1[n % 2], bank(n % 2)).then_inc(s["s1_copied"], 1)
                if n in (5, 9):
                    hats(2 + n // 9)
            for n in range(1, 16, 2):
                v.wait_ge(s["bk_mm"], n + 1)
                back_out(v.tensor_copy, n).then_inc(s["bk_dve"], 1)
            with v.Fori(0, PAIRS // 2) as k:
                for j in range(4):
                    v.wait_ge(s["pw_mm"], 4 * k + j + 1)
                    v.tensor_tensor(half(X, 2 * k + j // 2, j % 2), bank(4 + j),
                                    half(X, 2 * k + j // 2, j % 2), ALU.add).then_inc(s["res_done"], 1)

        @block.scalar
        def _(a):
            act = a.activation
            ch = Chain(a, s["act_step"])
            link = ch.link
            a.wait_ge(s["packed"], 16)
            act(AEXP, W[:, OFF["al0"]:OFF["al0"] + STATE], ACT.Exp).then_inc(s["exp_a"], 1)

            def gates(p, b):
                a.wait_ge(s["xz_mm"], p + 1)
                act(pair(ZS, p), two(4 * b + 2), ACT.Silu).then_inc(s["siluz_done"], 1)
                a.wait_ge(s["taps_done"], p + 1)
                act(pair(XS, p), AC[b], ACT.Silu).then_inc(s["silux_done"], 1)

            with a.Fori(0, PAIRS // 2) as k:
                gates(2 * k, 0)
                gates(2 * k + 1, 1)

            a.preload_act_table_set("natural_log_exp_and_others")
            a.wait_ge(s["setup_done"], 1)

            def soft(p, h):
                n = 2 * p + h
                a.wait_ge(s["dt_mm"], n + 1)
                need(a, s["dt_done"], n - 1)
                act(tE[h], bank(0), ACT.Abs, bias=col("bdt")).then_inc(s["dta_read"], 1)
                need(a, s["da_done"], n - 1)
                need(a, s["dtx_done"], n - 1)
                act(tM[h], bank(0), ACT.Relu, bias=col("bdt")).then_inc(s["dt_read"], 1)
                a.wait_ge(s["dta_read"], n + 1)
                act(tE[h], tE[h], ACT.Exp, scale=-1.0).then_inc(s["e_done"], 1)
                a.wait_ge(s["e_done"], n + 1)
                need(a, s["b_read"], n - 1)
                act(tU[h], tE[h], ACT.Identity, bias=ONE).then_inc(s["u_done"], 1)

            def soft_log(p, h):
                n = 2 * p + h
                a.wait_ge(s["nd_done"], n + 1)
                act(tU[h], tU[h], ACT.Ln).then_inc(s["ln_done"], 1)

            def grow(p, h):
                n = 2 * p + h
                a.wait_ge(s["dt_done"], n + 1)
                need(a, s["y_done"], n - 1)
                for j in range(STATE):
                    i = act(tA[h][j], tM[h], ACT.Exp, scale=ANEG[:, j:j + 1])
                i.then_inc(s["da_done"], 1)

            def square(p, h):
                n = 2 * p + h
                a.wait_ge(s["o_mm"], n + 1)
                need(a, s["v_mm"], n - 1)
                act(tQ[h], bank(5), ACT.Square).then_inc(s["sq_done"], 1)

            def inverse_sd(p, h):
                n = 2 * p + h
                a.wait_ge(s["v_mm"], n + 1)
                need(a, s["blk0_done"], n - 1)
                link(act(tR[h], bank(6), ACT.Ln, bias=EPSC))
                act(tR[h], tR[h], ACT.Exp, scale=-0.5).then_inc(s["r_done"], 1)

            def turn(p, h, lead=True, lag=True):
                if lag:
                    square(*before(p, h))
                if lead:
                    soft(p + 1, h)
                if lag:
                    inverse_sd(*before(p, h))
                if lead or h == 0:
                    grow(*after(p, h))
                if lead:
                    soft_log(p + 1, h)

            for h in range(2):
                soft(0, h)
                soft_log(0, h)
            grow(0, 0)
            turn(0, 0, lag=False)
            turn(0, 1)
            with a.Fori(1, PAIRS - 1) as p:
                ch.enter(p - 1, 2)
                turn(p, 0)
                turn(p, 1)
                ch.leave(PAIRS - 2)
            turn(PAIRS - 1, 0, lead=False)
            turn(PAIRS - 1, 1, lead=False)
            square(PAIRS - 1, 1)
            inverse_sd(PAIRS - 1, 1)

            def high(p, b):
                a.wait_ge(s["u_ready"], p + 1)
                need(a, s["conv_mm"], 2 * p - 2)
                act(inner(UH[b]), UF[b].rearrange("p (y x) -> p y x", y=HH), ACT.Copy)\
                    .then_inc(s["uh_done"], 1)

            a.wait_ge(s["zero_done"], 1)
            high(0, 0)
            high(1, 1)
            with a.Fori(1, PAIRS // 2) as k:
                high(2 * k, 0)
                high(2 * k + 1, 1)

            a.wait_ge(s["coef_ready"], 4)

            def parts(q, h):
                a.wait_ge(s["z_mm"], 2 * q + h + 1)
                need(a, s["zf_done"], 2 * q + h - 1)
                act(EQ[h], bank(6 + h), ACT.Identity, bias=AB, scale=col("a12"))
                act(ER[h], bank(6 + h), ACT.Relu, bias=col("b12")).then_inc(s["z_read"], 1)

            def high_z(q, h):
                if h == 0:
                    need(a, s["stack_in"], 16 * NMOVES * q)
                a.wait_ge(s["zf_done"], 2 * q + h + 1)
                act(ZH[:, h * HALF:(h + 1) * HALF], EF[h], ACT.Copy).then_inc(s["hi_done"], 1)

            def probs(p, n):
                j, par = STEPS[n]
                slot = PT[j % SLOTS][par]
                if par == 0:
                    need(a, s["pv_done"], 2 * (CHUNKS * p + j - SLOTS + 1))
                    need(a, s["add_done"], 6 * p + (-2, -2, -1, 0, 1, 1, 2, 3)[j])
                for h in range(2):
                    a.wait_ge(s["t_mm"], 32 * p + 2 * n + h + 1)
                    act(slot[:, h * HALF:(h + 1) * HALF], bank(4 + h), ACT.Exp).then_inc(s["p_ready"], 1)

            def max_rows(q, b, par):
                for h in range(2):
                    a.wait_ge(s["mrow_mm"], 4 * q + 2 * par + h + 1)
                    act(stack(b, par, 0)[96:98, h * HALF:(h + 1) * HALF], PS[96:98, 6 + h, :],
                        ACT.Copy).then_inc(s["m_copied"], 1)

            def product_out(p, h):
                a.wait_ge(s["pv_done"], 2 * CHUNKS * p + 2 * CHUNKS - 1 + h)
                if isinstance(p, int) and p == PAIRS - 1:
                    a.wait_ge(s["x2_done"], 2 * p + h - 1)
                act(OT[h], bank(h), ACT.Copy).then_inc(s["acc_read"], 1)

            def inverse(p, h):
                n = 2 * p + h
                q = slice(h * HALF, (h + 1) * HALF)
                a.wait_ge(s["sum_mm"], n + 1)
                act(RC[:, q], bank(6 + h), ACT.Ln).then_inc(s["sum_read"], 1)
                a.wait_ge(s["sum_read"], n + 1)
                act(RC[:, q], RC[:, q], ACT.Exp, scale=-1.0).then_inc(s["rec_done"], 1)

            def attend(p, b, lead=True, lag=True):
                for n in range(2 * CHUNKS):
                    probs(p, n)
                    if n == 0:
                        max_rows(p, b, 1)
                    if n in (1, 2) and lead:
                        parts(p + 2, n - 1)
                    if n in (2, 3) and lag:
                        product_out(p - 1, n - 2)
                    if n in (3, 4) and lead:
                        high_z(p + 2, n - 3)
                    if n in (4, 5) and lag:
                        inverse(p - 1, n - 4)
                    if n == 15 and lead:
                        max_rows(p + 1, (b + 1) % 3, 0)

            for q in range(2):
                for h in range(2):
                    parts(q, h)
                for h in range(2):
                    high_z(q, h)
            max_rows(0, 0, 0)
            attend(0, 0, lag=False)
            with a.Fori(0, 2) as k:
                for c in range(3):
                    attend(3 * k + c + 1, (c + 1) % 3)
            attend(PAIRS - 1, 1, lead=False)
            for h in range(2):
                product_out(PAIRS - 1, h)
            for h in range(2):
                inverse(PAIRS - 1, h)

            a.wait_ge(s["coef_ready"], 5)
            for p in (0, 1, 4, 5):
                act(G3[:, p, :], X[:, p, :], ACT.Identity, bias=SH[:, p:p + 1], scale=SC[:, p:p + 1])\
                    .then_inc(s["g3_act"], 1)

            def copy(o, i):
                return act(o, i, ACT.Copy)
            for n in range(0, 16, 2):
                a.wait_ge(s["tr_mm"], n + 1)
                transposed_out(copy, n).then_inc(s["tr_act"], 1)
            for n in range(16):
                a.wait_ge(s["s2_mm"], n + 1)
                act(E[:, :, :, 4 * n:4 * n + 4].rearrange("p x g c -> p c g x"),
                    bank(2 + n % 2).rearrange("p (c g x) -> p c g x", c=4, g=4), ACT.Copy)\
                    .then_inc(s["s2_copied"], 1)
            for n in range(0, 16, 2):
                a.wait_ge(s["bk_mm"], n + 1)
                back_out(copy, n).then_inc(s["bk_act"], 1)

        @block.gpsimd
        def _(g):
            ch = Chain(g, s["pool_step"])
            link = ch.link

            def power(turn):
                g.wait_ge(s["var_ready"], turn + 1)
                if turn == 2:
                    g.tensor_tensor(BT[:, 4:5], BT[:, 3:4], MHALF[:, 0:1], ALU.pow).then_inc(s["pow_done"], 1)
                else:
                    g.tensor_tensor(SC, VAR, MHALF, ALU.pow).then_inc(s["pow_done"], 1)

            g.memset(R[:, 0:4 * PW * PW].bitcast(F32), 0.0).then_inc(s["zero_done"], 1)

            power(0)
            g.wait_ge(s["coef_ready"], 1)
            for p in range(PAIRS):
                need(g, s["xz_mm"], p - 1)
                g.tensor_scalar(G[p % 2], X[:, p, :], SC[:, p:p + 1], SH[:, p:p + 1], ALU.mult, ALU.add)\
                    .then_inc(s["g_ready"], 1)
                g.wait_ge(s["g_ready"], p + 1)
                g.tensor_scalar(X[:, p, :], X[:, p, :], col("lnb"), None, ALU.add).then_inc(s["xb_done"], 1)

            def soft(p, h):
                n = 2 * p + h
                g.wait_ge(s["ln_done"], n + 1)
                g.wait_ge(s["dt_read"], n + 1)
                link(g.tensor_tensor(tM[h], tM[h], tU[h], ALU.add))
                g.tensor_tensor(tM[h], tM[h], tE[h], ALU.subtract).then_inc(s["dt_done"], 1)
                g.wait_ge(s["dt_done"], n + 1)
                g.tensor_tensor(tU[h], tM[h], half(XS, p, h), ALU.mult).then_inc(s["dtx_done"], 1)

            def output(p, h):
                n = 2 * p + h
                g.wait_ge(s["hc_done"], n + 1)
                need(g, s["o_mm"], n - 1)
                link(g.tensor_tensor(tY[h], tA[h][0], tA[h][1], ALU.add))
                g.tensor_tensor(tY[h], tY[h], half(ZS, p, h), ALU.mult).then_inc(s["y_done"], 1)

            g.wait_ge(s["silux_done"], PAIRS)
            g.wait_ge(s["siluz_done"], PAIRS)
            soft(0, 0)
            soft(0, 1)
            output(0, 0)
            with g.Fori(1, PAIRS) as p:
                ch.enter(p - 1, 4)
                soft(p, 0)
                output(p - 1, 1)
                soft(p, 1)
                output(p, 0)
                ch.leave(PAIRS - 1)
            output(PAIRS - 1, 1)

            power(1)
            power(2)
            g.wait_ge(s["coef_ready"], 3)
            for p in range(PAIRS):
                b = p % 2
                need(g, s["ul_done"], p - 1)
                g.tensor_scalar(UF[b], X[:, p, :], SB[:, p:p + 1], TB[:, p:p + 1], ALU.mult, ALU.add)\
                    .then_inc(s["u_ready"], 1)
                need(g, s["y1_done"], 2 * p - 2)
                g.tensor_scalar(GF[b], X[:, p, :], SC[:, p:p + 1], SH[:, p:p + 1], ALU.mult, ALU.add)\
                    .then_inc(s["g1_ready"], 1)
            power(3)
            g.wait_ge(s["coef_ready"], 4)

            def normed(q):
                need(g, s["asm_mm"], 2 * q - 4)
                m = min(q, PAIRS - 1)
                g.tensor_scalar(GB[q % 3], X[:, m, :], SC[:, m:m + 1], SH[:, m:m + 1], ALU.mult, ALU.add)\
                    .then_inc(s["gb_ready"], 1)

            def low_z(q):
                for h in range(2):
                    g.wait_ge(s["hi_done"], 2 * q + h + 1)
                    if h == 0:
                        need(g, s["stack_in"], 16 * NMOVES * q)
                    cols = slice(h * HALF, (h + 1) * HALF)
                    g.tensor_tensor(ZL[:, cols], EF[h], ZH[:, cols], ALU.subtract).then_inc(s["lo_done"], 1)

            def sums(p):
                for j in (1, 2, 3, 5, 6, 7):
                    grp = j // 4
                    g.wait_ge(s["p_ready"], 32 * p + 2 * LAST[j] + 2)
                    if j % 4 == 1:
                        need(g, s["sum_mm"], 2 * p)
                    for par in range(2):
                        first = PT[(j - 1) % SLOTS][par] if j % 4 == 1 else SA[grp][par]
                        i = g.tensor_tensor(SA[grp][par], first, PT[j % SLOTS][par], ALU.add)
                    i.then_inc(s["add_done"], 1)
                    g.wait_ge(s["add_done"], 6 * p + (0, 1, 2, 3, 0, 4, 5, 6)[j])
                    if j == 3 and p < PAIRS - 1:
                        low_z(p + 2)

            for q in range(3):
                normed(q)
            for q in range(2):
                low_z(q)
            for p in range(PAIRS):
                if p < PAIRS - 2:
                    normed(p + 3)
                sums(p)

            power(4)
            g.memset(RB[:, PAIRS * L + 2 * CG * P:2 * PAIRS * L], 0.0).then_inc(s["am_zero"], 1)
            g.wait_ge(s["coef_ready"], 5)
            for p in (2, 3, 6, 7):
                g.tensor_scalar(G3[:, p, :], X[:, p, :], SC[:, p:p + 1], SH[:, p:p + 1], ALU.mult, ALU.add)\
                    .then_inc(s["g3_pool"], 1)

        @block.tensor
        def _(t):
            mm = t.matmul

            def group(turn):
                t.wait_ge(s["stat_ready"], turn + 1)
                if turn == 2:
                    i = mm(PS[:, 7, 0:2], mat("batch"), BS)
                else:
                    i = mm(PS[:, 7, 0:2 * PAIRS], mat("pairs"), MV.rearrange("p a b -> p (a b)"))
                i.then_inc(s["group_mm"], 1)

            t.wait_ge(s["packed"], 16)
            mm(PS[:, 6, 0:P], W[0:2 * RANK, OFF["dtl"]:OFF["dtl"] + P],
               W[0:2 * RANK, OFF["dtr"]:OFF["dtr"] + P]).then_inc(s["wdt_mm"], 1)
            group(0)
            t.wait_ge(s["coef_ready"], 1)

            def project(p, b):
                t.wait_ge(s["g_ready"], p + 1)
                need(t, s["taps_done"], p - 1)
                need(t, s["siluz_done"], p - 1)
                for w, o in (("winx", 0), ("winz", 2)):
                    for h in range(2):
                        i = mm(bank(4 * b + o + h), mat(w), G[b][:, h * HALF:(h + 1) * HALF])
                i.then_inc(s["xz_mm"], 1)

            project(0, 0)
            project(1, 1)
            with t.Fori(1, PAIRS // 2) as k:
                project(2 * k, 0)
                project(2 * k + 1, 1)

            t.wait_ge(s["silux_done"], PAIRS)
            t.wait_ge(s["siluz_done"], PAIRS)
            t.wait_ge(s["setup_done"], 1)

            def dt(p, h):
                n = 2 * p + h
                need(t, s["dt_read"], n)
                mm(bank(0), WDT[:, :], half(XS, p, h)).then_inc(s["dt_mm"], 1)

            def states(p, h, o):
                n = 2 * p + h
                need(t, s["c_read" if o else "b_read"], n)
                for j in range(STATE):
                    i = mm(bank(1 + 2 * o + j), mat("bc%d" % (2 * o + j)), half(XS, p, h))
                i.then_inc(s["c_mm" if o else "b_mm"], 1)

            def project_out(p, h):
                n = 2 * p + h
                t.wait_ge(s["y_done"], n + 1)
                need(t, s["o_read"], n)
                mm(bank(5), mat("wout"), tY[h]).then_inc(s["o_mm"], 1)

            def variance(p, h):
                n = 2 * p + h
                t.wait_ge(s["sq_done"], n + 1)
                need(t, s["r_done"], n)
                mm(bank(6), mat("mean64"), tQ[h]).then_inc(s["v_mm"], 1)

            def turn(p, h, lead=True, lag=True):
                if lag:
                    project_out(*before(p, h))
                if lead:
                    dt(p + 1, h)
                if lag:
                    variance(*before(p, h))
                if lead or h == 0:
                    states(*after(p, h), 0)
                    states(*after(p, h), 1)

            dt(0, 0)
            states(0, 0, 0)
            states(0, 0, 1)
            dt(0, 1)
            turn(0, 0, lag=False)
            turn(0, 1)
            with t.Fori(1, PAIRS - 1) as p:
                turn(p, 0)
                turn(p, 1)
            turn(PAIRS - 1, 0, lead=False)
            turn(PAIRS - 1, 1, lead=False)
            project_out(PAIRS - 1, 1)
            variance(PAIRS - 1, 1)
            group(1)
            group(2)

            t.wait_ge(s["coef_ready"], 3)

            def conv(p, b, h):
                if h == 0:
                    t.wait_ge(s["uh_done"], p + 1)
                    t.wait_ge(s["ul_done"], p + 1)
                need(t, s["y1_done"], 2 * p + h - 3)
                rows = HH // 2
                for n, (w, u) in enumerate(((0, UH), (0, UL), (1, UH))):
                    for tap in range(9):
                        y, xx = divmod(tap, 3)
                        i = mm(PS[:, 2 * b + h, :].rearrange("p (y x) -> p y x", y=rows), WS[:, w, tap, :],
                               u[b][:, h * rows + y:h * rows + y + rows, xx:xx + WW],
                               start=(n == 0 and tap == 0), stop=(n == 2 and tap == 8))
                i.then_inc(s["conv_mm"], 1)

            def pointwise(p, b, h):
                t.wait_ge(s["y1_done"], 2 * p + h + 1)
                mm(bank(4 + 2 * b + h), mat("w11"), YF[b][:, h * HALF:(h + 1) * HALF]).then_inc(s["w1_mm"], 1)

            def turn1(p, b, lag=True):
                conv(p, b, 0)
                conv(p, b, 1)
                if lag:
                    pointwise(p - 1, 1 - b, 0)
                    pointwise(p - 1, 1 - b, 1)

            turn1(0, 0, lag=False)
            turn1(1, 1)
            with t.Fori(1, PAIRS // 2) as k:
                turn1(2 * k, 0)
                turn1(2 * k + 1, 1)
            pointwise(PAIRS - 1, 1, 0)
            pointwise(PAIRS - 1, 1, 1)
            group(3)

            t.wait_ge(s["coef_ready"], 4)
            t.wait_ge(s["minus_done"], 1)

            def operands(q, b, h):
                if h == 0:
                    t.wait_ge(s["gb_ready"], q + 1)
                    if isinstance(q, int) and q < 2:
                        need(t, s["z_read"], 2 * q)
                    else:
                        t.wait_ge(s["m_copied"], 4 * q - 4)
                mm(bank(6 + h), mat("e12"), GB[b][:, h * HALF:(h + 1) * HALF]).then_inc(s["z_mm"], 1)

            def values(q, b, h):
                if isinstance(q, int) and q < 2:
                    t.wait_ge(s["z_read"], 2 * q + 3 + h)
                else:
                    t.wait_ge(s["sum_read"], 2 * q - 3 + h)
                for c in range(CHUNKS // 2):
                    at = h * HALF + c * P
                    i = mm(PS[:, 6 + h, c * P:(c + 1) * P], GB[b][:, at:at + P], mat("wa"))
                i.then_inc(s["asm_mm"], 1)

            def rows(q, b, n, h):
                par, tile = divmod(n, CHUNKS)
                if n == 0 and h == 0:
                    t.wait_ge(s["stack_in"], 16 * NMOVES * q + 16 * NMOVES)
                need(t, s["s_read"], 32 * q + 2 * n + h - 1)
                mm(bank(2 + h), stack(b, par, 0)[0:96, tile * P:(tile + 1) * P],
                   stack(b, par, 1)[0:96, h * HALF:(h + 1) * HALF]).then_inc(s["s_mm"], 1)

            def max_rows(q, par):
                if par == 0:
                    t.wait_ge(s["asm_read"], 2 * q + 2)
                t.wait_ge(s["m_ready"], 2 * q + par + 1)
                for h in range(2):
                    if par:
                        t.wait_ge(s["m_copied"], 4 * q + h + 1)
                    for c in range(4):
                        i = mm(PS[96:98, 6 + h, c * P:(c + 1) * P], MB[:, par, 4 * h + c, :], IB[:, :])
                    i.then_inc(s["mrow_mm"], 1)

            def scores(p, b, n):
                j, par = STEPS[n]
                if j == 0:
                    t.wait_ge(s["m_copied"], 4 * p + 2 + 2 * par)
                for h in range(2):
                    need(t, s["p_ready"], 32 * p + 2 * n + h - 1)
                    mm(bank(4 + h), stack(b, par, 1)[0:98, j * P:(j + 1) * P],
                       stack(b, par, 0)[0:98, h * HALF:(h + 1) * HALF]).then_inc(s["t_mm"], 1)

            def products(p, b, j, h):
                if h == 0:
                    t.wait_ge(s["p_ready"], 32 * p + 2 * LAST[j] + 2)
                if j == 0:
                    t.wait_ge(s["v_done"], 2 * p + 2)
                    need(t, s["acc_read"], 2 * p + h - 1)
                for par in range(2):
                    i = mm(PS[par * C:(par + 1) * C, h, :], V[b][:, j, par * C:(par + 1) * C],
                           PT[j % SLOTS][par][:, h * HALF:(h + 1) * HALF],
                           start=(j == 0), stop=(j == CHUNKS - 1))
                i.then_inc(s["pv_done"], 1)

            def sums(p, h):
                if h == 0:
                    t.wait_ge(s["add_done"], 6 * p + 6)
                if isinstance(p, int) and p == PAIRS - 1:
                    t.wait_ge(s["sum_read"], 2 * p)
                elif isinstance(p, int) and p == PAIRS - 2:
                    t.wait_ge(s["m_copied"], 4 * PAIRS)
                else:
                    t.wait_ge(s["z_read"], 2 * p + 7 + h)
                for grp in range(2):
                    for par in range(2):
                        i = mm(PS[par * C:(par + 1) * C, 6 + h, :], mat("ones", C),
                               SA[grp][par][:, h * HALF:(h + 1) * HALF], start=(grp == 0), stop=(grp == 1))
                i.then_inc(s["sum_mm"], 1)

            def tail(p, b, n):
                products(p, b, CHUNKS - 2 + n // 2, n % 2)

            def attend(p, b, lead=True, lag=True):
                for n in range(2 * CHUNKS):
                    scores(p, b, n)
                    if lead:
                        rows(p + 1, (b + 1) % 3, n, 0)
                    if n >= 4:
                        products(p, b, n // 2 - 2, n % 2)
                    elif lag:
                        tail(p - 1, (b + 2) % 3, n)
                    if n == 0:
                        max_rows(p, 1)
                    if n in (1, 2) and lead:
                        operands(p + 2, (b + 2) % 3, n - 1)
                    if n in (4, 5) and lag:
                        sums(p - 1, n - 4)
                    if n in (6, 7) and lead:
                        values(p + 1, (b + 1) % 3, n - 6)
                    if n == 14 and lead:
                        max_rows(p + 1, 0)
                    if lead:
                        rows(p + 1, (b + 1) % 3, n, 1)

            for q in range(2):
                for h in range(2):
                    operands(q, q, h)
            for h in range(2):
                values(0, 0, h)
            for n in range(2 * CHUNKS):
                for h in range(2):
                    rows(0, 0, n, h)
                if n == 14:
                    max_rows(0, 0)
            attend(0, 0, lag=False)
            with t.Fori(0, 2) as k:
                for c in range(3):
                    attend(3 * k + c + 1, (c + 1) % 3)
            attend(PAIRS - 1, 1, lead=False)
            for n in range(4):
                tail(PAIRS - 1, 1, n)
            for h in range(2):
                sums(PAIRS - 1, h)
            group(4)

            t.wait_ge(s["coef_ready"], 5)

            for n in range(16):
                q, xb = divmod(n, 8)
                if xb == 0:
                    t.wait_ge(s["g3_act"], 2 * q + 2)
                    t.wait_ge(s["g3_pool"], 2 * q + 2)
                if n >= 4:
                    t.wait_ge(s["tr_dve" if n % 2 else "tr_act"], (n - 4) // 2 + 1)
                for c in range(4):
                    xx = 4 * xb + c
                    src = G3[:, 4 * q:4 * q + 4, :].rearrange("p b (y x) -> p x (b y)", x=WW)[:, xx]
                    i = t.transpose(PS[:, n % 4, c * P:(c + 1) * P], src, mat("ident"))
                i.then_inc(s["tr_mm"], 1)

            def shift_y(n):
                if n % 4 == 0:
                    t.wait_ge(s["am_ready"], 2 * (n // 4) + 2)
                need(t, s["s1_copied"], n - 1)
                for c in range(4):
                    ch = 4 * n + c
                    i = mm(PS[:, n % 2, c * P:(c + 1) * P], D[:, ch, :], AM[ch // CG % 2][0][:, ch % CG, :])
                i.then_inc(s["s1_mm"], 1)

            def shift_x(n):
                t.wait_ge(s["s1_copied"], n + 1)
                need(t, s["s2_copied"], n - 1)
                for c in range(4):
                    ch = 4 * n + c
                    i = mm(PS[:, 2 + n % 2, c * P:(c + 1) * P], D1[n % 2][:, c * P:(c + 1) * P],
                           AM[ch // CG % 2][1][:, ch % CG, :])
                i.then_inc(s["s2_mm"], 1)

            t.wait_ge(s["tr_act"], 8)
            t.wait_ge(s["tr_dve"], 8)
            for n in range(17):
                if n < 16:
                    shift_y(n)
                if n:
                    shift_x(n - 1)
            t.wait_ge(s["s2_copied"], 16)
            for n in range(16):
                q, xb = divmod(n, 8)
                if n >= 4:
                    t.wait_ge(s["bk_dve" if n % 2 else "bk_act"], (n - 4) // 2 + 1)
                for c in range(4):
                    xx = 4 * xb + c
                    src = E[:, xx, 2 * q:2 * q + 2, :].rearrange("p a c -> p (a c)")
                    i = t.transpose(PS[:, n % 4, c * P:(c + 1) * P], src, mat("ident"))
                i.then_inc(s["bk_mm"], 1)
            t.wait_ge(s["bk_act"], 8)
            t.wait_ge(s["bk_dve"], 8)
            for j in range(4):
                mm(bank(4 + j), mat("wpw"), half(S3, j // 2, j % 2)).then_inc(s["pw_mm"], 1)
            with t.Fori(1, PAIRS // 2) as k:
                for j in range(4):
                    t.wait_ge(s["res_done"], 4 * k + j - 3)
                    mm(bank(4 + j), mat("wpw"), half(S3, 2 * k + j // 2, j % 2)).then_inc(s["pw_mm"], 1)


def _packed(w):
    pack = np.zeros((P, NPACK + 9 * P), np.float32)

    def both(name, m):
        for par in range(2):
            o = (name if isinstance(name, int) else OFF[name]) + par * C
            pack[par * C:(par + 1) * C, o:o + m.shape[1]] = m

    def column(name, v, n=2):
        pack[:n * len(v), OFF[name]] = np.tile(v, n)

    win, wxp = w["L0_conv_W_in"], w["L0_conv_W_xproj"]
    both("winx", win[:C].T)
    both("winz", win[C:].T)
    for n in range(2 * STATE):
        both("bc%d" % n, np.broadcast_to(wxp[RANK + n][:, None], (C, C)))
    both("wout", w["L0_conv_W_out"].T)
    both("w11", w["L1_conv_w_1x1"][:, :, 0, 0].T)
    both("wpw", w["L3_conv_w_pw"].T)
    both("wa", w["L2_conv_wa"].T)
    pack[:, OFF["ba"]:OFF["ba"] + P] = np.tile(w["L2_conv_ba"], 2)[None]
    for k in range(4):
        e, par = divmod(k, 2)
        pack[par * C:(par + 1) * C, OFF["e12"] + k * CR:OFF["e12"] + (k + 1) * CR] = w["L2_conv_w%d" % (e + 1)].T
    for t in range(9):
        both(NPACK + t * P, w["L1_conv_w_lbp"][:, :, t // 3, t % 3].T)
    for par in range(2):
        r = slice(par * RANK, (par + 1) * RANK)
        pack[r, OFF["dtl"] + par * C:OFF["dtl"] + (par + 1) * C] = wxp[:RANK]
        pack[r, OFF["dtr"] + par * C:OFF["dtr"] + (par + 1) * C] = w["L0_conv_W_dt"].T
    pack[:, OFF["thy"]:OFF["thy"] + C] = w["L3_conv_theta_s"][None, :, 0]
    pack[:, OFF["thx"]:OFF["thx"] + C] = w["L3_conv_theta_s"][None, :, 1]
    for j in range(TAPS):
        column("cw%d" % j, w["L0_conv_conv_w"][:, 0, j])
    for name, key in (("cb", "L0_conv_conv_b"), ("bdt", "L0_conv_b_dt"), ("dpar", "L0_conv_D_param"),
                      ("lng", "L0_conv_ln_g"), ("lnb", "L0_conv_ln_b"), ("gamma", "L1_conv_gamma"),
                      ("beta", "L1_conv_beta"), ("b11", "L1_conv_b_1x1"), ("wdw", "L3_conv_w_dw")):
        column(name, w[key])
    for j in range(STATE):
        column("al%d" % j, w["L0_conv_A_log"][:, j])
    pack[:, OFF["b12"]] = np.concatenate([np.tile(w["L2_conv_b%d" % e], 2) for e in (1, 2)])
    pack[:, OFF["a12"]] = np.repeat([w["L2_conv_a1"], w["L2_conv_a2"]], C)
    pack[:, OFF["aa"]] = w["L2_conv_aa"]
    i = np.arange(P)
    pack[:, OFF["mean64"]:OFF["mean64"] + P] = (i[:, None] // C == i[None] // C) / C
    pack[:, OFF["pairs"]:OFF["pairs"] + P] = (i[:, None] // 2 == i[None] // 2) / 2
    pack[:, OFF["batch"]:OFF["batch"] + P] = (i[:, None] % C == i[None] % C) / IMAGES
    pack[:, OFF["ident"]:OFF["ident"] + P] = np.eye(P)
    pack[:, OFF["grid"]:OFF["grid"] + WW] = (i % HH)[:, None] - np.arange(WW)[None]
    pack[:, OFF["ones"]:OFF["ones"] + C] = 1
    return pack


def kernel(**inputs):
    import concourse.bacc as bacc
    from concourse.bass_utils import run_bass_kernel_spmd

    w = {k: np.asarray(v) for k, v in inputs.items()}
    arrays = {"x": np.ascontiguousarray(w["x"]), "pack": _packed(w)}
    nc = bacc.Bacc("TRN2", target_bir_lowering=False, num_devices=1)
    args = [nc.dram_tensor(n, a.shape, F32, kind="ExternalInput").ap() for n, a in arrays.items()]
    args.append(nc.dram_tensor("out", arrays["x"].shape, F32, kind="ExternalOutput").ap())
    build(nc, *args)
    return run_bass_kernel_spmd(nc, [arrays], core_ids=[0]).results[0]["out"]
```

```python
import numpy as np
import concourse.bass as bass
from concourse import mybir
from concourse.alu_op_type import AluOpType as ALU
from contextlib import ExitStack

F32 = mybir.dt.float32
F32R = mybir.dt.float32r
BF16 = mybir.dt.bfloat16
ACT = mybir.ActivationFunctionType
AX = mybir.AxisListType

P = 128
IMAGES, C, HH, WW = 16, 64, 32, 32
L = HH * WW
HALF = L // 2
PAIRS = IMAGES // 2
STATE = 2
RANK = 4
TAPS = 4
CR = C // 2
CHUNKS = L // P
PW = WW + 2
EPS = 1e-5

MATS = (["e12", "batch", "mean64", "wout", "winx", "winz"] + ["bc%d" % n for n in range(2 * STATE)]
        + ["w11", "wpw", "wa", "ba", "pairs", "ident"])
COLS = ["cw0", "cw1", "cw2", "cw3", "cb", "bdt", "al0", "al1", "dpar", "lng", "lnb", "gamma",
        "beta", "b11", "b12", "a12", "aa", "wdw"]
OFF, _at = {}, 0
for _n in MATS:
    OFF[_n] = _at
    _at += P
for _n, _w in (("dtl", P), ("dtr", P), ("thy", C), ("thx", C), ("grid", WW), ("ones", C)):
    OFF[_n] = _at
    _at += _w
for _n in COLS:
    OFF[_n] = _at
    _at += 1
NPACK = _at


class Chain:

    def __init__(self, eng, sem):
        self.eng, self.sem, self.base, self.k, self.fixed = eng, sem, 0, 0, 0

    def link(self, ins):
        self.k += 1
        ins.then_inc(self.sem, 1)
        self.eng.wait_ge(self.sem, self.base + self.k)

    def enter(self, i, per):
        self.fixed, self.per = self.fixed + self.k, per
        self.base, self.k = self.fixed + i * per, 0

    def leave(self, turns):
        assert self.k == self.per, (self.k, self.per)
        self.fixed += turns * self.per
        self.base, self.k = self.fixed, 0


def need(eng, sem, value):
    if not (isinstance(value, int) and value <= 0):
        eng.wait_ge(sem, value)


def before(p, h):
    return (p, 0) if h else (p - 1, 1)


def after(p, h):
    return (p + 1, 0) if h else (p, 1)


def build(nc, x, pack, out):
    with ExitStack() as ctx:
        def sb(name, shape, dt=F32):
            return ctx.enter_context(nc.sbuf_tensor(name, shape, dt))

        X = sb("X", [P, PAIRS, L])
        W = sb("W", [P, NPACK])
        RA = sb("RA", [P, PAIRS, L])
        RB = sb("RB", [P, 2 * PAIRS * L])
        R = sb("R", [P, 12 * L], F32R)
        WS = sb("WS", [P, 2, 9, P], F32R)
        WDT = sb("WDT", [P, P])
        SM = sb("SM", [P, 512])
        EX = sb("EX", [P, 2 * L])
        MB = sb("MB", [P, 2, CHUNKS, 2], BF16)
        IB = sb("IB", [P, P], BF16)
        PS = ctx.enter_context(nc.psum_tensor("PS", [P, 8, HALF], F32))

        def mat(name, w=P):
            return W[:, OFF[name]:OFF[name] + w]

        def col(name, n=P):
            return W[0:n, OFF[name]:OFF[name] + 1]

        def bank(n):
            return PS[:, n, :]

        def two(n):
            return PS[:, n:n + 2, :].rearrange("p a b -> p (a b)")

        def pair(t, p):
            if isinstance(p, int):
                return t[:, p, :]
            return t[:, bass.ds(p, 1), :].rearrange("p a n -> p (a n)")

        def half(t, p, h):
            if isinstance(p, int):
                return t[:, p, h * HALF:(h + 1) * HALF]
            return t[:, bass.ds(p, 1), h * HALF:(h + 1) * HALF].rearrange("p a n -> p (a n)")

        at = [0]

        def small(*shape):
            n = int(np.prod(shape))
            v = SM[:, at[0]:at[0] + n]
            at[0] += n
            assert at[0] <= 512
            names = "abc"[:len(shape)]
            if len(shape) > 1:
                v = v.rearrange("p (%s) -> p %s" % (" ".join(names), " ".join(names)),
                                **dict(zip(names[:-1], shape)))
            return v

        BST = small(PAIRS, 2, 6)
        MV = small(PAIRS, 2)
        GS = small(PAIRS, 2)
        SQ = small(PAIRS)
        VAR = small(PAIRS)
        MHALF = small(PAIRS)
        SC = small(PAIRS)
        SH = small(PAIRS)
        SB = small(PAIRS)
        TB = small(PAIRS)
        BM = small(2, PAIRS)
        BS = small(2)
        BT = small(8)
        ANEG = small(STATE)
        AEXP = small(STATE)
        OMA = small(1)
        AB = small(1)
        MEANO = small(1)
        MX = small(2, CHUNKS, 2)
        MXX = small(2, CHUNKS)
        EPSC = small(1)
        ONE = small(1)

        XS = RA
        ZS = RB[:, 0:PAIRS * L].rearrange("p (a n) -> p a n", a=PAIRS)
        TMP = RB[:, PAIRS * L:2 * PAIRS * L]
        G = [TMP[:, b * L:(b + 1) * L] for b in range(2)]
        AC = [TMP[:, (2 + b) * L:(3 + b) * L] for b in range(2)]

        def temp(n):
            k = [2 * n, 2 * n + 1]
            return [TMP[:, i * HALF:(i + 1) * HALF] if i < 16 else EX[:, (i - 16) * HALF:(i - 15) * HALF]
                    for i in k]

        tE = temp(0)
        tU = temp(1)
        tM = temp(2)
        tA = list(zip(temp(3), temp(4)))
        tB = list(zip(temp(5), temp(6)))
        tQ = temp(7)
        tR = temp(8)
        tY = temp(9)
        LBP = TMP[:, 4 * L:4 * L + 9 * P]

        def padded(n):
            return R[:, n * PW * PW:(n + 1) * PW * PW].rearrange("p (a c) -> p a c", a=PW)
        UH, UL = [padded(0), padded(1)], [padded(2), padded(3)]
        UF = [TMP[:, b * L:(b + 1) * L] for b in range(2)]
        GF = [TMP[:, (2 + b) * L:(3 + b) * L] for b in range(2)]
        YF = [TMP[:, (4 + b) * L:(5 + b) * L] for b in range(2)]

        def inner(u):
            return u[:, 1:HH + 1, 1:WW + 1]

        def stack(b, par, e):
            k = 2 * par + e
            k += 4 * ((b + 2) % 3)
            return R[:, k * L:(k + 1) * L]
        G3 = RA
        SLOTS = 4
        PT = [[RB[:, (2 * n + par) * L:(2 * n + par + 1) * L] for par in range(2)] for n in range(SLOTS)]
        SA = [[t[:, par * L:(par + 1) * L] for par in range(2)]
              for t in (RB[:, 8 * L:10 * L], RB[:, 10 * L:12 * L], EX)]
        V = [v.rearrange("p (c m) -> p c m", c=CHUNKS)
             for v in (RA[:, 4, :], RB[:, 12 * L:13 * L], RB[:, 13 * L:14 * L])]
        GB = [RB[:, 14 * L:15 * L], RA[:, 5, :], RA[:, 6, :]]
        RC = RB[:, 15 * L:16 * L]
        OT = [RA[:, 7, 0:HALF], RA[:, 7, HALF:L]]
        EQ, ER, EF, VT = [[RA[:, i, h * HALF:(h + 1) * HALF] for h in range(2)] for i in range(4)]
        ZEARLY = [R[:, i * L:(i + 1) * L] for i in (5, 6)]
        ZLATE = [WS[:, i, :, :].rearrange("p a b -> p (a b)")[:, 0:L] for i in range(2)]

        def parts_of(q):
            return ZEARLY if isinstance(q, int) and q < 2 else ZLATE

        PER = 27
        FILLS = {(6, 0): (4, 19), (6, 1): (9, 0), (7, 0): (9, 0), (7, 1): (10, 0)}
        STEPS = [(0, 0), (1, 0), (0, 1), (1, 1)] + [(j, par) for j in range(2, CHUNKS) for par in range(2)]
        LAST = [2, 3] + list(range(5, 2 * CHUNKS, 2))
        NMOVES = 12

        CG = 16
        D = RB[:, 0:PAIRS * L].rearrange("p (c g) -> p c g", c=C)
        AM = [[RB[:, PAIRS * L + (2 * n + a) * CG * P:PAIRS * L + (2 * n + a + 1) * CG * P]
               .rearrange("p (c m) -> p c m", c=CG) for a in range(2)] for n in range(2)]
        D1 = [EX[:, i * HALF:(i + 1) * HALF] for i in range(2)]
        HAT = [EX[:, i * HALF:(i + 1) * HALF].rearrange("p (c y) -> p c y", c=CG) for i in range(4)]
        HATV = W[:, OFF["e12"]:OFF["e12"] + HALF].rearrange("p (c y) -> p c y", c=CG)
        E = RA.rearrange("p b n -> p (b n)").rearrange("p (x g c) -> p x g c", g=4, c=C)
        S3 = RB[:, 0:PAIRS * L].rearrange("p (b n) -> p b n", b=PAIRS)

        IN_A, IN_B, GN1, BN1, GN2A, GN2B, GN3A, GN3B = range(8)
        HALFWAY = PAIRS // 2

        names = """packed lbp_in zero_done exp_a wdt_mm setup_done dve_step act_step pool_step
            stat_ready group_mm var_ready pow_done coef_ready
            g_ready xb_done xz_mm tap_done taps_done silux_done siluz_done
            dt_mm b_mm c_mm o_mm v_mm e_done dta_read u_done dt_read nd_done ln_done dt_done dtx_done
            b_read da_done scan_done c_read hc_done y_done sq_done r_done o_read blk0_done
            u_ready g1_ready uh_done ul_done conv_mm y1_done w1_mm x1_done
            minus_done gb_ready z_mm z_read zf_done hi_done lo_done stack_in asm_mm asm_read v_part v_done
            s_mm s_read m_ready
            mrow_mm m_copied t_mm p_ready pv_done first_added add_done add_dve sum_mm sum_read rec_done acc_read x2_done
            g3_done dist_done am_zero am_dve am_act tr_mm tr_act tr_dve s1_mm s1_copied s2_mm s2_copied
            bk_mm bk_act bk_dve pw_mm res_done stored""".split()
        s = {n: ctx.enter_context(nc.semaphore(n)) for n in names}
        x_in = [ctx.enter_context(nc.semaphore("x_in%d" % p)) for p in range(PAIRS)]

        block = ctx.enter_context(nc.Block())
        xd = x.rearrange("(p two) c h w -> (two c) p (h w)", two=2)
        od = out.rearrange("(p two) c h w -> (two c) p (h w)", two=2)

        def transposed_out(copy, n):
            q, xb = divmod(n, 8)
            src = bank(n % 4).rearrange("p (x a c) -> p x a c", x=4, a=2)
            dst = D.rearrange("p c (q a x) -> p q x a c", q=2, a=2)[:, q, 4 * xb:4 * xb + 4]
            for a in range(2):
                last = copy(dst[:, :, a], src[:, :, a])
            return last

        def back_out(copy, n):
            q, xb = divmod(n, 8)
            src = bank(n % 4).rearrange("p (x b y) -> p x b y", x=4, b=4)
            dst = S3[:, 4 * q:4 * q + 4, :].rearrange("p b (y x) -> p x b y", x=WW)[:, 4 * xb:4 * xb + 4]
            return copy(dst, src)

        @block.sync
        def _(sp):
            for p in range(PAIRS):
                sp.dma_start(X[:, p, :], xd[:, p, :]).then_inc(x_in[p], 16)
                if p == 1:
                    sp.dma_start(W[:, :], pack[:, 0:NPACK]).then_inc(s["packed"], 16)
            sp.dma_start(LBP, pack[:, NPACK:NPACK + 9 * P]).then_inc(s["lbp_in"], 16)

            def stacked(q, b):
                need(sp, s["t_mm"], 32 * q - 64)
                if isinstance(q, int) and q == 1:
                    sp.wait_ge(s["conv_mm"], 2 * PAIRS)
                if isinstance(q, int) and q == 2:
                    sp.wait_ge(s["stack_in"], 32 * NMOVES)
                sp.wait_ge(s["hi_done"], 2 * q + 2)
                zh, zl = parts_of(q)
                for src, places in ((zh, ((0, 32), (0, 64))), (zl, ((64,), (32,)))):
                    if src is zl:
                        sp.wait_ge(s["lo_done"], 2 * q + 2)
                    for par in range(2):
                        for e in range(2):
                            for r in places[e]:
                                k = 2 * e + par
                                sp.dma_start(stack(b, par, e)[r:r + CR, :].bitcast(F32),
                                             src[k * CR:(k + 1) * CR, :].bitcast(F32))\
                                    .then_inc(s["stack_in"], 16)

            for q in range(3):
                stacked(q, q)
            with sp.Fori(1, 3) as k:
                for c in range(3):
                    stacked(3 * k + c, c)
            sp.wait_ge(s["stack_in"], 16 * NMOVES * (PAIRS + 1))

            for p in range(PAIRS - 1):
                sp.wait_ge(s["res_done"], 2 * p + 2)
                sp.dma_start(od[:, p, :], X[:, p, :]).then_inc(s["stored"], 16)
            for h in range(2):
                sp.wait_ge(s["res_done"], 2 * PAIRS - 1 + h)
                sp.dma_start(half(od, PAIRS - 1, h), half(X, PAIRS - 1, h)).then_inc(s["stored"], 16)
            sp.wait_ge(s["stored"], 16 * (PAIRS + 1))

        @block.vector
        def _(v):
            ch = Chain(v, s["dve_step"])
            link = ch.link

            def coefs_stat(lo=0, hi=PAIRS):
                for p in range(lo, hi):
                    i = v.bn_aggr(MV[:, p, :], BST[:, p, :, :].rearrange("p h k -> p (h k)"))
                link(i)
                mean, var = MV[:, lo:hi, 0], MV[:, lo:hi, 1]
                link(v.tensor_tensor(SQ[:, lo:hi], mean, mean, ALU.mult))
                v.tensor_tensor(var, var, SQ[:, lo:hi], ALU.add).then_inc(s["stat_ready"], 1)

            def coefs_var(nth, lo=0, hi=PAIRS):
                v.wait_ge(s["group_mm"], nth + 1)
                link(v.tensor_copy(GS[:, lo:hi].rearrange("p a b -> p (a b)"), PS[:, 7, 0:2 * (hi - lo)]))
                link(v.tensor_tensor(SQ[:, lo:hi], GS[:, lo:hi, 0], GS[:, lo:hi, 0], ALU.mult))
                link(v.tensor_tensor(VAR[:, lo:hi], GS[:, lo:hi, 1], SQ[:, lo:hi], ALU.subtract))
                v.tensor_scalar(VAR[:, lo:hi], VAR[:, lo:hi], EPS, None, ALU.add).then_inc(s["var_ready"], 1)

            def coefs_shift(nth, lo=0, hi=PAIRS):
                v.wait_ge(s["pow_done"], nth + 1)
                v.scalar_tensor_tensor(SH[:, lo:hi], GS[:, lo:hi, 0], -1.0, SC[:, lo:hi], ALU.mult, ALU.mult)\
                    .then_inc(s["coef_ready"], 1)
                v.wait_ge(s["coef_ready"], nth + 1)

            def coefs(nth, lo=0, hi=PAIRS):
                coefs_stat(lo, hi)
                coefs_var(nth, lo, hi)
                coefs_shift(nth, lo, hi)

            def stats(p, h):
                if isinstance(p, int):
                    return v.bn_stats(BST[:, p, h, :], half(X, p, h))
                return v.bn_stats(BST[:, bass.ds(p, 1), h, :].rearrange("p a k -> p (a k)"), half(X, p, h))

            def input_stats(p):
                v.wait_ge(x_in[p], 16)
                for h in range(2):
                    i = stats(p, h)
                return i

            link(v.memset(MHALF, -0.5))
            link(v.memset(EPSC, EPS))
            link(v.memset(ONE, 1.0))
            input_stats(0)
            input_stats(1)
            v.wait_ge(s["packed"], 16)
            link(v.tensor_copy(IB[:, :], mat("ident")))
            for par in range(2):
                q = slice(par * C, (par + 1) * C)
                o = slice(OFF["wout"] + par * C, OFF["wout"] + (par + 1) * C)
                link(v.tensor_reduce(MEANO[q], W[q, o], AX.X, ALU.add))
                link(v.tensor_scalar(MEANO[q], MEANO[q], 1.0 / C, None, ALU.mult))
                link(v.tensor_scalar(W[q, o], W[q, o], MEANO[q], None, ALU.subtract))
            link(v.tensor_scalar(OMA, col("a12"), -1.0, 1.0, ALU.mult, ALU.add))
            link(v.tensor_tensor(AB, col("a12"), col("b12"), ALU.mult))
            link(v.tensor_scalar(mat("wpw"), mat("wpw"), col("wdw"), None, ALU.mult))
            v.wait_ge(s["wdt_mm"], 1)
            link(v.tensor_copy(WDT[:, :], PS[:, 6, 0:P]))
            v.wait_ge(s["exp_a"], 1)
            v.tensor_scalar(ANEG, AEXP, -1.0, None, ALU.mult).then_inc(s["setup_done"], 1)
            v.wait_ge(s["setup_done"], 1)

            for p in range(2, HALFWAY):
                i = input_stats(p)
            link(i)
            coefs(IN_A, 0, HALFWAY)

            for par in range(2):
                i = v.memset(stack(0, par, 1)[96:98, :].bitcast(F32), -1.0)
            i.then_inc(s["minus_done"], 1)

            def taps(p, b):
                v.wait_ge(s["tap_done"], p + 1)
                xp = two(2 * b)
                for j in (1, 2, 3):
                    i = v.scalar_tensor_tensor(AC[b][:, j:L], xp[:, 0:L - j], col("cw%d" % (3 - j)),
                                               AC[b][:, j:L], ALU.mult, ALU.add)
                    if j < 3:
                        link(i)
                i.then_inc(s["taps_done"], 1)

            taps(0, 0)
            input_stats(4)
            input_stats(5)
            taps(1, 1)
            input_stats(6)
            link(input_stats(7))
            coefs(IN_B, HALFWAY, PAIRS)
            with v.Fori(1, PAIRS // 2) as k:
                ch.enter(k - 1, 4)
                taps(2 * k, 0)
                taps(2 * k + 1, 1)
                ch.leave(PAIRS // 2 - 1)
            v.wait_ge(s["lbp_in"], 16)
            link(v.tensor_copy(WS[:, 0, :, :].rearrange("p a b -> p (a b)"), LBP))
            link(v.tensor_tensor(WS[:, 1, :, :].rearrange("p a b -> p (a b)"), LBP,
                                 WS[:, 0, :, :].rearrange("p a b -> p (a b)"), ALU.subtract))

            def soft(p, h):
                n = 2 * p + h
                v.wait_ge(s["u_done"], n + 1)
                v.scalar_tensor_tensor(tE[h], tU[h], -1.0, tE[h], ALU.add, ALU.subtract)\
                    .then_inc(s["nd_done"], 1)

            def inputs(p, h):
                n = 2 * p + h
                v.wait_ge(s["dtx_done"], n + 1)
                v.wait_ge(s["b_mm"], n + 1)
                for j in range(STATE):
                    i = v.tensor_tensor(tB[h][j], bank(1 + j), tU[h], ALU.mult)
                i.then_inc(s["b_read"], 1)

            def scan(p, h):
                n = 2 * p + h
                v.wait_ge(s["b_read"], n + 1)
                v.wait_ge(s["da_done"], n + 1)
                for j in range(STATE):
                    first = 0.0 if h == 0 else tB[0][j][:, HALF - 1:HALF]
                    i = v.tensor_tensor_scan(tB[h][j], tA[h][j], tB[h][j], first, ALU.mult, ALU.add)
                i.then_inc(s["scan_done"], 1)

            def outputs(p, h):
                n = 2 * p + h
                v.wait_ge(s["scan_done"], n + 1)
                v.wait_ge(s["c_mm"], n + 1)
                for j in range(STATE):
                    i = v.tensor_tensor(tA[h][j], bank(3 + j), tB[h][j], ALU.mult)
                i.then_inc(s["c_read"], 1)

            def skip(p, h):
                n = 2 * p + h
                v.wait_ge(s["c_read"], n + 1)
                v.scalar_tensor_tensor(tA[h][0], half(XS, p, h), col("dpar"), tA[h][0], ALU.mult, ALU.add)\
                    .then_inc(s["hc_done"], 1)

            def norm(p, h):
                n = 2 * p + h
                v.wait_ge(s["r_done"], n + 1)
                v.tensor_tensor(tR[h], bank(5), tR[h], ALU.mult).then_inc(s["o_read"], 1)

            def residual0(p, h):
                n = 2 * p + h
                v.wait_ge(s["o_read"], n + 1)
                v.scalar_tensor_tensor(half(X, p, h), tR[h], col("lng"), half(X, p, h), ALU.mult, ALU.add)\
                    .then_inc(s["blk0_done"], 1)

            def stats0(p, h):
                v.wait_ge(s["blk0_done"], 2 * p + h + 1)
                return stats(p, h)

            def turn(p, h, lead=True, lag=True):
                inputs(p, h)
                scan(p, h)
                outputs(p, h)
                skip(p, h)
                if lead:
                    soft(p + 1, h)
                if lag:
                    norm(*before(p, h))
                    residual0(*before(p, h))
                    stats0(*before(p, h))

            v.wait_ge(s["xb_done"], PAIRS)
            soft(0, 0)
            soft(0, 1)
            turn(0, 0, lag=False)
            turn(0, 1)
            with v.Fori(1, PAIRS - 1) as p:
                turn(p, 0)
                turn(p, 1)
            turn(PAIRS - 1, 0, lead=False)
            turn(PAIRS - 1, 1, lead=False)
            norm(PAIRS - 1, 1)
            residual0(PAIRS - 1, 1)
            link(stats0(PAIRS - 1, 1))

            coefs(GN1)
            mean, msq, b0, b1 = MV[:, :, 0], MV[:, :, 1], BM[:, 0, :], BM[:, 1, :]
            link(v.tensor_tensor(b0, mean, SC, ALU.mult))
            link(v.tensor_tensor(SQ, b0, SH, ALU.mult))
            link(v.tensor_tensor(b0, b0, SH, ALU.add))
            link(v.tensor_tensor(b1, msq, SC, ALU.mult))
            link(v.tensor_tensor(b1, b1, SC, ALU.mult))
            link(v.scalar_tensor_tensor(b1, SQ, 2.0, b1, ALU.mult, ALU.add))
            link(v.tensor_tensor(SQ, SH, SH, ALU.mult))
            link(v.tensor_tensor(b1, b1, SQ, ALU.add))
            v.tensor_reduce(BS, BM, AX.X, ALU.add).then_inc(s["stat_ready"], 1)
            v.wait_ge(s["group_mm"], BN1 + 1)
            link(v.tensor_copy(BT[:, 0:2], PS[:, 7, 0:2]))
            link(v.tensor_tensor(BT[:, 2:3], BT[:, 0:1], BT[:, 0:1], ALU.mult))
            link(v.tensor_tensor(BT[:, 3:4], BT[:, 1:2], BT[:, 2:3], ALU.subtract))
            v.tensor_scalar(BT[:, 3:4], BT[:, 3:4], EPS, None, ALU.add).then_inc(s["var_ready"], 1)
            v.wait_ge(s["pow_done"], BN1 + 1)
            link(v.tensor_tensor(BT[:, 5:6], BT[:, 4:5], col("gamma"), ALU.mult))
            link(v.tensor_tensor(BT[:, 6:7], BT[:, 5:6], BT[:, 0:1], ALU.mult))
            link(v.tensor_tensor(BT[:, 6:7], col("beta"), BT[:, 6:7], ALU.subtract))
            link(v.tensor_scalar(SB, SC, BT[:, 5:6], None, ALU.mult))
            v.tensor_scalar(TB, SH, BT[:, 5:6], BT[:, 6:7], ALU.mult, ALU.add).then_inc(s["coef_ready"], 1)
            v.wait_ge(s["coef_ready"], BN1 + 1)

            def low(p, b):
                if isinstance(p, int) and p == 0:
                    v.wait_ge(s["u_ready"], 1)
                v.wait_ge(s["uh_done"], p + 1)
                need(v, s["conv_mm"], 2 * p - 2)
                v.tensor_tensor(inner(UL[b]), UF[b].rearrange("p (y x) -> p y x", y=HH), inner(UH[b]),
                                ALU.subtract).then_inc(s["ul_done"], 1)

            def relu(p, b, h):
                v.wait_ge(s["g1_ready"], p + 1)
                q = slice(h * HALF, (h + 1) * HALF)
                v.wait_ge(s["conv_mm"], 2 * p + h + 1)
                v.scalar_tensor_tensor(YF[b][:, q], bank(h), 0.0, GF[b][:, q], ALU.max, ALU.add)\
                    .then_inc(s["y1_done"], 1)

            def add1(p, b):
                for h in range(2):
                    v.wait_ge(s["w1_mm"], 2 * p + h + 1)
                    v.scalar_tensor_tensor(half(X, p, h), bank(4 + h), col("b11"), half(X, p, h),
                                           ALU.add, ALU.add).then_inc(s["x1_done"], 1)
                v.wait_ge(s["x1_done"], 2 * p + 2)
                for h in range(2):
                    i = stats(p, h)
                return i

            def turn1(p, b, lead=True, lag=True):
                if lead:
                    low(p + 1, 1 - b)
                relu(p, b, 0)
                relu(p, b, 1)
                if lag:
                    return add1(p - 1, 1 - b)

            def operands(q, h):
                v.wait_ge(s["z_read"], 2 * q + h + 1)
                need(v, s["hi_done"], 2 * q + h - 1)
                need(v, s["lo_done"], 2 * q + h - 1)
                v.scalar_tensor_tensor(EF[h], ER[h], OMA, EQ[h], ALU.mult, ALU.add).then_inc(s["zf_done"], 1)

            def biased(q, c):
                v.wait_ge(s["asm_mm"], 2 * q + c + 1)
                ba = mat("ba").unsqueeze(1).to_broadcast([P, CHUNKS // 2, P])
                v.tensor_tensor(VT[c].rearrange("p (c m) -> p c m", c=CHUNKS // 2),
                                bank(6 + c).rearrange("p (c m) -> p c m", c=CHUNKS // 2),
                                ba, ALU.add).then_inc(s["asm_read"], 1)

            def v_chunks(b, c):
                return V[b][:, c * 4:c * 4 + 4, :].rearrange("p c m -> p (c m)")

            def negative(q, b, c):
                v.wait_ge(s["asm_read"], 2 * q + c + 1)
                v.tensor_scalar(v_chunks(b, c), VT[c], 0.0, col("aa"), ALU.min, ALU.mult).then_inc(s["v_part"], 1)

            def positive(q, b, c):
                v.wait_ge(s["v_part"], 2 * q + c + 1)
                v.scalar_tensor_tensor(v_chunks(b, c), VT[c], 0.0, v_chunks(b, c), ALU.max, ALU.add)\
                    .then_inc(s["v_done"], 1)
                v.wait_ge(s["v_done"], 2 * q + c + 1)

            def maximum(q, n, h):
                par, tile = divmod(n, CHUNKS)
                v.wait_ge(s["s_mm"], 32 * q + 2 * n + h + 1)
                v.tensor_reduce(MX[:, par, tile, h:h + 1], bank(2 + h), AX.X, ALU.max)\
                    .then_inc(s["s_read"], 1)

            def both_parts(q, par):
                v.wait_ge(s["s_read"], 32 * q + 16 * par + 16)
                need(v, s["mrow_mm"], 4 * q - 2 + 2 * par)
                link(v.tensor_reduce(MXX[:, par], MX[:, par], AX.X, ALU.max))
                link(v.tensor_copy(MB[:, par, :, 0], MXX[:, par]))
                v.tensor_tensor(MB[:, par, :, 1], MXX[:, par], MB[:, par, :, 0], ALU.subtract)\
                    .then_inc(s["m_ready"], 1)

            def scaled(p, h):
                v.wait_ge(s["acc_read"], 2 * p + h + 1)
                v.wait_ge(s["rec_done"], 2 * p + h + 1)
                link(v.tensor_tensor(OT[h], OT[h], RC[:, h * HALF:(h + 1) * HALF], ALU.mult))

            def residual(p, h):
                v.tensor_tensor(half(X, p, h), OT[h], half(X, p, h), ALU.add).then_inc(s["x2_done"], 1)

            def end_stats(p, h):
                v.wait_ge(s["x2_done"], 2 * p + h + 1)
                return stats(p, h)

            def add_first(p, b, par):
                v.wait_ge(s["p_ready"], 32 * p + 8)
                v.tensor_tensor(SA[b][par], PT[0][par], PT[1][par], ALU.add).then_inc(s["first_added"], 1)

            def attend(p, b, lead=True, lag=True, extra={}):
                for n in range(2 * CHUNKS):
                    if n in extra:
                        extra[n]()
                    if lead:
                        for h in range(2):
                            maximum(p + 1, n, h)
                        if n in (2, 3):
                            operands(p + 2, n - 2)
                        if n in (8, 9):
                            biased(p + 1, n - 8)
                        if n == 10:
                            for c in range(2):
                                negative(p + 1, (b + 1) % 3, c)
                        if n in (11, 13):
                            positive(p + 1, (b + 1) % 3, n // 13)
                        if n == 12:
                            both_parts(p + 1, 0)
                    if n in (4, 5):
                        add_first(p, b, n - 4)
                    if lag:
                        if n in (6, 7):
                            scaled(p - 1, n - 6)
                            residual(p - 1, n - 6)
                        if n in (14, 15):
                            end_stats(p - 1, n - 14)
                if lead:
                    both_parts(p + 1, 1)

            low(0, 0)
            turn1(0, 0, lag=False)
            with v.Fori(0, 2) as k:
                turn1(2 * k + 1, 1)
                turn1(2 * k + 2, 0)
            coefs(GN2A, 0, 3)
            low(6, 0)
            relu(5, 1, 0)
            for h in range(2):
                operands(0, h)
            relu(5, 1, 1)
            add1(4, 0)
            low(7, 1)
            for c in range(2):
                biased(0, c)
                negative(0, 0, c)
                positive(0, 0, c)
            for h in range(2):
                operands(1, h)
            at = 0
            for (p, h), (count, _) in FILLS.items():
                for n in range(at, at + count):
                    maximum(0, *divmod(n, 2))
                    if n == 17:
                        both_parts(0, 0)
                at += count
                if h == 1 and p == 7:
                    both_parts(0, 1)
                relu(p, p % 2, h)
                if h == 1 and p == 6:
                    add1(5, 1)
            add1(6, 0)
            link(add1(7, 1))
            attend(0, 0, lag=False, extra={9: lambda: coefs_stat(3, PAIRS), 11: lambda: coefs_var(GN2B, 3, PAIRS),
                                           14: lambda: coefs_shift(GN2B, 3, PAIRS)})
            with v.Fori(0, 2) as k:
                ch.enter(k, 3 * 6)
                for c in range(3):
                    attend(3 * k + c + 1, (c + 1) % 3)
                ch.leave(2)

            grid = mat("grid", WW).unsqueeze(1).to_broadcast([P, CG, WW])

            def hat(g, a):
                w = HAT[2 * min(g, 1) + a]
                tv = mat(("thy", "thx")[a], C)[:, g * CG:(g + 1) * CG].unsqueeze(2).to_broadcast([P, CG, WW])
                link(v.tensor_tensor(HATV, grid, tv, ALU.add))
                link(v.tensor_scalar(w, HATV, -1.0, 1.0, ALU.mult, ALU.add))
                link(v.scalar_tensor_tensor(w, HATV, 1.0, w, ALU.add, ALU.min))

            def place(g, a):
                if g >= 2:
                    v.wait_ge(s["s2_mm"], (g - 1) * CG // 4)
                for q in range(4):
                    r = slice(32 * q, 32 * q + 32)
                    i = v.tensor_scalar(AM[g % 2][a][r, :, 32 * q:32 * q + 32], HAT[2 * min(g, 1) + a][r], 0.0, None,
                                        ALU.max)
                i.then_inc(s["am_dve"], 1)
                v.wait_ge(s["am_dve"], 1 + a if g == 0 else 2 + g + a - (g > 1))

            def normed3(p):
                v.tensor_scalar(G3[:, p, :], X[:, p, :], SC[:, p:p + 1], SH[:, p:p + 1], ALU.mult, ALU.add)\
                    .then_inc(s["g3_done"], 1)

            def add(j):
                v.wait_ge(s["p_ready"], 32 * (PAIRS - 1) + 2 * LAST[j] + 2)
                v.tensor_tensor(SA[1][0], SA[1][0], PT[j % SLOTS][0], ALU.add).then_inc(s["add_dve"], 1)
                v.wait_ge(s["add_dve"], j - 1)

            q = PAIRS - 2
            coefs_stat(0, q)
            coefs_var(GN3A, 0, q)
            for par in range(2):
                add_first(PAIRS - 1, 1, par)
            v.wait_ge(s["first_added"], 2 * PAIRS)
            for h in range(2):
                scaled(q, h)
                residual(q, h)
            add(2)
            hat(0, 0)
            end_stats(q, 0)
            end_stats(q, 1)
            coefs_shift(GN3A, 0, q)
            add(3)
            for p in range(q):
                if p == 3:
                    add(4)
                normed3(p)
            for j in (5, 6, 7):
                add(j)
            hat(0, 1)
            hat(1, 0)
            q = PAIRS - 1
            for h in range(2):
                scaled(q, h)
                residual(q, h)
                i = end_stats(q, h)
            link(i)
            coefs_stat(q - 1, PAIRS)
            coefs_var(GN3B, q - 1, PAIRS)
            coefs_shift(GN3B, q - 1, PAIRS)
            normed3(q - 1)
            v.wait_ge(s["am_zero"], 1)
            place(0, 0)
            place(0, 1)

            for n in range(9, 16, 2):
                v.wait_ge(s["tr_mm"], n + 1)
                transposed_out(v.tensor_copy, n).then_inc(s["tr_dve"], 1)
            for n in range(16):
                v.wait_ge(s["s1_mm"], n + 1)
                need(v, s["s2_mm"], n - 1)
                v.tensor_copy(D1[n % 2], bank(n % 2)).then_inc(s["s1_copied"], 1)
                if n == 0:
                    hat(1, 1)
                    v.wait_ge(s["am_zero"], 2)
                    place(1, 0)
                    place(1, 1)
                if n in (2, 6):
                    hat(2 + n // 6, 1)
                if n in (4, 8):
                    place(1 + n // 4, 1)
            for n in range(1, 16, 2):
                v.wait_ge(s["bk_mm"], n + 1)
                back_out(v.tensor_copy, n).then_inc(s["bk_dve"], 1)
            with v.Fori(0, PAIRS // 2) as k:
                for j in range(4):
                    v.wait_ge(s["pw_mm"], 4 * k + j + 1)
                    v.tensor_tensor(half(X, 2 * k + j // 2, j % 2), bank(4 + j),
                                    half(X, 2 * k + j // 2, j % 2), ALU.add).then_inc(s["res_done"], 1)

        @block.scalar
        def _(a):
            act = a.activation
            ch = Chain(a, s["act_step"])
            link = ch.link
            a.wait_ge(s["packed"], 16)
            act(AEXP, W[:, OFF["al0"]:OFF["al0"] + STATE], ACT.Exp).then_inc(s["exp_a"], 1)
            a.preload_act_table_set("silu_and_others")

            def first(p, b):
                a.wait_ge(s["xz_mm"], 2 * p + 1)
                need(a, s["silux_done"], p - 1)
                act(AC[b], two(2 * b), ACT.Identity, bias=col("cb"), scale=col("cw3")).then_inc(s["tap_done"], 1)
                a.wait_ge(s["xz_mm"], 2 * p + 2)
                act(pair(ZS, p), two(4), ACT.Silu).then_inc(s["siluz_done"], 1)
                act(pair(X, p), pair(X, p), ACT.Identity, bias=col("lnb")).then_inc(s["xb_done"], 1)

            def second(p, b):
                a.wait_ge(s["taps_done"], p + 1)
                act(pair(XS, p), AC[b], ACT.Silu).then_inc(s["silux_done"], 1)

            def soft_parts(p, h):
                n = 2 * p + h
                a.wait_ge(s["dt_mm"], n + 1)
                need(a, s["dt_done"], n - 1)
                act(tE[h], bank(7), ACT.Abs, bias=col("bdt")).then_inc(s["dta_read"], 1)
                need(a, s["da_done"], n - 1)
                need(a, s["dtx_done"], n - 1)
                act(tM[h], bank(7), ACT.Relu, bias=col("bdt")).then_inc(s["dt_read"], 1)

            def soft(p, h):
                n = 2 * p + h
                a.wait_ge(s["dta_read"], n + 1)
                act(tE[h], tE[h], ACT.Exp, scale=-1.0).then_inc(s["e_done"], 1)
                a.wait_ge(s["e_done"], n + 1)
                need(a, s["b_read"], n - 1)
                act(tU[h], tE[h], ACT.Identity, bias=ONE).then_inc(s["u_done"], 1)

            first(0, 0)
            first(1, 1)
            second(0, 0)
            with a.Fori(1, PAIRS // 2) as k:
                first(2 * k, 0)
                second(2 * k - 1, 1)
                first(2 * k + 1, 1)
                second(2 * k, 0)
            a.wait_ge(s["silux_done"], PAIRS - 1)
            soft_parts(0, 0)
            second(PAIRS - 1, 1)

            a.preload_act_table_set("natural_log_exp_and_others")
            a.wait_ge(s["setup_done"], 1)

            def soft_log(p, h):
                n = 2 * p + h
                a.wait_ge(s["nd_done"], n + 1)
                act(tU[h], tU[h], ACT.Ln).then_inc(s["ln_done"], 1)

            def grow(p, h):
                n = 2 * p + h
                a.wait_ge(s["dt_done"], n + 1)
                need(a, s["y_done"], n - 1)
                for j in range(STATE):
                    i = act(tA[h][j], tM[h], ACT.Exp, scale=ANEG[:, j:j + 1])
                i.then_inc(s["da_done"], 1)

            def square(p, h):
                n = 2 * p + h
                a.wait_ge(s["o_mm"], n + 1)
                need(a, s["v_mm"], n - 1)
                act(tQ[h], bank(5), ACT.Square).then_inc(s["sq_done"], 1)

            def inverse_sd(p, h):
                n = 2 * p + h
                a.wait_ge(s["v_mm"], n + 1)
                need(a, s["blk0_done"], n - 1)
                link(act(tR[h], bank(6), ACT.Ln, bias=EPSC))
                act(tR[h], tR[h], ACT.Exp, scale=-0.5).then_inc(s["r_done"], 1)

            def turn(p, h, lead=True, lag=True):
                if lag:
                    square(*before(p, h))
                if lead:
                    soft_parts(p + 1, h)
                    soft(p + 1, h)
                if lag:
                    inverse_sd(*before(p, h))
                if lead or h == 0:
                    grow(*after(p, h))
                if lead:
                    soft_log(p + 1, h)

            soft(0, 0)
            soft_log(0, 0)
            soft_parts(0, 1)
            soft(0, 1)
            soft_log(0, 1)
            grow(0, 0)
            turn(0, 0, lag=False)
            turn(0, 1)
            turn(1, 0)
            turn(1, 1)
            with a.Fori(2, PAIRS - 1) as p:
                ch.enter(p - 2, 2)
                turn(p, 0)
                turn(p, 1)
                ch.leave(PAIRS - 3)
            turn(PAIRS - 1, 0, lead=False)
            turn(PAIRS - 1, 1, lead=False)
            square(PAIRS - 1, 1)
            inverse_sd(PAIRS - 1, 1)

            def high(p, b):
                a.wait_ge(s["u_ready"], p + 1)
                need(a, s["conv_mm"], 2 * p - 2)
                act(inner(UH[b]), UF[b].rearrange("p (y x) -> p y x", y=HH), ACT.Copy)\
                    .then_inc(s["uh_done"], 1)

            a.wait_ge(s["zero_done"], 1)
            a.wait_ge(s["coef_ready"], BN1 + 1)
            act(inner(UH[0]), X[:, 0, :].rearrange("p (y x) -> p y x", y=HH), ACT.Identity,
                scale=SB[:, 0:1], bias=TB[:, 0:1]).then_inc(s["uh_done"], 1)
            high(1, 1)
            with a.Fori(1, 3) as k:
                high(2 * k, 0)
                high(2 * k + 1, 1)

            def parts(q, h):
                a.wait_ge(s["z_mm"], 2 * q + h + 1)
                need(a, s["zf_done"], 2 * q + h - 1)
                act(EQ[h], bank(6 + h), ACT.Identity, bias=AB, scale=col("a12"))
                act(ER[h], bank(6 + h), ACT.Relu, bias=col("b12")).then_inc(s["z_read"], 1)

            def high_z(q, h):
                if h == 0:
                    need(a, s["stack_in"], 16 * NMOVES * q)
                a.wait_ge(s["zf_done"], 2 * q + h + 1)
                act(parts_of(q)[0][:, h * HALF:(h + 1) * HALF], EF[h], ACT.Copy).then_inc(s["hi_done"], 1)

            def probs(p, n):
                j, par = STEPS[n]
                slot = PT[j % SLOTS][par]
                if par == 0:
                    need(a, s["pv_done"], 2 * (CHUNKS * p + j - SLOTS + 1))
                    if j in (SLOTS, SLOTS + 1):
                        a.wait_ge(s["first_added"], 2 * p + 2)
                    else:
                        need(a, s["add_done"], 6 * p + j - (3 if j < SLOTS else 5))
                    if isinstance(p, int) and p == PAIRS - 1 and j >= SLOTS + 2:
                        a.wait_ge(s["add_dve"], j - SLOTS - 1)
                for h in range(2):
                    a.wait_ge(s["t_mm"], 32 * p + 2 * n + h + 1)
                    act(slot[:, h * HALF:(h + 1) * HALF], bank(4 + h), ACT.Exp).then_inc(s["p_ready"], 1)

            def max_rows(q, b, par):
                for h in range(2):
                    a.wait_ge(s["mrow_mm"], 4 * q + 2 * par + h + 1)
                    act(stack(b, par, 0)[96:98, h * HALF:(h + 1) * HALF], PS[96:98, 6 + h, :],
                        ACT.Copy).then_inc(s["m_copied"], 1)

            def product_out(p, h):
                a.wait_ge(s["pv_done"], 2 * CHUNKS * p + 2 * CHUNKS - 1 + h)
                if isinstance(p, int) and p == PAIRS - 1:
                    a.wait_ge(s["x2_done"], 2 * p + h - 1)
                act(OT[h], bank(h), ACT.Copy).then_inc(s["acc_read"], 1)

            def inverse(p, h):
                n = 2 * p + h
                q = slice(h * HALF, (h + 1) * HALF)
                a.wait_ge(s["sum_mm"], n + 1)
                act(RC[:, q], bank(6 + h), ACT.Ln).then_inc(s["sum_read"], 1)
                a.wait_ge(s["sum_read"], n + 1)
                act(RC[:, q], RC[:, q], ACT.Exp, scale=-1.0).then_inc(s["rec_done"], 1)

            def attend(p, b, lead=True, lag=True):
                for n in range(2 * CHUNKS):
                    probs(p, n)
                    if n == 0:
                        max_rows(p, b, 1)
                    if n in (1, 2) and lead:
                        parts(p + 2, n - 1)
                    if n in (2, 3) and lag:
                        product_out(p - 1, n - 2)
                    if n in (3, 4) and lead:
                        high_z(p + 2, n - 3)
                    if n in (4, 5) and lag:
                        inverse(p - 1, n - 4)
                    if n == 14 and lead:
                        max_rows(p + 1, (b + 1) % 3, 0)

            for q in range(2):
                high(6 + q, q)
                for h in range(2):
                    parts(q, h)
                for h in range(2):
                    high_z(q, h)
            max_rows(0, 0, 0)
            attend(0, 0, lag=False)
            with a.Fori(0, 2) as k:
                for c in range(3):
                    attend(3 * k + c + 1, (c + 1) % 3)
            attend(PAIRS - 1, 1, lead=False)
            for h in range(2):
                product_out(PAIRS - 1, h)
            for h in range(2):
                inverse(PAIRS - 1, h)

            def copy(o, i):
                return act(o, i, ACT.Copy)
            a.wait_ge(s["add_done"], 6 * PAIRS)
            a.wait_ge(s["add_dve"], 6)
            for n in list(range(8)) + list(range(8, 16, 2)):
                if n == 6:
                    a.wait_ge(s["coef_ready"], GN3B + 1)
                    act(G3[:, PAIRS - 1, :], X[:, PAIRS - 1, :], ACT.Identity, scale=SC[:, PAIRS - 1:PAIRS],
                        bias=SH[:, PAIRS - 1:PAIRS]).then_inc(s["g3_done"], 1)
                a.wait_ge(s["tr_mm"], n + 1)
                transposed_out(copy, n).then_inc(s["tr_act"], 1)
            def place(g):
                a.wait_ge(s["dist_done"], g - 1)
                link(act(HAT[2], HAT[2], ACT.Abs))
                a.wait_ge(s["s2_mm"], (g - 1) * CG // 4)
                for q in range(4):
                    r = slice(32 * q, 32 * q + 32)
                    i = act(AM[g % 2][0][r, :, 32 * q:32 * q + 32], HAT[2][r], ACT.Relu, bias=ONE[r], scale=-1.0)
                i.then_inc(s["am_act"], 1)

            for n in range(16):
                a.wait_ge(s["s2_mm"], n + 1)
                act(E[:, :, :, 4 * n:4 * n + 4].rearrange("p x g c -> p c g x"),
                    bank(2 + n % 2).rearrange("p (c g x) -> p c g x", c=4, g=4), ACT.Copy)\
                    .then_inc(s["s2_copied"], 1)
                if n in (3, 7):
                    place(2 + n // 7)
            for n in range(0, 16, 2):
                a.wait_ge(s["bk_mm"], n + 1)
                back_out(copy, n).then_inc(s["bk_act"], 1)

        @block.gpsimd
        def _(g):
            ch = Chain(g, s["pool_step"])
            link = ch.link

            def power(nth, lo=0, hi=PAIRS):
                g.wait_ge(s["var_ready"], nth + 1)
                if nth == BN1:
                    g.tensor_tensor(BT[:, 4:5], BT[:, 3:4], MHALF[:, 0:1], ALU.pow).then_inc(s["pow_done"], 1)
                else:
                    g.tensor_tensor(SC[:, lo:hi], VAR[:, lo:hi], MHALF[:, lo:hi], ALU.pow)\
                        .then_inc(s["pow_done"], 1)

            g.memset(R[:, 0:4 * PW * PW].bitcast(F32), 0.0).then_inc(s["zero_done"], 1)

            power(IN_A, 0, HALFWAY)
            g.wait_ge(s["coef_ready"], IN_A + 1)
            for p in range(PAIRS):
                if p == HALFWAY:
                    power(IN_B, HALFWAY, PAIRS)
                    g.wait_ge(s["coef_ready"], IN_B + 1)
                need(g, s["xz_mm"], 2 * p - 2)
                g.tensor_scalar(G[p % 2], X[:, p, :], SC[:, p:p + 1], SH[:, p:p + 1], ALU.mult, ALU.add)\
                    .then_inc(s["g_ready"], 1)

            def soft(p, h):
                n = 2 * p + h
                g.wait_ge(s["ln_done"], n + 1)
                g.wait_ge(s["dt_read"], n + 1)
                link(g.tensor_tensor(tM[h], tM[h], tU[h], ALU.add))
                g.tensor_tensor(tM[h], tM[h], tE[h], ALU.subtract).then_inc(s["dt_done"], 1)
                g.wait_ge(s["dt_done"], n + 1)
                g.tensor_tensor(tU[h], tM[h], half(XS, p, h), ALU.mult).then_inc(s["dtx_done"], 1)

            def output(p, h):
                n = 2 * p + h
                g.wait_ge(s["hc_done"], n + 1)
                need(g, s["o_mm"], n - 1)
                link(g.tensor_tensor(tY[h], tA[h][0], tA[h][1], ALU.add))
                g.tensor_tensor(tY[h], tY[h], half(ZS, p, h), ALU.mult).then_inc(s["y_done"], 1)

            g.wait_ge(s["silux_done"], PAIRS)
            g.wait_ge(s["siluz_done"], PAIRS)
            soft(0, 0)
            soft(0, 1)
            output(0, 0)
            soft(1, 0)
            output(0, 1)
            soft(1, 1)
            output(1, 0)
            with g.Fori(2, PAIRS) as p:
                ch.enter(p - 2, 4)
                soft(p, 0)
                output(p - 1, 1)
                soft(p, 1)
                output(p, 0)
                ch.leave(PAIRS - 2)
            output(PAIRS - 1, 1)

            power(GN1)
            power(BN1)
            g.wait_ge(s["coef_ready"], BN1 + 1)

            def u1(p):
                need(g, s["ul_done"], p - 1)
                g.tensor_scalar(UF[p % 2], X[:, p, :], SB[:, p:p + 1], TB[:, p:p + 1], ALU.mult, ALU.add)\
                    .then_inc(s["u_ready"], 1)

            def g1(p):
                need(g, s["y1_done"], 2 * p - 2)
                g.tensor_scalar(GF[p % 2], X[:, p, :], SC[:, p:p + 1], SH[:, p:p + 1], ALU.mult, ALU.add)\
                    .then_inc(s["g1_ready"], 1)

            for p in range(7):
                u1(p)
                g1(p)

            def normed(q):
                need(g, s["asm_mm"], 2 * q - 4)
                m = min(q, PAIRS - 1)
                g.tensor_scalar(GB[q % 3], X[:, m, :], SC[:, m:m + 1], SH[:, m:m + 1], ALU.mult, ALU.add)\
                    .then_inc(s["gb_ready"], 1)

            def low_z(q):
                for h in range(2):
                    g.wait_ge(s["hi_done"], 2 * q + h + 1)
                    if h == 0:
                        need(g, s["stack_in"], 16 * NMOVES * q)
                    cols = slice(h * HALF, (h + 1) * HALF)
                    zh, zl = parts_of(q)
                    g.tensor_tensor(zl[:, cols], EF[h], zh[:, cols], ALU.subtract).then_inc(s["lo_done"], 1)

            def sums(p):
                for j in range(2, CHUNKS):
                    if j == 2:
                        g.wait_ge(s["first_added"], 2 * p + 2)
                    g.wait_ge(s["p_ready"], 32 * p + 2 * LAST[j] + 2)
                    for par in range(1 if p == PAIRS - 1 else 0, 2):
                        out = SA[p % 3][par]
                        i = g.tensor_tensor(out, out, PT[j % SLOTS][par], ALU.add)
                    i.then_inc(s["add_done"], 1)
                    g.wait_ge(s["add_done"], 6 * p + j - 1)
                    if j == 4 and p == 0:
                        power(GN2B, 3, PAIRS)
                    if j == 5 and p == 0:
                        g.wait_ge(s["coef_ready"], GN2B + 1)
                        normed(3)

            def minus(b):
                for par in range(2):
                    g.memset(stack(b, par, 1)[96:98, :].bitcast(F32), -1.0).then_inc(s["minus_done"], 1)
                    need(g, s["minus_done"], 2 * b + par)

            power(GN2A, 0, 3)
            g.wait_ge(s["coef_ready"], GN2A + 1)
            for q in range(3):
                normed(q)
            u1(7)
            low_z(0)
            g1(7)
            low_z(1)
            g.wait_ge(s["lo_done"], 4)
            g.wait_ge(s["conv_mm"], 2 * PAIRS)
            minus(1)
            g.wait_ge(s["y1_done"], 2 * PAIRS)
            for p in range(PAIRS):
                if 0 < p < PAIRS - 2:
                    normed(p + 3)
                if p == PAIRS - 1:
                    power(GN3A, 0, PAIRS - 2)
                if p == 0:
                    g.wait_ge(s["stack_in"], 32 * NMOVES)
                    minus(2)
                if p < PAIRS - 1:
                    low_z(p + 2)
                sums(p)

            for n in range(2):
                if n == 0:
                    g.wait_ge(s["sum_mm"], 2 * PAIRS)
                else:
                    g.wait_ge(s["x2_done"], 2 * PAIRS)
                g.memset(RB[:, PAIRS * L + 2 * n * CG * P:PAIRS * L + 2 * (n + 1) * CG * P], 0.0)\
                    .then_inc(s["am_zero"], 1)
                g.wait_ge(s["am_zero"], n + 1)
                if n == 0:
                    power(GN3B, PAIRS - 2, PAIRS)
                    g.wait_ge(s["pow_done"], GN3B + 1)
            g.wait_ge(s["am_dve"], 3)
            grid = mat("grid", WW).unsqueeze(1).to_broadcast([P, CG, WW])
            for gr in (2, 3):
                tv = mat("thy", C)[:, gr * CG:(gr + 1) * CG].unsqueeze(2).to_broadcast([P, CG, WW])
                need(g, s["am_act"], gr - 2)
                g.tensor_tensor(HAT[2], grid, tv, ALU.add).then_inc(s["dist_done"], 1)
                g.wait_ge(s["dist_done"], gr - 1)

        @block.tensor
        def _(t):
            mm = t.matmul

            def group(nth, lo=0, hi=PAIRS):
                t.wait_ge(s["stat_ready"], nth + 1)
                if nth == BN1:
                    i = mm(PS[:, 7, 0:2], mat("batch"), BS)
                else:
                    i = mm(PS[:, 7, 0:2 * (hi - lo)], mat("pairs"), MV[:, lo:hi].rearrange("p a b -> p (a b)"))
                i.then_inc(s["group_mm"], 1)

            t.wait_ge(s["packed"], 16)
            mm(PS[:, 6, 0:P], W[0:2 * RANK, OFF["dtl"]:OFF["dtl"] + P],
               W[0:2 * RANK, OFF["dtr"]:OFF["dtr"] + P]).then_inc(s["wdt_mm"], 1)
            group(IN_A, 0, HALFWAY)
            t.wait_ge(s["coef_ready"], IN_A + 1)

            def project(p, b):
                t.wait_ge(s["g_ready"], p + 1)
                need(t, s["taps_done"], p - 1)
                for h in range(2):
                    i = mm(bank(2 * b + h), mat("winx"), G[b][:, h * HALF:(h + 1) * HALF])
                i.then_inc(s["xz_mm"], 1)
                need(t, s["siluz_done"], p)
                for h in range(2):
                    i = mm(bank(4 + h), mat("winz"), G[b][:, h * HALF:(h + 1) * HALF])
                i.then_inc(s["xz_mm"], 1)

            for p in range(HALFWAY):
                project(p, p % 2)
            group(IN_B, HALFWAY, PAIRS)
            with t.Fori(HALFWAY // 2, PAIRS // 2) as k:
                project(2 * k, 0)
                project(2 * k + 1, 1)

            t.wait_ge(s["setup_done"], 1)
            t.wait_ge(s["silux_done"], 1)

            def dt(p, h):
                n = 2 * p + h
                need(t, s["dt_read"], n)
                mm(bank(7), WDT[:, :], half(XS, p, h)).then_inc(s["dt_mm"], 1)

            def states(p, h, o):
                n = 2 * p + h
                need(t, s["c_read" if o else "b_read"], n)
                for j in range(STATE):
                    i = mm(bank(1 + 2 * o + j), mat("bc%d" % (2 * o + j)), half(XS, p, h))
                i.then_inc(s["c_mm" if o else "b_mm"], 1)

            def project_out(p, h):
                n = 2 * p + h
                t.wait_ge(s["y_done"], n + 1)
                need(t, s["o_read"], n)
                mm(bank(5), mat("wout"), tY[h]).then_inc(s["o_mm"], 1)

            def variance(p, h):
                n = 2 * p + h
                t.wait_ge(s["sq_done"], n + 1)
                need(t, s["r_done"], n)
                mm(bank(6), mat("mean64"), tQ[h]).then_inc(s["v_mm"], 1)

            def turn(p, h, lead=True, lag=True):
                if lead:
                    dt(p + 1, h)
                if lag:
                    project_out(*before(p, h))
                    variance(*before(p, h))
                if lead or h == 0:
                    states(*after(p, h), 0)
                    states(*after(p, h), 1)

            dt(0, 0)
            t.wait_ge(s["taps_done"], PAIRS)
            t.wait_ge(s["siluz_done"], PAIRS)
            states(0, 0, 0)
            dt(0, 1)
            states(0, 0, 1)
            t.wait_ge(s["silux_done"], PAIRS)
            turn(0, 0, lag=False)
            turn(0, 1)
            with t.Fori(1, PAIRS - 1) as p:
                turn(p, 0)
                turn(p, 1)
            turn(PAIRS - 1, 0, lead=False)
            turn(PAIRS - 1, 1, lead=False)
            project_out(PAIRS - 1, 1)
            variance(PAIRS - 1, 1)
            group(GN1)
            group(BN1)

            t.wait_ge(s["coef_ready"], BN1 + 1)

            def conv(p, b, h, extra={}):
                if h == 0:
                    t.wait_ge(s["uh_done"], p + 1)
                need(t, s["y1_done"], 2 * p + h - 1)
                rows = HH // 2
                for n in range(PER):
                    w, u = ((0, UH), (1, UH), (0, UL))[n // 9]
                    if h == 0 and n == 18:
                        t.wait_ge(s["ul_done"], p + 1)
                    y, xx = divmod(n % 9, 3)
                    for step in extra.get(n, ()):
                        step()
                    i = mm(bank(h).rearrange("p (y x) -> p y x", y=rows), WS[:, w, n % 9, :],
                           u[b][:, h * rows + y:h * rows + y + rows, xx:xx + WW], start=(n == 0), stop=(n == PER - 1))
                i.then_inc(s["conv_mm"], 1)

            def pointwise(p, b, h, ahead=True):
                t.wait_ge(s["y1_done"], 2 * p + 3 if ahead else 2 * p + h + 1)
                mm(bank(4 + h), mat("w11"), YF[b][:, h * HALF:(h + 1) * HALF]).then_inc(s["w1_mm"], 1)

            def turn1(p, b, lag=True, extra=({}, {})):
                conv(p, b, 0, extra[0])
                conv(p, b, 1, extra[1])
                if lag:
                    pointwise(p - 1, 1 - b, 0)
                    pointwise(p - 1, 1 - b, 1)

            def operands(q, b, h):
                if h == 0:
                    t.wait_ge(s["gb_ready"], q + 1)
                    if isinstance(q, int) and q < 2:
                        need(t, s["asm_read"], 2 * q)
                    else:
                        t.wait_ge(s["m_copied"], 4 * q - 4)
                mm(bank(6 + h), mat("e12"), GB[b][:, h * HALF:(h + 1) * HALF]).then_inc(s["z_mm"], 1)

            def values(q, b, h):
                if isinstance(q, int) and q < 2:
                    t.wait_ge(s["z_read"], 4 * q + 1 + h)
                else:
                    t.wait_ge(s["sum_read"], 2 * q - 3 + h)
                for c in range(CHUNKS // 2):
                    at = h * HALF + c * P
                    i = mm(PS[:, 6 + h, c * P:(c + 1) * P], GB[b][:, at:at + P], mat("wa"))
                i.then_inc(s["asm_mm"], 1)

            def rows(q, b, n, h):
                par, tile = divmod(n, CHUNKS)
                if n == 0 and h == 0:
                    t.wait_ge(s["stack_in"], 16 * NMOVES * q + 16 * NMOVES)
                need(t, s["s_read"], 32 * q + 2 * n + h - 1)
                mm(bank(2 + h), stack(b, par, 0)[0:96, tile * P:(tile + 1) * P],
                   stack(b, par, 1)[0:96, h * HALF:(h + 1) * HALF]).then_inc(s["s_mm"], 1)

            def max_rows(q, par):
                if par == 0:
                    t.wait_ge(s["asm_read"], 2 * q + 2)
                t.wait_ge(s["m_ready"], 2 * q + par + 1)
                for h in range(2):
                    if par:
                        t.wait_ge(s["m_copied"], 4 * q + h + 1)
                    for c in range(4):
                        i = mm(PS[96:98, 6 + h, c * P:(c + 1) * P], MB[:, par, 4 * h + c, :], IB[:, :])
                    i.then_inc(s["mrow_mm"], 1)

            def scores(p, b, n):
                j, par = STEPS[n]
                if j == 0:
                    t.wait_ge(s["m_copied"], 4 * p + 2 + 2 * par)
                for h in range(2):
                    need(t, s["p_ready"], 32 * p + 2 * n + h - 1)
                    mm(bank(4 + h), stack(b, par, 1)[0:98, j * P:(j + 1) * P],
                       stack(b, par, 0)[0:98, h * HALF:(h + 1) * HALF]).then_inc(s["t_mm"], 1)

            def products(p, b, j, h):
                if h == 0:
                    t.wait_ge(s["p_ready"], 32 * p + 2 * LAST[j] + 2)
                if j == 0:
                    t.wait_ge(s["v_done"], 2 * p + 2)
                    need(t, s["acc_read"], 2 * p + h - 1)
                for par in range(2):
                    i = mm(PS[par * C:(par + 1) * C, h, :], V[b][:, j, par * C:(par + 1) * C],
                           PT[j % SLOTS][par][:, h * HALF:(h + 1) * HALF],
                           start=(j == 0), stop=(j == CHUNKS - 1))
                i.then_inc(s["pv_done"], 1)

            def sums(p, b, h):
                if h == 0:
                    t.wait_ge(s["add_done"], 6 * p + 6)
                if isinstance(p, int) and p == PAIRS - 1:
                    t.wait_ge(s["add_dve"], 6)
                    t.wait_ge(s["sum_read"], 2 * p)
                elif isinstance(p, int) and p == PAIRS - 2:
                    t.wait_ge(s["m_copied"], 4 * PAIRS)
                    t.wait_ge(s["var_ready"], GN3A + 1)
                else:
                    t.wait_ge(s["z_read"], 2 * p + 7 + h)
                for par in range(2):
                    i = mm(PS[par * C:(par + 1) * C, 6 + h, :], mat("ones", C),
                           SA[b][par][:, h * HALF:(h + 1) * HALF])
                i.then_inc(s["sum_mm"], 1)

            def tail(p, b, n):
                products(p, b, CHUNKS - 2 + n // 2, n % 2)

            def attend(p, b, lead=True, lag=True, first=False):
                for n in range(2 * CHUNKS):
                    scores(p, b, n)
                    if lead:
                        rows(p + 1, (b + 1) % 3, n, 0)
                    if n >= 4:
                        products(p, b, n // 2 - 2, n % 2)
                    elif lag:
                        tail(p - 1, (b + 2) % 3, n)
                    if n == 0:
                        max_rows(p, 1)
                    if n == 1 and not lead:
                        t.wait_ge(s["m_copied"], 4 * PAIRS)
                        group(GN3A, 0, PAIRS - 2)
                    if n in (1, 2) and lead:
                        operands(p + 2, (b + 2) % 3, n - 1)
                    if n in (4, 5) and lag:
                        sums(p - 1, (b + 2) % 3, n - 4)
                    if n in (7, 8) and lead:
                        values(p + 1, (b + 1) % 3, n - 7)
                    if n == 10 and first:
                        t.wait_ge(s["asm_read"], 4)
                        group(GN2B, 3, PAIRS)
                    if n == 13 and lead:
                        max_rows(p + 1, 0)
                    if lead:
                        rows(p + 1, (b + 1) % 3, n, 1)

            turn1(0, 0, lag=False)
            with t.Fori(0, 2) as k:
                turn1(2 * k + 1, 1)
                turn1(2 * k + 2, 0)
            turn1(5, 1, extra=({18: [lambda: group(GN2A, 0, 3)]},
                               {18: [lambda: t.wait_ge(s["coef_ready"], GN2A + 1), lambda: operands(0, 0, 0)],
                                20: [lambda: operands(0, 0, 1)]}))
            extras, at = {(6, 0): {2: [lambda: values(0, 0, 0)], 5: [lambda: values(0, 0, 1)],
                                   16: [lambda: operands(1, 1, 0)], 18: [lambda: operands(1, 1, 1)]}}, 0
            for key, (count, start) in FILLS.items():
                for j in range(count):
                    extras.setdefault(key, {}).setdefault(start + j * (PER - start) // count, [])\
                        .append(lambda m=at + j: rows(0, 0, *divmod(m, 2)))
                at += count
            extras[7, 1].setdefault(22, []).extend([lambda: t.wait_ge(s["z_read"], 4), lambda: max_rows(0, 0)])
            turn1(6, 0, extra=(extras[6, 0], extras[6, 1]))
            conv(7, 1, 0, extras[7, 0])
            conv(7, 1, 1, extras[7, 1])
            for p in (6, 7):
                for h in range(2):
                    if p == 7:
                        t.wait_ge(s["x1_done"], 13 + h)
                    pointwise(p, p % 2, h, p == 6)
            t.wait_ge(s["minus_done"], 1)
            t.wait_ge(s["x1_done"], 2 * PAIRS)
            attend(0, 0, lag=False, first=True)
            t.wait_ge(s["minus_done"], 5)
            with t.Fori(0, 2) as k:
                for c in range(3):
                    attend(3 * k + c + 1, (c + 1) % 3)
            attend(PAIRS - 1, 1, lead=False)
            for n in range(4):
                tail(PAIRS - 1, 1, n)
            for h in range(2):
                sums(PAIRS - 1, 1, h)

            t.wait_ge(s["acc_read"], 2 * PAIRS)
            for n in range(16):
                q, xb = divmod(n, 8)
                if n == 5:
                    t.wait_ge(s["sum_read"], 2 * PAIRS)
                    group(GN3B, PAIRS - 2, PAIRS)
                if xb == 0:
                    t.wait_ge(s["g3_done"], 4 * q + 4)
                if n >= 4:
                    m = n - 4
                    if m < 8 or m % 2 == 0:
                        t.wait_ge(s["tr_act"], m + 1 if m < 8 else m // 2 + 5)
                    else:
                        t.wait_ge(s["tr_dve"], (m - 8) // 2 + 1)
                for c in range(4):
                    xx = 4 * xb + c
                    src = G3[:, 4 * q:4 * q + 4, :].rearrange("p b (y x) -> p x (b y)", x=WW)[:, xx]
                    i = t.transpose(PS[:, n % 4, c * P:(c + 1) * P], src, mat("ident"))
                i.then_inc(s["tr_mm"], 1)

            def shift_y(n):
                if n % 4 == 0:
                    g = n // 4
                    t.wait_ge(s["am_dve"], (2, 4, 5, 6)[g])
                    need(t, s["am_act"], g - 1)
                need(t, s["s1_copied"], n - 1)
                for c in range(4):
                    ch = 4 * n + c
                    i = mm(PS[:, n % 2, c * P:(c + 1) * P], D[:, ch, :], AM[ch // CG % 2][0][:, ch % CG, :])
                i.then_inc(s["s1_mm"], 1)

            def shift_x(n):
                t.wait_ge(s["s1_copied"], n + 1)
                need(t, s["s2_copied"], n - 1)
                for c in range(4):
                    ch = 4 * n + c
                    i = mm(PS[:, 2 + n % 2, c * P:(c + 1) * P], D1[n % 2][:, c * P:(c + 1) * P],
                           AM[ch // CG % 2][1][:, ch % CG, :])
                i.then_inc(s["s2_mm"], 1)

            t.wait_ge(s["tr_act"], 12)
            t.wait_ge(s["tr_dve"], 4)
            for n in range(17):
                if n < 16:
                    shift_y(n)
                if n:
                    shift_x(n - 1)
            t.wait_ge(s["s2_copied"], 16)
            for n in range(16):
                q, xb = divmod(n, 8)
                if n >= 4:
                    t.wait_ge(s["bk_dve" if n % 2 else "bk_act"], (n - 4) // 2 + 1)
                for c in range(4):
                    xx = 4 * xb + c
                    src = E[:, xx, 2 * q:2 * q + 2, :].rearrange("p a c -> p (a c)")
                    i = t.transpose(PS[:, n % 4, c * P:(c + 1) * P], src, mat("ident"))
                i.then_inc(s["bk_mm"], 1)
            t.wait_ge(s["bk_act"], 8)
            t.wait_ge(s["bk_dve"], 8)
            for j in range(4):
                mm(bank(4 + j), mat("wpw"), half(S3, j // 2, j % 2)).then_inc(s["pw_mm"], 1)
            with t.Fori(1, PAIRS // 2) as k:
                for j in range(4):
                    t.wait_ge(s["res_done"], 4 * k + j - 3)
                    mm(bank(4 + j), mat("wpw"), half(S3, 2 * k + j // 2, j % 2)).then_inc(s["pw_mm"], 1)


def _packed(w):
    pack = np.zeros((P, NPACK + 9 * P), np.float32)

    def both(name, m):
        for par in range(2):
            o = (name if isinstance(name, int) else OFF[name]) + par * C
            pack[par * C:(par + 1) * C, o:o + m.shape[1]] = m

    def column(name, v, n=2):
        pack[:n * len(v), OFF[name]] = np.tile(v, n)

    win, wxp = w["L0_conv_W_in"], w["L0_conv_W_xproj"]
    both("winx", win[:C].T)
    both("winz", win[C:].T)
    for n in range(2 * STATE):
        both("bc%d" % n, np.broadcast_to(wxp[RANK + n][:, None], (C, C)))
    both("wout", w["L0_conv_W_out"].T)
    both("w11", w["L1_conv_w_1x1"][:, :, 0, 0].T)
    both("wpw", w["L3_conv_w_pw"].T)
    both("wa", w["L2_conv_wa"].T)
    pack[:, OFF["ba"]:OFF["ba"] + P] = np.tile(w["L2_conv_ba"], 2)[None]
    for k in range(4):
        e, par = divmod(k, 2)
        pack[par * C:(par + 1) * C, OFF["e12"] + k * CR:OFF["e12"] + (k + 1) * CR] = w["L2_conv_w%d" % (e + 1)].T
    for t in range(9):
        both(NPACK + t * P, w["L1_conv_w_lbp"][:, :, t // 3, t % 3].T)
    for par in range(2):
        r = slice(par * RANK, (par + 1) * RANK)
        pack[r, OFF["dtl"] + par * C:OFF["dtl"] + (par + 1) * C] = wxp[:RANK]
        pack[r, OFF["dtr"] + par * C:OFF["dtr"] + (par + 1) * C] = w["L0_conv_W_dt"].T
    pack[:, OFF["thy"]:OFF["thy"] + C] = w["L3_conv_theta_s"][None, :, 0]
    pack[:, OFF["thx"]:OFF["thx"] + C] = w["L3_conv_theta_s"][None, :, 1]
    for j in range(TAPS):
        column("cw%d" % j, w["L0_conv_conv_w"][:, 0, j])
    for name, key in (("cb", "L0_conv_conv_b"), ("bdt", "L0_conv_b_dt"), ("dpar", "L0_conv_D_param"),
                      ("lng", "L0_conv_ln_g"), ("lnb", "L0_conv_ln_b"), ("gamma", "L1_conv_gamma"),
                      ("beta", "L1_conv_beta"), ("b11", "L1_conv_b_1x1"), ("wdw", "L3_conv_w_dw")):
        column(name, w[key])
    for j in range(STATE):
        column("al%d" % j, w["L0_conv_A_log"][:, j])
    pack[:, OFF["b12"]] = np.concatenate([np.tile(w["L2_conv_b%d" % e], 2) for e in (1, 2)])
    pack[:, OFF["a12"]] = np.repeat([w["L2_conv_a1"], w["L2_conv_a2"]], C)
    pack[:, OFF["aa"]] = w["L2_conv_aa"]
    i = np.arange(P)
    pack[:, OFF["mean64"]:OFF["mean64"] + P] = (i[:, None] // C == i[None] // C) / C
    pack[:, OFF["pairs"]:OFF["pairs"] + P] = (i[:, None] // 2 == i[None] // 2) / 2
    pack[:, OFF["batch"]:OFF["batch"] + P] = (i[:, None] % C == i[None] % C) / IMAGES
    pack[:, OFF["ident"]:OFF["ident"] + P] = np.eye(P)
    pack[:, OFF["grid"]:OFF["grid"] + WW] = (i % HH)[:, None] - np.arange(WW)[None]
    pack[:, OFF["ones"]:OFF["ones"] + C] = 1
    return pack


def kernel(**inputs):
    import concourse.bacc as bacc
    from concourse.bass_utils import run_bass_kernel_spmd

    w = {k: np.asarray(v) for k, v in inputs.items()}
    arrays = {"x": np.ascontiguousarray(w["x"]), "pack": _packed(w)}
    nc = bacc.Bacc("TRN2", target_bir_lowering=False, num_devices=1)
    args = [nc.dram_tensor(n, a.shape, F32, kind="ExternalInput").ap() for n, a in arrays.items()]
    args.append(nc.dram_tensor("out", arrays["x"].shape, F32, kind="ExternalOutput").ap())
    build(nc, *args)
    return run_bass_kernel_spmd(nc, [arrays], core_ids=[0]).results[0]["out"]
```
